# Optimizing a Trainium2 kernel written in Bass

```python
import numpy as np
import jax
import jax.numpy as jnp

def _softmax(x, axis=-1):
    return jax.nn.softmax(x, axis=axis)

def _gelu(x):
    return jax.nn.gelu(x, approximate=True)

def _silu(x):
    return jax.nn.silu(x)

def _sigmoid(x):
    return jax.nn.sigmoid(x)

def _layernorm(x, axis=-1, eps=1e-05):
    m = jnp.mean(x, axis=axis, keepdims=True)
    v = jnp.var(x, axis=axis, keepdims=True)
    return (x - m) / jnp.sqrt(v + eps)

def _scatter_add(tgt, idx, src, axis=0):
    return tgt.at[idx].add(src)

def _segment_sum(src, seg, n):
    return jax.ops.segment_sum(src, seg, n)
kernel_name = 'mk_prb_d2_jaxref_r8_81a8da'

def setup_inputs(seed: int=0):
    np.random.seed(seed)
    _w = jnp.asarray

    def _L0_attn_setup():
        import jax, jax.numpy as jnp
        import numpy as np
        N_HIDDEN = 256
        N_HEADS = 64
        EXPAND = 2
        D_STATE = 128
        D_CONV = 4
        CHUNK = 128
        DT_MIN = 0.001
        DT_MAX = 0.1
        INNER = EXPAND * N_HIDDEN
        HEAD_DIM = INNER // N_HEADS
        CONV_DIM = INNER + 2 * D_STATE
        D_IN_PROJ = 2 * INNER + 2 * D_STATE + N_HEADS
        EPS = 1e-06

        def _segsum(x):
            t = x.shape[-1]
            cs = jnp.cumsum(x, axis=-1)
            seg = cs[..., :, None] - cs[..., None, :]
            mask = jnp.tril(jnp.ones((t, t), dtype=bool))
            return jnp.where(mask, seg, -jnp.inf)

        def _ssd(x, dt, a, b_mat, c_mat, d, dt_bias):
            bsz, seq, h, p = x.shape
            dt = jnp.clip(jax.nn.softplus(dt + dt_bias), DT_MIN, DT_MAX)
            d_res = d.reshape(1, 1, h, 1) * x
            x_disc = x * dt[..., None]
            a_disc = a * dt
            ch = lambda t_: t_.reshape(bsz, seq // CHUNK, CHUNK, *t_.shape[2:])
            x_blk, b_blk, c_blk = (ch(x_disc), ch(b_mat), ch(c_mat))
            a_blk = jnp.transpose(ch(a_disc), (0, 3, 1, 2))
            a_cum = jnp.cumsum(a_blk, axis=-1)
            l_mat = jnp.exp(_segsum(a_blk))
            y_diag = jnp.einsum('bclhn,bcshn,bhcls,bcshp->bclhp', c_blk, b_blk, l_mat, x_blk)
            decay_states = jnp.exp(a_cum[..., -1:] - a_cum)
            states = jnp.einsum('bclhn,bhcl,bclhp->bchpn', b_blk, decay_states, x_blk)
            states = jnp.concatenate([jnp.zeros_like(states[:, :1]), states], axis=1)
            a_end = jnp.pad(a_cum[..., -1], ((0, 0), (0, 0), (1, 0)))
            decay_chunk = jnp.exp(_segsum(a_end))
            new_states = jnp.einsum('bhzc,bchpn->bzhpn', decay_chunk, states)
            states = new_states[:, :-1]
            y_off = jnp.einsum('bclhn,bchpn,bhcl->bclhp', c_blk, states, jnp.exp(a_cum))
            y = (y_diag + y_off).reshape(bsz, seq, h, p)
            return y + d_res
        key = jax.random.key(seed)
        ks = jax.random.split(key, 10)
        B, L = (2, 256)
        s = lambda fan_in: 1.0 / np.sqrt(fan_in)
        return {'x': jax.random.normal(ks[0], (B, L, N_HIDDEN), jnp.float32), 'W_in': jax.random.normal(ks[1], (N_HIDDEN, D_IN_PROJ), jnp.float32) * s(N_HIDDEN), 'b_in': jnp.zeros((D_IN_PROJ,), jnp.float32), 'conv_w': jax.random.normal(ks[2], (D_CONV, 1, CONV_DIM), jnp.float32) * s(D_CONV), 'conv_b': jnp.zeros((CONV_DIM,), jnp.float32), 'A_log': jnp.log(jnp.arange(1, N_HEADS + 1, dtype=jnp.float32)), 'dt_bias': jax.random.normal(ks[3], (N_HEADS,), jnp.float32) * 0.1, 'D_param': jnp.ones((N_HEADS,), jnp.float32), 'norm_w': jnp.ones((INNER,), jnp.float32), 'W_out': jax.random.normal(ks[4], (INNER, N_HIDDEN), jnp.float32) * s(INNER), 'b_out': jnp.zeros((N_HIDDEN,), jnp.float32)}
    _L0_attn_in = _L0_attn_setup()

    def _L0_ffn_setup():
        import jax, jax.numpy as jnp
        import numpy as np
        B, T, D = (2, 128, 256)
        E, K, H = (64, 4, 64)
        S, HS = (2, H * K)
        CAP = 64
        key = jax.random.key(seed)
        ks = jax.random.split(key, 9)
        scale = 0.02
        return {'x': jax.random.normal(ks[0], (B, T, D), jnp.float32), 'Wr': jax.random.normal(ks[1], (D, E), jnp.float32) * scale, 'router_bias': jnp.zeros((E,), jnp.float32), 'Wg': jax.random.normal(ks[2], (E, D, H), jnp.float32) * scale, 'Wu': jax.random.normal(ks[3], (E, D, H), jnp.float32) * scale, 'Wd': jax.random.normal(ks[4], (E, H, D), jnp.float32) * scale, 'Sg': jax.random.normal(ks[5], (S, D, HS), jnp.float32) * scale, 'Su': jax.random.normal(ks[6], (S, D, HS), jnp.float32) * scale, 'Sd': jax.random.normal(ks[7], (S, HS, D), jnp.float32) * scale}
    _L0_ffn_in = _L0_ffn_setup()

    def _L1_attn_setup():
        import jax, jax.numpy as jnp
        import numpy as np
        B, S, D = (2, 512, 256)
        H, HKV, DH = (16, 4, 128)
        CHUNK = 64
        GROUPS = H // HKV

        def _alibi_slopes(n_heads):
            i = jnp.arange(1, n_heads + 1, dtype=jnp.float32)
            return jnp.exp2(-8.0 * i / n_heads)

        def _rope(x):
            s, d = (x.shape[2], x.shape[3])
            inv_freq = 1.0 / 10000.0 ** (jnp.arange(0, d, 2, dtype=jnp.float32) / d)
            freqs = jnp.arange(s, dtype=jnp.float32)[:, None] * inv_freq[None, :]
            cos = jnp.concatenate([jnp.cos(freqs), jnp.cos(freqs)], axis=-1)
            sin = jnp.concatenate([jnp.sin(freqs), jnp.sin(freqs)], axis=-1)
            x1, x2 = (x[..., :d // 2], x[..., d // 2:])
            rot = jnp.concatenate([-x2, x1], axis=-1)
            return x * cos[None, None] + rot * sin[None, None]

        def _lightning_attn(q, k, v):
            b, h, s, dh = q.shape
            nc = s // CHUNK
            lam = _alibi_slopes(h)
            r = jnp.arange(CHUNK, dtype=jnp.float32)
            diff = r[:, None] - r[None, :]
            diag = jnp.where(diff >= 0, jnp.exp(-lam[:, None, None] * diff), 0.0)
            q_dec = jnp.exp(-lam[:, None] * (r + 1.0))
            k_dec = jnp.exp(-lam[:, None] * (CHUNK - 1.0 - r))
            blk = jnp.exp(-lam * CHUNK)
            qc = q.reshape(b, h, nc, CHUNK, dh).transpose(2, 0, 1, 3, 4)
            kc = k.reshape(b, h, nc, CHUNK, dh).transpose(2, 0, 1, 3, 4)
            vc = v.reshape(b, h, nc, CHUNK, dh).transpose(2, 0, 1, 3, 4)

            def step(kv, inp):
                qi, ki, vi = inp
                scores = jnp.einsum('bhid,bhjd->bhij', qi, ki) * diag[None]
                o_intra = jnp.einsum('bhij,bhje->bhie', scores, vi)
                o_inter = jnp.einsum('bhid,bhde->bhie', qi * q_dec[None, :, :, None], kv)
                kv = blk[None, :, None, None] * kv + jnp.einsum('bhjd,bhje->bhde', ki * k_dec[None, :, :, None], vi)
                return (kv, o_intra + o_inter)
            kv0 = jnp.zeros((b, h, dh, dh), q.dtype)
            _, o = jax.lax.scan(step, kv0, (qc, kc, vc))
            return o.transpose(1, 2, 0, 3, 4).reshape(b, h, s, dh)
        key = jax.random.key(seed)
        ks = jax.random.split(key, 5)
        sc = 0.02
        return {'x': jax.random.normal(ks[0], (B, S, D), jnp.float32), 'wq': jax.random.normal(ks[1], (H * DH, D), jnp.float32) * sc, 'wk': jax.random.normal(ks[2], (HKV * DH, D), jnp.float32) * sc, 'wv': jax.random.normal(ks[3], (HKV * DH, D), jnp.float32) * sc, 'wo': jax.random.normal(ks[4], (D, H * DH), jnp.float32) * sc}
    _L1_attn_in = _L1_attn_setup()

    def _L1_ffn_setup():
        import jax, jax.numpy as jnp
        import numpy as np
        from jax import lax
        TOP_K = 4
        ROUTED_SCALING = 1.0
        RENORMALIZE = True

        def _swiglu_ffn(x, wg, wu, wd):
            return jax.nn.silu(x @ wg.T) * (x @ wu.T) @ wd.T
        key = jax.random.key(seed)
        ks = jax.random.split(key, 9)
        H, I, E = (256, 128, 16)
        s = 0.02
        return {'hidden_states': jax.random.normal(ks[0], (2, 128, H), jnp.float32), 'gate_w': jax.random.normal(ks[1], (E, H), jnp.float32) * s, 'expert_bias': jax.random.normal(ks[2], (E,), jnp.float32) * s, 'w_gate': jax.random.normal(ks[3], (E, I, H), jnp.float32) * s, 'w_up': jax.random.normal(ks[4], (E, I, H), jnp.float32) * s, 'w_down': jax.random.normal(ks[5], (E, H, I), jnp.float32) * s, 'sw_gate': jax.random.normal(ks[6], (I, H), jnp.float32) * s, 'sw_up': jax.random.normal(ks[7], (I, H), jnp.float32) * s, 'sw_down': jax.random.normal(ks[8], (H, I), jnp.float32) * s}
    _L1_ffn_in = _L1_ffn_setup()
    _d = {'L0_attn_x': _L0_attn_in['x'], 'L0_attn_W_in': _L0_attn_in['W_in'], 'L0_attn_b_in': _L0_attn_in['b_in'], 'L0_attn_conv_w': _L0_attn_in['conv_w'], 'L0_attn_conv_b': _L0_attn_in['conv_b'], 'L0_attn_A_log': _L0_attn_in['A_log'], 'L0_attn_dt_bias': _L0_attn_in['dt_bias'], 'L0_attn_D_param': _L0_attn_in['D_param'], 'L0_attn_norm_w': _L0_attn_in['norm_w'], 'L0_attn_W_out': _L0_attn_in['W_out'], 'L0_attn_b_out': _L0_attn_in['b_out'], 'L0_ffn_Wr': _L0_ffn_in['Wr'], 'L0_ffn_router_bias': _L0_ffn_in['router_bias'], 'L0_ffn_Wg': _L0_ffn_in['Wg'], 'L0_ffn_Wu': _L0_ffn_in['Wu'], 'L0_ffn_Wd': _L0_ffn_in['Wd'], 'L0_ffn_Sg': _L0_ffn_in['Sg'], 'L0_ffn_Su': _L0_ffn_in['Su'], 'L0_ffn_Sd': _L0_ffn_in['Sd'], 'L1_attn_wq': _L1_attn_in['wq'], 'L1_attn_wk': _L1_attn_in['wk'], 'L1_attn_wv': _L1_attn_in['wv'], 'L1_attn_wo': _L1_attn_in['wo'], 'L1_ffn_gate_w': _L1_ffn_in['gate_w'], 'L1_ffn_expert_bias': _L1_ffn_in['expert_bias'], 'L1_ffn_w_gate': _L1_ffn_in['w_gate'], 'L1_ffn_w_up': _L1_ffn_in['w_up'], 'L1_ffn_w_down': _L1_ffn_in['w_down'], 'L1_ffn_sw_gate': _L1_ffn_in['sw_gate'], 'L1_ffn_sw_up': _L1_ffn_in['sw_up'], 'L1_ffn_sw_down': _L1_ffn_in['sw_down']}
    _x0 = _d['L0_attn_x']
    _d['L0_attn_x'] = jax.random.normal(jax.random.fold_in(jax.random.key(seed), 1), (4, 1024, 256), dtype=_x0.dtype)
    del _x0
    return _d

def reference(L0_attn_x, L0_attn_W_in, L0_attn_b_in, L0_attn_conv_w, L0_attn_conv_b, L0_attn_A_log, L0_attn_dt_bias, L0_attn_D_param, L0_attn_norm_w, L0_attn_W_out, L0_attn_b_out, L0_ffn_Wr, L0_ffn_router_bias, L0_ffn_Wg, L0_ffn_Wu, L0_ffn_Wd, L0_ffn_Sg, L0_ffn_Su, L0_ffn_Sd, L1_attn_wq, L1_attn_wk, L1_attn_wv, L1_attn_wo, L1_ffn_gate_w, L1_ffn_expert_bias, L1_ffn_w_gate, L1_ffn_w_up, L1_ffn_w_down, L1_ffn_sw_gate, L1_ffn_sw_up, L1_ffn_sw_down):

    def _L0_attn_ref(x, W_in, b_in, conv_w, conv_b, A_log, dt_bias, D_param, norm_w, W_out, b_out):
        import jax, jax.numpy as jnp
        import numpy as np
        N_HIDDEN = 256
        N_HEADS = 64
        EXPAND = 2
        D_STATE = 128
        D_CONV = 4
        CHUNK = 128
        DT_MIN = 0.001
        DT_MAX = 0.1
        INNER = EXPAND * N_HIDDEN
        HEAD_DIM = INNER // N_HEADS
        CONV_DIM = INNER + 2 * D_STATE
        D_IN_PROJ = 2 * INNER + 2 * D_STATE + N_HEADS
        EPS = 1e-06

        def _segsum(x):
            t = x.shape[-1]
            cs = jnp.cumsum(x, axis=-1)
            seg = cs[..., :, None] - cs[..., None, :]
            mask = jnp.tril(jnp.ones((t, t), dtype=bool))
            return jnp.where(mask, seg, -jnp.inf)

        def _ssd(x, dt, a, b_mat, c_mat, d, dt_bias):
            bsz, seq, h, p = x.shape
            dt = jnp.clip(jax.nn.softplus(dt + dt_bias), DT_MIN, DT_MAX)
            d_res = d.reshape(1, 1, h, 1) * x
            x_disc = x * dt[..., None]
            a_disc = a * dt
            ch = lambda t_: t_.reshape(bsz, seq // CHUNK, CHUNK, *t_.shape[2:])
            x_blk, b_blk, c_blk = (ch(x_disc), ch(b_mat), ch(c_mat))
            a_blk = jnp.transpose(ch(a_disc), (0, 3, 1, 2))
            a_cum = jnp.cumsum(a_blk, axis=-1)
            l_mat = jnp.exp(_segsum(a_blk))
            y_diag = jnp.einsum('bclhn,bcshn,bhcls,bcshp->bclhp', c_blk, b_blk, l_mat, x_blk)
            decay_states = jnp.exp(a_cum[..., -1:] - a_cum)
            states = jnp.einsum('bclhn,bhcl,bclhp->bchpn', b_blk, decay_states, x_blk)
            states = jnp.concatenate([jnp.zeros_like(states[:, :1]), states], axis=1)
            a_end = jnp.pad(a_cum[..., -1], ((0, 0), (0, 0), (1, 0)))
            decay_chunk = jnp.exp(_segsum(a_end))
            new_states = jnp.einsum('bhzc,bchpn->bzhpn', decay_chunk, states)
            states = new_states[:, :-1]
            y_off = jnp.einsum('bclhn,bchpn,bhcl->bclhp', c_blk, states, jnp.exp(a_cum))
            y = (y_diag + y_off).reshape(bsz, seq, h, p)
            return y + d_res
        B, L, _ = x.shape
        zxbcdt = x @ W_in + b_in
        z = zxbcdt[..., :INNER]
        xBC = zxbcdt[..., INNER:INNER + CONV_DIM]
        dt = zxbcdt[..., -N_HEADS:]
        xp = jnp.pad(xBC, ((0, 0), (D_CONV - 1, 0), (0, 0)))
        xBC = jax.lax.conv_general_dilated(xp, conv_w, window_strides=(1,), padding='VALID', dimension_numbers=('NWC', 'WIO', 'NWC'), feature_group_count=CONV_DIM) + conv_b
        xBC = jax.nn.silu(xBC)
        x_ssm = xBC[..., :INNER].reshape(B, L, N_HEADS, HEAD_DIM)
        b_mat = jnp.broadcast_to(xBC[..., INNER:INNER + D_STATE][:, :, None, :], (B, L, N_HEADS, D_STATE))
        c_mat = jnp.broadcast_to(xBC[..., INNER + D_STATE:][:, :, None, :], (B, L, N_HEADS, D_STATE))
        a = -jnp.exp(A_log)
        y = _ssd(x_ssm, dt, a, b_mat, c_mat, D_param, dt_bias)
        y = y.reshape(B, L, INNER)
        y = y * jax.nn.silu(z)
        y = y * jax.lax.rsqrt(jnp.mean(y * y, axis=-1, keepdims=True) + EPS) * norm_w
        return y @ W_out + b_out

    def _L0_ffn_ref(x, Wr, router_bias, Wg, Wu, Wd, Sg, Su, Sd):
        import jax, jax.numpy as jnp
        import numpy as np
        B, T, D = (2, 128, 256)
        E, K, H = (64, 4, 64)
        S, HS = (2, H * K)
        CAP = 64
        Bx, Tx, Dx = x.shape
        N = Bx * Tx
        flat = x.reshape(N, Dx)
        logits = flat @ Wr + router_bias
        scores = jax.nn.softmax(logits, axis=-1)
        topk_scores, topk_idx = jax.lax.top_k(scores, K)
        topk_scores = topk_scores / topk_scores.sum(-1, keepdims=True)
        eid = topk_idx.reshape(-1)
        w = topk_scores.reshape(-1)
        tok = jnp.repeat(jnp.arange(N), K)
        oh = jax.nn.one_hot(eid, E, dtype=jnp.int32)
        pos = (jnp.cumsum(oh, axis=0) * oh).sum(-1) - 1
        valid = pos < CAP
        xb = jnp.zeros((E, CAP, Dx), x.dtype).at[eid, pos].set(flat[tok], mode='drop')
        h = jax.nn.silu(jnp.einsum('ecd,edh->ech', xb, Wg)) * jnp.einsum('ecd,edh->ech', xb, Wu)
        yb = jnp.einsum('ech,ehd->ecd', h, Wd)
        y = yb[eid, jnp.minimum(pos, CAP - 1)] * (w * valid)[:, None]
        out = jnp.zeros((N, Dx), x.dtype).at[tok].add(y)
        hs = jax.nn.silu(jnp.einsum('nd,sdh->nsh', flat, Sg)) * jnp.einsum('nd,sdh->nsh', flat, Su)
        out = out + jnp.einsum('nsh,shd->nd', hs, Sd)
        return out.reshape(Bx, Tx, Dx)

    def _L1_attn_ref(x, wq, wk, wv, wo):
        import jax, jax.numpy as jnp
        import numpy as np
        B, S, D = (2, 512, 256)
        H, HKV, DH = (16, 4, 128)
        CHUNK = 64
        GROUPS = H // HKV

        def _alibi_slopes(n_heads):
            i = jnp.arange(1, n_heads + 1, dtype=jnp.float32)
            return jnp.exp2(-8.0 * i / n_heads)

        def _rope(x):
            s, d = (x.shape[2], x.shape[3])
            inv_freq = 1.0 / 10000.0 ** (jnp.arange(0, d, 2, dtype=jnp.float32) / d)
            freqs = jnp.arange(s, dtype=jnp.float32)[:, None] * inv_freq[None, :]
            cos = jnp.concatenate([jnp.cos(freqs), jnp.cos(freqs)], axis=-1)
            sin = jnp.concatenate([jnp.sin(freqs), jnp.sin(freqs)], axis=-1)
            x1, x2 = (x[..., :d // 2], x[..., d // 2:])
            rot = jnp.concatenate([-x2, x1], axis=-1)
            return x * cos[None, None] + rot * sin[None, None]

        def _lightning_attn(q, k, v):
            b, h, s, dh = q.shape
            nc = s // CHUNK
            lam = _alibi_slopes(h)
            r = jnp.arange(CHUNK, dtype=jnp.float32)
            diff = r[:, None] - r[None, :]
            diag = jnp.where(diff >= 0, jnp.exp(-lam[:, None, None] * diff), 0.0)
            q_dec = jnp.exp(-lam[:, None] * (r + 1.0))
            k_dec = jnp.exp(-lam[:, None] * (CHUNK - 1.0 - r))
            blk = jnp.exp(-lam * CHUNK)
            qc = q.reshape(b, h, nc, CHUNK, dh).transpose(2, 0, 1, 3, 4)
            kc = k.reshape(b, h, nc, CHUNK, dh).transpose(2, 0, 1, 3, 4)
            vc = v.reshape(b, h, nc, CHUNK, dh).transpose(2, 0, 1, 3, 4)

            def step(kv, inp):
                qi, ki, vi = inp
                scores = jnp.einsum('bhid,bhjd->bhij', qi, ki) * diag[None]
                o_intra = jnp.einsum('bhij,bhje->bhie', scores, vi)
                o_inter = jnp.einsum('bhid,bhde->bhie', qi * q_dec[None, :, :, None], kv)
                kv = blk[None, :, None, None] * kv + jnp.einsum('bhjd,bhje->bhde', ki * k_dec[None, :, :, None], vi)
                return (kv, o_intra + o_inter)
            kv0 = jnp.zeros((b, h, dh, dh), q.dtype)
            _, o = jax.lax.scan(step, kv0, (qc, kc, vc))
            return o.transpose(1, 2, 0, 3, 4).reshape(b, h, s, dh)
        b, s, _ = x.shape
        q = jnp.einsum('bsd,ed->bse', x, wq).reshape(b, s, H, DH).transpose(0, 2, 1, 3)
        k = jnp.einsum('bsd,ed->bse', x, wk).reshape(b, s, HKV, DH).transpose(0, 2, 1, 3)
        v = jnp.einsum('bsd,ed->bse', x, wv).reshape(b, s, HKV, DH).transpose(0, 2, 1, 3)
        q = _rope(q)
        k = _rope(k)
        k = jnp.repeat(k, GROUPS, axis=1)
        v = jnp.repeat(v, GROUPS, axis=1)
        o = _lightning_attn(q, k, v)
        o = o.transpose(0, 2, 1, 3).reshape(b, s, H * DH)
        return jnp.einsum('bse,de->bsd', o, wo)

    def _L1_ffn_ref(hidden_states, gate_w, expert_bias, w_gate, w_up, w_down, sw_gate, sw_up, sw_down):
        import jax, jax.numpy as jnp
        import numpy as np
        from jax import lax
        TOP_K = 4
        ROUTED_SCALING = 1.0
        RENORMALIZE = True

        def _swiglu_ffn(x, wg, wu, wd):
            return jax.nn.silu(x @ wg.T) * (x @ wu.T) @ wd.T
        orig_shape = hidden_states.shape
        H = orig_shape[-1]
        x = hidden_states.reshape(-1, H)
        T = x.shape[0]
        logits = x.astype(jnp.float32) @ gate_w.T
        scores = jax.nn.sigmoid(logits)
        _, topk_idx = lax.top_k(scores + expert_bias[None, :], TOP_K)
        topk_w = jnp.take_along_axis(scores, topk_idx, axis=-1)
        if RENORMALIZE:
            topk_w = topk_w / jnp.sum(topk_w, axis=-1, keepdims=True)
        topk_w = topk_w * ROUTED_SCALING
        E = gate_w.shape[0]
        combine = jnp.zeros((T, E), dtype=x.dtype).at[jnp.arange(T)[:, None], topk_idx].set(topk_w.astype(x.dtype))

        def step(acc, ws):
            wg, wu, wd, cw = ws
            return (acc + cw[:, None] * _swiglu_ffn(x, wg, wu, wd), None)
        routed, _ = lax.scan(step, jnp.zeros_like(x), (w_gate, w_up, w_down, combine.T))
        shared = _swiglu_ffn(x, sw_gate, sw_up, sw_down)
        return (routed + shared).reshape(orig_shape)
    x = L0_attn_x
    xn = _layernorm(x, axis=-1)
    x = x + _L0_attn_ref(xn, L0_attn_W_in, L0_attn_b_in, L0_attn_conv_w, L0_attn_conv_b, L0_attn_A_log, L0_attn_dt_bias, L0_attn_D_param, L0_attn_norm_w, L0_attn_W_out, L0_attn_b_out) + _L0_ffn_ref(xn, L0_ffn_Wr, L0_ffn_router_bias, L0_ffn_Wg, L0_ffn_Wu, L0_ffn_Wd, L0_ffn_Sg, L0_ffn_Su, L0_ffn_Sd)
    xn = _layernorm(x, axis=-1)
    x = x + _L1_attn_ref(xn, L1_attn_wq, L1_attn_wk, L1_attn_wv, L1_attn_wo) + _L1_ffn_ref(xn, L1_ffn_gate_w, L1_ffn_expert_bias, L1_ffn_w_gate, L1_ffn_w_up, L1_ffn_w_down, L1_ffn_sw_gate, L1_ffn_sw_up, L1_ffn_sw_down)
    return x

_drawn_inputs = setup_inputs


def setup_inputs(seed=0):
    import zlib

    import numpy as np

    out = dict(_drawn_inputs(seed))
    spreads = {'L0_attn_b_in': (0.0, 0.1),
     'L0_attn_conv_b': (0.0, 0.1),
     'L0_attn_D_param': (1.0, 0.2),
     'L0_attn_norm_w': (1.0, 0.2),
     'L0_attn_b_out': (0.0, 0.1),
     'L0_ffn_router_bias': (0.0, 0.8)}
    factors = {'L0_attn_dt_bias': 8.0,
     'L0_ffn_Wr': 8.0,
     'L0_ffn_Wg': 8.0,
     'L0_ffn_Wu': 8.0,
     'L0_ffn_Wd': 8.0,
     'L1_ffn_gate_w': 8.0,
     'L1_ffn_expert_bias': 8.0,
     'L1_ffn_w_gate': 8.0,
     'L1_ffn_w_up': 8.0,
     'L1_ffn_w_down': 8.0,
     'L1_ffn_sw_gate': 8.0,
     'L1_ffn_sw_up': 8.0,
     'L1_ffn_sw_down': 8.0}
    for name, (base, spread) in spreads.items():
        noise = np.random.default_rng([zlib.crc32(name.encode()), seed]).standard_normal(out[name].shape)
        drawn = base * np.exp(spread * noise) if base else spread * noise
        out[name] = jnp.asarray(drawn.astype(out[name].dtype))
    for name, factor in factors.items():
        out[name] = (out[name] * factor).astype(out[name].dtype)
    return out
```

```python
from contextlib import ExitStack

import concourse.bass as bass
from concourse import mybir

ALU = mybir.AluOpType
ACT = mybir.ActivationFunctionType
F32 = mybir.dt.float32
U32 = mybir.dt.uint32
AX = mybir.AxisListType
P = 128
NB, SEQ_LEN, D = 4, 1024, 256
NC = SEQ_LEN // P
N_TOK = NB * SEQ_LEN
INNER, HEADS, D_STATE = 512, 64, 128
D_PROJ = 2 * INNER + 2 * D_STATE + HEADS
LEVELS = 7
HQ, HKV, DH = 16, 4, 128
E1 = 16
GATE_STEPS = 10
EXPERTS, K0, CAP, HID0 = 64, 4, 64, 64
ROUTER_STEPS = 31
SUM_END, SUM_POST, SUM_START, SUM_ALL = LEVELS, LEVELS + 1, 2 * LEVELS, 2 * LEVELS + 1
N_SUMS = 2 * LEVELS + 2
PRE_D = 4
POOL_ADDS = [1, 3, 5, "off"]
MIX_STEPS = (37, 4, 0)


def h1(ap):
    return ap.rearrange("p (h e) -> p h e", e=8)


def h8(ap, n):
    return ap.rearrange("p k (h e) -> p k h e", e=8)


def h8b(ap, n):
    return h1(ap).unsqueeze(1).to_broadcast([P, n, HEADS, 8])

DEBUG = False
def level_constants():
    import numpy as np
    t = np.arange(128)
    sums = np.zeros((N_SUMS, 128, 128), np.float32)
    pairs = np.zeros((LEVELS, 128, 128), np.float32)
    for k in range(LEVELS):
        for m in range(128):
            mid = ((m >> (k + 1)) << (k + 1)) + (1 << k)
            if m < mid:
                sums[k, :, m] = (t > m) & (t <= (mid if k == 0 else mid - 1))
                pairs[k, m, :] = (t >= mid) & (t < mid + (1 << k))
            elif k > 0:
                sums[SUM_POST + k - 1, :, m] = (t >= mid) & (t <= m)
    for m in range(128):
        sums[SUM_END, :, m] = t > m
        sums[SUM_START, :, m] = t <= m
    sums[SUM_ALL] = 1.0
    return np.ascontiguousarray(sums.transpose(1, 0, 2)), np.ascontiguousarray(pairs.transpose(1, 0, 2))


def mixer_phase(nc, io, scratch):
    with ExitStack() as ctx:
        def sb(name, shape, dt=F32):
            return ctx.enter_context(nc.sbuf_tensor("m_" + name, shape, dt))

        def sem(name):
            return ctx.enter_context(nc.semaphore("m_" + name))

        w_in = sb("w_in", [P, 2, D_PROJ])
        w_out = sb("w_out", [P, 4, D])
        s_gate = sb("s_gate", [P, 2, 512])
        s_up = sb("s_up", [P, 2, 512])
        s_down = sb("s_down", [P, 4, D])
        b_xbc = sb("b_xbc", [P, 6])
        b_z = sb("b_z", [P, 4])
        cw = sb("cw", [P, 6, 4])
        cb = sb("cb", [P, 6])
        normw = sb("normw", [P, 4])
        dt_add = sb("dt_add", [P, HEADS])
        dt_add2 = sb("dt_add2", [P, HEADS])
        a_exp = sb("a_exp", [P, HEADS])
        d_par = sb("d_par", [P, HEADS])
        b_out = sb("b_out", [P, D])
        sums = sb("sums", [P, N_SUMS, P])
        pairs = sb("pairs", [P, LEVELS, P])
        ident = sb("ident", [P, P])
        ones = sb("ones", [P, 2])
        eps = sb("eps", [P, 2])
        x_ln = sb("x_ln", [P, NB, D])
        x_res = sb("x_res", [P, NB, D])
        xn = sb("xn", [P, NB, D])
        stats = sb("stats", [P, NB, 6])
        mv = sb("mv", [P, NB, 2])
        lnv = sb("lnv", [P, NB])
        rstd = sb("rstd", [P, NB])
        xnT = sb("xnT", [P, 2, NB, P])
        xin = sb("xin", [P, 6, NB, P + 3])
        xc = sb("xc", [P, 6, NB, P])
        zs = sb("zs", [P, 4, NB, P])
        hs = sb("hs", [P, 4, NB, P])
        E = sb("E", [P, N_SUMS, NB, HEADS])
        dtr = sb("dtr", [P, NB, HEADS])
        dtu = sb("dtu", [P, NB, HEADS])
        dtw = sb("dtw", [P, NB, HEADS])
        dtl = sb("dtl", [P, NB, HEADS])
        dtd = sb("dtd", [P, NB, HEADS])
        dtc = sb("dtc", [P, NB, HEADS])
        adt = sb("adt", [P, NB, HEADS])
        d_over = sb("d_over", [P, NB, HEADS])
        Xd = sb("Xd", [P, 2, 512])
        Xp = sb("Xp", [P, 2, 8, 512])
        Gm = sb("Gm", [P, 2, LEVELS, P])
        gj = sb("gj", [P, P])
        gd = sb("gd", [P, 2])
        coef = sb("coef", [P, 2, HEADS])
        Btok = sb("Btok", [P, 2, P])
        Yd = sb("Yd", [P, 2, 512])
        Yp = sb("Yp", [P, 2, 512])
        T = sb("T", [P, 4, 512])
        S = sb("S", [P, NB, 512])
        yg = sb("yg", [P, 2, 4, P])
        y2 = sb("y2", [P, 2, 4, P])
        lss = sb("lss", [P, 2])
        rss = sb("rss", [P, 2])
        res = sb("res", [P, 2, D])
        NA, ND = 2, 6
        psA = [ctx.enter_context(nc.psum_tensor(f"m_psA{i}", [P, 512], F32)) for i in range(NA)]
        psD = [ctx.enter_context(nc.psum_tensor(f"m_psD{i}", [P, 512], F32)) for i in range(ND)]

        SEQ = [1, 2, 0, 3, 4, 5, 6, "off"]

        def tile_order():
            yield ("T1", 0)
            for b in range(NB):
                if b + 1 < NB:
                    yield ("T1", b + 1)
                if b >= 2:
                    yield ("T4", b - 2)
                yield ("T2", b)
                if b >= 1:
                    yield ("T3", b - 1)
            yield ("T4", NB - 2)
            yield ("T3", NB - 1)
            yield ("T4", NB - 1)

        A = [("xt", i) for i in range(2)] + [("xbc", g) for g in range(6)] + [("z", g) for g in range(4)] \
            + [("g", g) for g in range(4)] + [("E", i) for i in range(8)]
        DJ = [("dt", 0)] + [("u", g) for g in range(4)]
        for stage, b in tile_order():
            if stage == "T1":
                A.append(("btok", b))
                DJ += [("xtok", b), ("G", b)]
            if stage == "T2":
                DJ += [("L", b, k) for k in SEQ] + [("snew", b)]
            if stage == "T3":
                DJ.append(("yT", b))
            if stage == "T4":
                A.append(("ss", b))
                DJ.append(("out", b))
        PA, PD = len(A), len(DJ)

        def bank(jobs, ring, job):
            return ring[jobs.index(job) % len(ring)]

        def a_bank(*job):
            return bank(A, psA, job)

        def d_bank(*job):
            return bank(DJ, psD, job)

        def done(c, *job):
            return c * PD + DJ.index(job) + 1 + ND

        def adone(c, *job):
            return c * PA + A.index(job) + 1 + NA

        def credit(jobs, n, job):
            j = jobs.index(job)
            before = j - n if j >= n else max(i for i in range(len(jobs)) if i % n == j) - len(jobs)
            return before + 1 + n

        a_full, a_done = sem("a_full"), sem("a_done")
        d_full, d_done = sem("d_full"), sem("d_done")
        loaded, x_ready, xres_ready = sem("loaded"), sem("x_ready"), sem("xres_ready")
        x_used, xres_used = sem("x_used"), sem("xres_used")
        stored, xn_stored, xnT_stored = [sem("stored0"), sem("stored1")], sem("xn_stored"), sem("xnT_stored")
        setup, zeroed = sem("setup"), sem("zeroed")
        mv_ready, rstd_ready, xn_ready = sem("mv_ready"), sem("rstd_ready"), sem("xn_ready")
        act_step, dve_step, pool_step = sem("act_step"), sem("dve_step"), sem("pool_step")
        conv_ready, xc_ready, hist = sem("conv_ready"), sem("xc_ready"), sem("hist")
        dt_in, dtu_ready, dtw_ready, dtl_ready, adt_ready = (sem(k) for k in ("dt_in", "dtu_ready", "dtw_ready", "dtl_ready", "adt_ready"))
        Gm_ready, XpD_ready, XpP_ready, coef_ready = sem("Gm_ready"), sem("XpD_ready"), sem("XpP_ready"), sem("coef_ready")
        T_used, S_decayed, Y_ready, y2_ready, rss_ready = (sem(k) for k in ("T_used", "S_decayed", "Y_ready", "y2_ready", "rss_ready"))
        xb_ready, stats_ready = sem("xb_ready"), sem("stats_ready")
        carry = sem("carry")
        DVE_STEPS, POOL_STEPS, ACT_STEPS = MIX_STEPS
        seen = {}

        block = ctx.enter_context(nc.Block())
        x_t = io["x"].rearrange("b (c t) d -> c t b d", t=P)
        acc_t = scratch["acc0"].rearrange("(b c t) d -> c b t d", c=NC, t=P)
        xn_t = scratch["xn"].rearrange("(b c t) d -> c t b d", c=NC, t=P)

        @block.sync
        def _(sp):
            rows = lambda v, n: v.rearrange("(a n) -> a n", a=1).to_broadcast([P, n])
            for dst, src in (
                (ident[:, :], io["ident"]), (w_in[:, :, :], io["W_in"].rearrange("(k p) n -> p k n", p=P)),
                (dt_add[:, :], rows(io["b_in"][D_PROJ - HEADS:D_PROJ], HEADS)), (dt_add2[:, :], rows(io["dt_bias"], HEADS)),
                (a_exp[:, :], rows(io["A_log"], HEADS)), (d_par[:, :], rows(io["D_param"], HEADS)),
                (b_out[:, :], rows(io["b_out"], D)), (b_xbc[:, :], io["b_xbc"]), (b_z[:, :], io["b_z"]),
                (cw[:, :, :], io["conv_w"]), (cb[:, :], io["conv_b"]), (normw[:, :], io["norm_w"]),
                (sums[:, :, :], io["sums"]), (pairs[:, :, :], io["pairs"]),
                (w_out[:, :, :], io["W_out"].rearrange("(g p) n -> p g n", p=P)),
                (s_gate[:, :, :].rearrange("p k (s h) -> p k s h", s=2), io["Sg"]),
                (s_up[:, :, :].rearrange("p k (s h) -> p k s h", s=2), io["Su"]),
                (s_down[:, :, :], io["Sd"].rearrange("s (q p) d -> p (s q) d", p=P)),
            ):
                sp.dma_start(dst, src).then_inc(loaded, 16)
            with sp.Fori(0, NC) as c:
                sp.wait_ge(x_used, c + 1)
                sp.dma_start(x_ln[:, :, :], x_t[c]).then_inc(x_ready, 16)
                sp.wait_ge(xres_used, c + 1)
                sp.dma_start(x_res[:, :, :], x_t[c]).then_inc(xres_ready, 16)
                sp.wait_ge(xn_ready, c * NB + NB)
                sp.dma_start(xn_t[c], xn[:, :, :]).then_inc(xn_stored, 16)
                sp.wait_ge(a_done, adone(c, "xt", 1))
                sp.dma_start(scratch["xnT"][c], xnT[:, :, :, :].rearrange("p k b t -> p (k b t)")).then_inc(xnT_stored, 16)
                for b in range(NB):
                    sp.wait_ge(d_done, done(c, "out", b))
                    sp.dma_start(acc_t[c, b], res[:, b % 2, :]).then_inc(stored[b % 2], 16)
            for s in stored:
                sp.wait_ge(s, 16 * NC * NB // 2 + 16)
            sp.wait_ge(xn_stored, 16 * NC + 16)
            sp.wait_ge(xnT_stored, 16 * NC + 16)

        @block.gpsimd
        def _(pool):
            n = [0]

            def link(ins):
                n[0] += 1
                ins.then_inc(pool_step, 1)
                pool.wait_ge(pool_step, c * POOL_STEPS + n[0])

            nc.gpsimd.memset(xin[:, :, :, 0:3], 0.0).then_inc(zeroed, 1)
            nc.gpsimd.memset(S[:, :, :], 0.0).then_inc(zeroed, 1)
            nc.gpsimd.memset(ones[:, :], 1.0).then_inc(zeroed, 1)
            nc.gpsimd.memset(eps[:, 0:1], 1e-5).then_inc(zeroed, 1)
            nc.gpsimd.memset(eps[:, 1:2], 1e-6).then_inc(zeroed, 1)
            pool.wait_ge(zeroed, 5)
            with pool.Fori(0, NC) as c:
                pool.wait_ge(xres_ready, c * 16 + 16)
                nc.gpsimd.tensor_tensor(x_res[:, :, :], x_res[:, :, :], b_out[:, :].unsqueeze(1).to_broadcast([P, NB, D]),
                                        ALU.add).then_inc(xb_ready, 1)
                for stage, b in tile_order():
                    q, m = b % 2, c * NB + b
                    if stage == "T1":
                        pool.wait_ge(a_done, adone(c, "E", 7))
                        pool.wait_ge(d_done, done(c, "xtok", b))
                        nc.gpsimd.tensor_tensor(h8(Xp[:, q, PRE_D:8, :], 8 - PRE_D), h8b(Xd[:, q, :], 8 - PRE_D),
                                                E[:, PRE_D:8, b, :].unsqueeze(3).to_broadcast([P, 8 - PRE_D, HEADS, 8]),
                                                ALU.mult).then_inc(XpP_ready, 1)
                        pool.wait_ge(coef_ready, m + 1)
                        link(nc.gpsimd.tensor_tensor(h1(Yp[:, q, :]), h1(Xd[:, q, :]),
                                                     coef[:, q, :].unsqueeze(2).to_broadcast([P, HEADS, 8]), ALU.mult))
                    if stage == "T2":
                        for i, k in enumerate(SEQ):
                            if k in POOL_ADDS:
                                j = POOL_ADDS.index(k)
                                pool.wait_ge(d_done, done(c, "L", b, k))
                                ins = nc.gpsimd.tensor_tensor(Yp[:, q, :], Yp[:, q, :], T[:, j % 2, :], ALU.add)
                                ins.then_inc(T_used, 1)
                                pool.wait_ge(T_used, m * 4 + j + 1 + 2)
                        pool.wait_ge(d_full, c * PD + DJ.index(("L", b, "off")) + 1)
                        nc.gpsimd.tensor_tensor(h1(S[:, b, :]), h1(S[:, b, :]),
                                                E[:, SUM_ALL, b, :].unsqueeze(2).to_broadcast([P, HEADS, 8]),
                                                ALU.mult).then_inc(S_decayed, 1)
                seen["pool"] = n[0]

        @block.scalar
        def _(act):
            def A_wait(*job):
                act.wait_ge(a_full, c * PA + A.index(job) + 1)

            act.sem_inc(a_done, NA)
            act.wait_ge(zeroed, 5)
            act.wait_ge(loaded, 16 * 18)
            nc.scalar.activation(a_exp[:, :], a_exp[:, :], ACT.Exp).then_inc(setup, 1)
            with act.Fori(0, NC) as c:
                act.wait_ge(mv_ready, c * NB + NB)
                nc.scalar.activation(lnv[:, :], mv[:, :, 1], ACT.Ln, bias=eps[:, 0:1]).then_inc(act_step, 1)
                act.wait_ge(act_step, c + 1)
                nc.scalar.activation(rstd[:, :], lnv[:, :], ACT.Exp, scale=-0.5).then_inc(rstd_ready, 1)
                for i in range(2):
                    A_wait("xt", i)
                    if i == 0:
                        act.wait_ge(xnT_stored, c * 16 + 16)
                    nc.scalar.activation(xnT[:, :, 2 * i:2 * i + 2, :].rearrange("p k b t -> p b k t"),
                                         a_bank("xt", i)[:, :].rearrange("p (b k t) -> p b k t", b=2, k=2),
                                         ACT.Copy).then_inc(a_done, 1)
                for g in range(6):
                    A_wait("xbc", g)
                    if g == 0:
                        act.wait_ge(hist, c + 1)
                    nc.scalar.activation(xin[:, g, :, 3:3 + P], a_bank("xbc", g)[:, :].rearrange("p (b t) -> p b t", b=NB),
                                         ACT.Identity, bias=b_xbc[:, g:g + 1]).then_inc(a_done, 1)
                    if g == 2:
                        act.wait_ge(dt_in, c + 1)
                        nc.scalar.activation(dtu[:, :, :], dtr[:, :, :], ACT.Exp).then_inc(dtu_ready, 1)
                    if g == 4:
                        act.wait_ge(dtw_ready, c + 1)
                        nc.scalar.activation(dtl[:, :, :], dtw[:, :, :], ACT.Ln).then_inc(dtl_ready, 1)
                for g in range(4):
                    A_wait("z", g)
                    nc.scalar.activation(zs[:, g, :, :].rearrange("p b t -> p (b t)"), a_bank("z", g)[:, :], ACT.Silu,
                                         bias=b_z[:, g:g + 1]).then_inc(a_done, 1)
                for g in range(4):
                    A_wait("g", g)
                    nc.scalar.activation(hs[:, g, :, :].rearrange("p b t -> p (b t)"), a_bank("g", g)[:, :],
                                         ACT.Silu).then_inc(a_done, 1)
                for g in range(6):
                    act.wait_ge(conv_ready, c * 6 + g + 1)
                    nc.scalar.activation(xc[:, g, :, :], xc[:, g, :, :], ACT.Silu).then_inc(xc_ready, 1)
                for i in range(8):
                    A_wait("E", i)
                    nc.scalar.activation(E[:, 2 * i:2 * i + 2, :, :].rearrange("p s b h -> p (s b h)"), a_bank("E", i)[:, :],
                                         ACT.Exp).then_inc(a_done, 1)
                for stage, b in tile_order():
                    q, m = b % 2, c * NB + b
                    if stage == "T1":
                        A_wait("btok", b)
                        nc.scalar.activation(Btok[:, q, :], a_bank("btok", b)[:, 0:P], ACT.Copy).then_inc(a_done, 1)
                    if stage == "T3":
                        act.wait_ge(d_done, done(c, "yT", b))
                        nc.scalar.activation(y2[:, q, :, :], yg[:, q, :, :], ACT.Square).then_inc(y2_ready, 1)
                    if stage == "T4":
                        A_wait("ss", b)
                        nc.scalar.activation(lss[:, q:q + 1], a_bank("ss", b)[:, 0:1], ACT.Ln, scale=1.0 / INNER,
                                             bias=eps[:, 1:2]).then_inc(a_done, 1)
                        act.wait_ge(a_done, adone(c, "ss", b))
                        nc.scalar.activation(rss[:, q:q + 1], lss[:, q:q + 1], ACT.Exp, scale=-0.5).then_inc(rss_ready, 1)

        @block.tensor
        def _(pe):
            def A_open(*job):
                pe.wait_ge(a_done, c * PA + credit(A, NA, job))

            def D_open(*job):
                pe.wait_ge(d_done, c * PD + credit(DJ, ND, job))

            pe.wait_ge(loaded, 16 * 18)
            pe.wait_ge(zeroed, 5)
            pe.wait_ge(setup, 1)
            with pe.Fori(0, NC) as c:
                pe.wait_ge(xn_ready, c * NB + NB)
                for i in range(2):
                    A_open("xt", i)
                    for b in range(2):
                        for k in range(2):
                            o = (b * 2 + k) * P
                            ins = nc.tensor.transpose(a_bank("xt", i)[:, o:o + P], xn[:, 2 * i + b, k * P:(k + 1) * P], ident[:, :])
                    ins.then_inc(a_full, 1)
                pe.wait_ge(a_done, adone(c, "xt", 1))
                D_open("dt", 0)
                for b in range(NB):
                    for k in range(2):
                        ins = nc.tensor.matmul(d_bank("dt", 0)[:, b * HEADS:(b + 1) * HEADS], xnT[:, k, b, :],
                                               w_in[:, k, D_PROJ - HEADS:D_PROJ], start=(k == 0), stop=(k == 1))
                ins.then_inc(d_full, 1)

                def project(dst, w, col, full):
                    for k in range(2):
                        ins = nc.tensor.matmul(dst[:, :], w[:, k, col:col + P], xnT[:, k, :, :].rearrange("p b t -> p (b t)"),
                                               start=(k == 0), stop=(k == 1))
                    ins.then_inc(full, 1)

                for g in range(6):
                    A_open("xbc", g)
                    project(a_bank("xbc", g), w_in, INNER + g * P, a_full)
                for g in range(4):
                    A_open("z", g)
                    project(a_bank("z", g), w_in, g * P, a_full)
                for g in range(4):
                    A_open("g", g)
                    project(a_bank("g", g), s_gate, g * P, a_full)
                    D_open("u", g)
                    project(d_bank("u", g), s_up, g * P, d_full)
                pe.wait_ge(adt_ready, c + 1)
                for i in range(8):
                    A_open("E", i)
                    for s in range(2):
                        ins = nc.tensor.matmul(a_bank("E", i)[:, s * 256:(s + 1) * 256], sums[:, 2 * i + s, :],
                                               adt[:, :, :].rearrange("p b h -> p (b h)"), start=True, stop=True)
                    ins.then_inc(a_full, 1)
                for stage, b in tile_order():
                    q, m = b % 2, c * NB + b
                    if stage == "T1":
                        pe.wait_ge(xc_ready, c * 6 + 6)
                        D_open("xtok", b)
                        for g in range(4):
                            ins = nc.tensor.transpose(d_bank("xtok", b)[:, g * P:(g + 1) * P], xc[:, g, b, :], ident[:, :])
                        ins.then_inc(d_full, 1)
                        A_open("btok", b)
                        nc.tensor.transpose(a_bank("btok", b)[:, 0:P], xc[:, 4, b, :], ident[:, :]).then_inc(a_full, 1)
                        D_open("G", b)
                        nc.tensor.matmul(d_bank("G", b)[:, 0:P], xc[:, 4, b, :], xc[:, 5, b, :], start=True, stop=True).then_inc(d_full, 1)
                    if stage == "T2":
                        pe.wait_ge(Gm_ready, m + 1)
                        pe.wait_ge(XpD_ready, m + 1)
                        pe.wait_ge(XpP_ready, m + 1)
                        for k in SEQ:
                            D_open("L", b, k)
                            if k == "off":
                                nc.tensor.matmul(d_bank("L", b, k)[:, :], xc[:, 5, b, :], S[:, b, :], start=True, stop=True).then_inc(d_full, 1)
                            else:
                                nc.tensor.matmul(d_bank("L", b, k)[:, :], Gm[:, q, k, :], Xp[:, q, k, :], start=True, stop=True).then_inc(d_full, 1)
                        pe.wait_ge(a_done, adone(c, "btok", b))
                        D_open("snew", b)
                        nc.tensor.matmul(d_bank("snew", b)[:, :], Btok[:, q, :], Xp[:, q, 7, :], start=True, stop=True).then_inc(d_full, 1)
                    if stage == "T3":
                        pe.wait_ge(Y_ready, m + 1)
                        D_open("yT", b)
                        for g in range(4):
                            ins = nc.tensor.transpose(d_bank("yT", b)[:, g * P:(g + 1) * P], Yd[:, q, g * P:(g + 1) * P], ident[:, :])
                        ins.then_inc(d_full, 1)
                    if stage == "T4":
                        pe.wait_ge(y2_ready, m + 1)
                        A_open("ss", b)
                        for g in range(4):
                            ins = nc.tensor.matmul(a_bank("ss", b)[:, 0:2], y2[:, q, g, :], ones[:, :], start=(g == 0), stop=(g == 3))
                        ins.then_inc(a_full, 1)
                        pe.wait_ge(d_done, done(c, "u", 3))
                        D_open("out", b)
                        for g in range(4):
                            nc.tensor.matmul(d_bank("out", b)[:, 0:D], yg[:, q, g, :], w_out[:, g, :], start=(g == 0), stop=(g == 3))
                        for g in range(4):
                            ins = nc.tensor.matmul(d_bank("out", b)[:, D:2 * D], hs[:, g, b, :], s_down[:, g, :], start=(g == 0), stop=(g == 3))
                        ins.then_inc(d_full, 1)

        @block.vector
        def _(dve):
            n = [0]
            v = nc.vector

            def link(ins):
                n[0] += 1
                ins.then_inc(dve_step, 1)
                dve.wait_ge(dve_step, c * DVE_STEPS + n[0] + 6)

            def D_wait(*job):
                dve.wait_ge(d_full, c * PD + DJ.index(job) + 1)

            def D_done(ins, *job):
                ins.then_inc(d_done, 1)
                dve.wait_ge(d_done, done(c, *job))

            dve.sem_inc(d_done, ND)
            dve.sem_inc(x_used, 1)
            dve.sem_inc(xres_used, 1)
            dve.sem_inc(T_used, 2)
            dve.sem_inc(hist, 1)
            dve.sem_inc(stored[0], 16)
            dve.sem_inc(stored[1], 16)
            dve.sem_inc(xn_stored, 16)
            dve.sem_inc(xnT_stored, 16)
            dve.wait_ge(loaded, 16 * 18)
            dve.wait_ge(zeroed, 5)
            for g in range(4):
                v.tensor_scalar(w_out[:, g, :], w_out[:, g, :], normw[:, g:g + 1], None, ALU.mult).then_inc(dve_step, 1)
            v.tensor_tensor(dt_add[:, :], dt_add[:, :], dt_add2[:, :], ALU.add).then_inc(dve_step, 1)
            v.memset(lss[:, :], 0.0).then_inc(dve_step, 1)
            dve.wait_ge(dve_step, 6)
            dve.wait_ge(setup, 1)
            dve.sem_inc(setup, 1)
            with dve.Fori(0, NC) as c:
                dve.wait_ge(x_ready, c * 16 + 16)
                for b in range(NB):
                    ins = v.bn_stats(stats[:, b, :], x_ln[:, b, :])
                ins.then_inc(stats_ready, 1)
                dve.wait_ge(stats_ready, c + 1)
                dve.sem_inc(carry, 1)
                for b in range(NB):
                    v.bn_aggr(mv[:, b, :], stats[:, b, :]).then_inc(mv_ready, 1)
                dve.wait_ge(rstd_ready, c + 1)
                dve.wait_ge(xn_stored, c * 16 + 16)
                for b in range(NB):
                    ins = v.tensor_scalar(xn[:, b, :], x_ln[:, b, :], mv[:, b, 0:1], rstd[:, b:b + 1], ALU.subtract, ALU.mult)
                    ins.then_inc(xn_ready, 1)
                dve.wait_ge(xn_ready, c * NB + NB)
                dve.sem_inc(x_used, 1)
                D_wait("dt", 0)
                ins = v.tensor_tensor(dtr[:, :, :], d_bank("dt", 0)[:, 0:NB * HEADS].rearrange("p (b h) -> p b h", b=NB),
                                      dt_add[:, :].unsqueeze(1).to_broadcast([P, NB, HEADS]), ALU.add)
                D_done(ins, "dt", 0)
                v.tensor_scalar(dtr[:, :, :], dtr[:, :, :], 30.0, None, ALU.min).then_inc(dt_in, 1)

                def conv(g):
                    dve.wait_ge(a_done, adone(c, "xbc", g))
                    link(v.tensor_scalar(xc[:, g, :, :], xin[:, g, :, 0:P], cw[:, g, 0:1], cb[:, g:g + 1], ALU.mult, ALU.add))
                    for t in range(1, 4):
                        ins = v.scalar_tensor_tensor(out=xc[:, g, :, :], in0=xin[:, g, :, t:t + P], scalar=cw[:, g, t:t + 1],
                                                     in1=xc[:, g, :, :], op0=ALU.mult, op1=ALU.add)
                        if t < 3:
                            link(ins)
                        else:
                            ins.then_inc(conv_ready, 1)

                def up(g):
                    D_wait("u", g)
                    dve.wait_ge(a_done, adone(c, "g", g))
                    v.tensor_tensor(hs[:, g, :, :].rearrange("p b t -> p (b t)"), hs[:, g, :, :].rearrange("p b t -> p (b t)"),
                                    d_bank("u", g)[:, :], ALU.mult).then_inc(d_done, 1)

                conv(0)
                dve.wait_ge(dtu_ready, c + 1)
                v.tensor_scalar(dtw[:, :, :], dtu[:, :, :], 1.0, None, ALU.add).then_inc(dtw_ready, 1)
                conv(1)
                dve.wait_ge(dtw_ready, c + 1)
                link(v.tensor_scalar(dtd[:, :, :], dtw[:, :, :], -1.0, 1e-30, ALU.add, ALU.max))
                link(v.reciprocal(dtd[:, :, :], dtd[:, :, :]))
                link(v.tensor_tensor(dtd[:, :, :], dtd[:, :, :], dtu[:, :, :], ALU.mult))
                conv(2)
                dve.wait_ge(dtl_ready, c + 1)
                link(v.tensor_tensor(dtc[:, :, :], dtl[:, :, :], dtd[:, :, :], ALU.mult))
                link(v.tensor_scalar(dtc[:, :, :], dtc[:, :, :], 0.001, 0.1, ALU.max, ALU.min))
                v.scalar_tensor_tensor(out=adt[:, :, :], in0=dtc[:, :, :], scalar=-1.0,
                                       in1=a_exp[:, :].unsqueeze(1).to_broadcast([P, NB, HEADS]), op0=ALU.mult,
                                       op1=ALU.mult).then_inc(adt_ready, 1)
                link(v.reciprocal(d_over[:, :, :], dtc[:, :, :]))
                link(v.tensor_tensor(d_over[:, :, :], d_over[:, :, :], d_par[:, :].unsqueeze(1).to_broadcast([P, NB, HEADS]), ALU.mult))
                conv(3)
                conv(4)
                conv(5)
                dve.wait_ge(conv_ready, c * 6 + 6)
                v.tensor_copy(xin[:, :, :, 0:3], xin[:, :, :, P:P + 3]).then_inc(hist, 1)
                for g in range(4):
                    up(g)
                for stage, b in tile_order():
                    q, m = b % 2, c * NB + b
                    if stage == "T1":
                        D_wait("xtok", b)
                        ins = v.tensor_tensor(h1(Xd[:, q, :]), h1(d_bank("xtok", b)[:, :]),
                                              dtc[:, b, :].unsqueeze(2).to_broadcast([P, HEADS, 8]), ALU.mult)
                        D_done(ins, "xtok", b)
                        dve.wait_ge(a_done, adone(c, "E", 7))
                        v.tensor_tensor(h8(Xp[:, q, 0:PRE_D, :], PRE_D), h8b(Xd[:, q, :], PRE_D),
                                        E[:, 0:PRE_D, b, :].unsqueeze(3).to_broadcast([P, PRE_D, HEADS, 8]),
                                        ALU.mult).then_inc(XpD_ready, 1)
                        D_wait("G", b)
                        v.tensor_tensor(Gm[:, q, :, :], d_bank("G", b)[:, 0:P].unsqueeze(1).to_broadcast([P, LEVELS, P]),
                                        pairs[:, :, :], ALU.mult).then_inc(Gm_ready, 1)
                        D_done(v.tensor_tensor_reduce(gj[:, :], d_bank("G", b)[:, 0:P], ident[:, :], 1.0, 0.0, ALU.mult, ALU.add,
                                                      gd[:, q:q + 1]), "G", b)
                        v.tensor_scalar(coef[:, q, :], d_over[:, b, :], gd[:, q:q + 1], None, ALU.add).then_inc(coef_ready, 1)
                    if stage == "T2":
                        for i, k in enumerate(SEQ):
                            D_wait("L", b, k)
                            src = d_bank("L", b, k)
                            if k == 0:
                                D_done(v.tensor_tensor(Yd[:, q, :], Yd[:, q, :], src[:, :], ALU.add), "L", b, k)
                                continue
                            e = SUM_START if k == "off" else SUM_POST + k - 1
                            post = E[:, e, b, :].unsqueeze(2).to_broadcast([P, HEADS, 8])
                            if k in POOL_ADDS:
                                j = POOL_ADDS.index(k)
                                dve.wait_ge(T_used, m * 4 + j + 1)
                                v.tensor_tensor(h1(T[:, j % 2, :]), h1(src[:, :]), post, ALU.mult).then_inc(d_done, 1)
                            elif k == 2:
                                D_done(v.tensor_tensor(h1(Yd[:, q, :]), h1(src[:, :]), post, ALU.mult), "L", b, k)
                            else:
                                D_done(v.tensor_tensor(h1(T[:, 2, :]), h1(src[:, :]), post, ALU.mult), "L", b, k)
                                link(v.tensor_tensor(Yd[:, q, :], Yd[:, q, :], T[:, 2, :], ALU.add))
                        D_wait("snew", b)
                        dve.wait_ge(S_decayed, m + 1)
                        v.tensor_tensor(S[:, b, :], S[:, b, :], d_bank("snew", b)[:, :], ALU.add).then_inc(d_done, 1)
                        dve.wait_ge(T_used, m * 4 + 4 + 2)
                        v.tensor_tensor(Yd[:, q, :], Yd[:, q, :], Yp[:, q, :], ALU.add).then_inc(Y_ready, 1)
                    if stage == "T3":
                        D_wait("yT", b)
                        dve.wait_ge(a_done, adone(c, "z", 3))
                        v.tensor_tensor(yg[:, q, :, :], d_bank("yT", b)[:, :].rearrange("p (g t) -> p g t", g=4),
                                        zs[:, :, b, :], ALU.mult).then_inc(d_done, 1)
                    if stage == "T4":
                        D_wait("out", b)
                        dve.wait_ge(rss_ready, m + 1)
                        dve.wait_ge(xb_ready, c + 1)
                        dve.wait_ge(stored[q], c * 32 + b // 2 * 16 + 16)
                        link(v.scalar_tensor_tensor(out=res[:, q, :], in0=d_bank("out", b)[:, 0:D], scalar=rss[:, q:q + 1],
                                                    in1=x_res[:, b, :], op0=ALU.mult, op1=ALU.add))
                        v.tensor_tensor(res[:, q, :], res[:, q, :], d_bank("out", b)[:, D:2 * D], ALU.add).then_inc(d_done, 1)
                dve.wait_ge(d_done, done(c, "out", NB - 1))
                dve.sem_inc(xres_used, 1)
                seen["dve"] = n[0]
        assert (seen["dve"], seen["pool"]) == (DVE_STEPS, POOL_STEPS), seen
def router_phase(nc, io, scratch, keep):
    with ExitStack() as ctx:
        def sb(name, shape, dt=F32):
            return ctx.enter_context(nc.sbuf_tensor("r_" + name, shape, dt))

        def sem(name):
            return ctx.enter_context(nc.semaphore("r_" + name))

        wr = sb("wr", [P, 2, EXPERTS])
        rb = sb("rb", [P, EXPERTS])
        iota = sb("iota", [P, EXPERTS])
        before = sb("before", [P, P])
        ones = sb("ones", [P, P])
        zero = sb("zero", [P, 2048])
        xT = sb("xT", [P, NC, 2, P])
        xr = sb("xr", [P, NC, D])
        sc = sb("sc", [P, NC, EXPERTS])
        mx = sb("mx", [P, NC])
        t8 = sb("t8", [P, NC, 8])
        i8 = sb("i8", [P, NC, 8], U32)
        idx = sb("idx", [P, NC, K0])
        hot = sb("hot", [P, NC, K0, EXPERTS])
        prod = sb("prod", [P, NC, K0, EXPERTS])
        took = sb("took", [P, NC, EXPERTS])
        earlier = sb("earlier", [P, NC + 1, EXPERTS])
        place = sb("place", [P, NC, K0])
        full = sb("full", [P, NC, K0])
        slot = sb("slot", [P, NC, K0])
        slot_f = sb("slot_f", [P, NC, K0])
        to = sb("to", [P, NC, K0], U32)
        ps_l = ctx.enter_context(nc.psum_tensor("r_ps_l", [P, 512], F32))
        ps_p = ctx.enter_context(nc.psum_tensor("r_ps_p", [P, 512], F32))
        loaded, ready, cleared, zeroed = sem("loaded"), sem("ready"), sem("cleared"), sem("zeroed")
        logits, exped, counted, to_ready, scattered = sem("logits"), sem("exped"), sem("counted"), sem("to_ready"), sem("scattered")
        carry = sem("carry")
        shifted, took_ready, step, scat_all = sem("shifted"), sem("took_ready"), sem("step"), sem("scat_all")
        block = ctx.enter_context(nc.Block())
        xT_t = scratch["xnT"].rearrange("c p (k b t) -> b k p c t", k=2, b=NB)
        xr_t = scratch["xn"].rearrange("(b c t) d -> b t c d", c=NC, t=P)
        STEPS = ROUTER_STEPS
        seen = {}

        @block.sync
        def _(sp):
            sp.dma_start(wr[:, :, :], io["Wr"].rearrange("(k p) e -> p k e", p=P)).then_inc(loaded, 16)
            sp.dma_start(rb[:, :], io["r_bias"].rearrange("(a n) -> a n", a=1).to_broadcast([P, EXPERTS])).then_inc(loaded, 16)
            sp.dma_start(before[:, :], io["before"]).then_inc(loaded, 16)
            sp.wait_ge(zeroed, 1)
            for i in range(4):
                sp.dma_start(scratch["xb"].rearrange("(i p r) d -> i p (r d)", i=4, p=P)[i], zero[:, :]).then_inc(cleared, 16)
            with sp.Fori(0, NB) as b:
                sp.wait_ge(scattered, b + 1)
                for k in range(2):
                    sp.dma_start(xT[:, :, k, :], xT_t[b, k]).then_inc(ready, 16)
                sp.dma_start(xr[:, :, :], xr_t[b]).then_inc(ready, 16)

        @block.gpsimd
        def _(pool):
            nc.gpsimd.memset(zero[:, :], 0.0).then_inc(zeroed, 1)
            nc.gpsimd.iota(iota[:, :], [[1, EXPERTS]], base=0, channel_multiplier=0,
                           allow_small_or_imprecise_dtypes=True).then_inc(zeroed, 1)
            nc.gpsimd.memset(ones[:, :], 1.0).then_inc(zeroed, 1)
            nc.gpsimd.memset(earlier[:, :, :], 0.0).then_inc(zeroed, 1)
            pool.sem_inc(scattered, 1)
            pool.wait_ge(cleared, 64)
            with pool.Fori(0, NB) as b:
                pool.wait_ge(to_ready, b + 1)
                pool.sem_inc(carry, 1)
                for c in range(NC):
                    for k in range(K0):
                        nc.gpsimd.indirect_dma_start(
                            out=scratch["xb"], out_offset=bass.IndirectOffsetOnAxis(ap=to[:, c, k:k + 1], axis=0),
                            in_=xr[:, c, :], in_offset=None, bounds_check=EXPERTS * CAP - 1, oob_is_err=False,
                        ).then_inc(scat_all, 16)
                pool.wait_ge(scat_all, b * 16 * NC * K0 + 16 * NC * K0)
                pool.sem_inc(scattered, 1)

        @block.scalar
        def _(act):
            with act.Fori(0, NB) as b:
                act.wait_ge(shifted, b + 1)
                nc.scalar.activation(sc[:, :, :], sc[:, :, :], ACT.Exp).then_inc(exped, 1)

        @block.tensor
        def _(pe):
            pe.wait_ge(loaded, 48)
            pe.wait_ge(zeroed, 4)
            with pe.Fori(0, NB) as b:
                pe.wait_ge(ready, b * 48 + 48)
                for c in range(NC):
                    for k in range(2):
                        ins = nc.tensor.matmul(ps_l[:, c * EXPERTS:(c + 1) * EXPERTS], xT[:, c, k, :], wr[:, k, :],
                                               start=(k == 0), stop=(k == 1))
                ins.then_inc(logits, 1)
                pe.wait_ge(took_ready, b + 1)
                nc.tensor.matmul(ps_p[:, :], before[:, :], took[:, :, :].rearrange("p c e -> p (c e)"), start=True, stop=False)
                nc.tensor.matmul(ps_p[:, :], ones[:, :], earlier[:, 0:NC, :].rearrange("p c e -> p (c e)"),
                                 start=False, stop=True).then_inc(counted, 1)

        @block.vector
        def _(dve):
            n = [0]
            v = nc.vector

            def link(ins):
                n[0] += 1
                ins.then_inc(step, 1)
                dve.wait_ge(step, b * STEPS + n[0])

            def wide(ap):
                return ap.unsqueeze(2).to_broadcast([P, NC, EXPERTS])

            dve.wait_ge(loaded, 48)
            dve.wait_ge(zeroed, 4)
            with dve.Fori(0, NB) as b:
                dve.wait_ge(logits, b + 1)
                link(v.tensor_tensor(sc[:, :, :], ps_l[:, :].rearrange("p (c e) -> p c e", c=NC),
                                     rb[:, :].unsqueeze(1).to_broadcast([P, NC, EXPERTS]), ALU.add))
                link(v.tensor_reduce(mx[:, :], sc[:, :, :], AX.X, ALU.max))
                v.tensor_tensor(sc[:, :, :], sc[:, :, :], wide(mx[:, :]), ALU.subtract).then_inc(shifted, 1)
                dve.wait_ge(exped, b + 1)
                link(v.tensor_reduce(mx[:, :], sc[:, :, :], AX.X, ALU.add))
                link(v.reciprocal(mx[:, :], mx[:, :]))
                link(v.tensor_tensor(sc[:, :, :], sc[:, :, :], wide(mx[:, :]), ALU.mult))
                dve.sem_inc(carry, 1)
                for c in range(NC):
                    ins = v.max(t8[:, c, :], sc[:, c, :])
                link(ins)
                dve.sem_inc(carry, 1)
                for c in range(NC):
                    ins = v.max_index(i8[:, c, :], t8[:, c, :], sc[:, c, :])
                link(ins)
                link(v.tensor_copy(idx[:, :, :], i8[:, :, 0:K0]))
                link(v.tensor_reduce(mx[:, :], t8[:, :, 0:K0], AX.X, ALU.add))
                link(v.reciprocal(mx[:, :], mx[:, :]))
                link(v.tensor_tensor(t8[:, :, 0:K0], t8[:, :, 0:K0], mx[:, :].unsqueeze(2).to_broadcast([P, NC, K0]), ALU.mult))
                link(v.tensor_tensor(hot[:, :, :, :], iota[:, :].unsqueeze(1).unsqueeze(1).to_broadcast([P, NC, K0, EXPERTS]),
                                     idx[:, :, :].unsqueeze(3).to_broadcast([P, NC, K0, EXPERTS]), ALU.is_equal))
                link(v.tensor_reduce(took[:, :, :], hot[:, :, :, :].rearrange("p c k e -> p c e k"), AX.X, ALU.add))
                for c in range(NC):
                    ins = v.tensor_tensor(earlier[:, c + 1, :], earlier[:, c, :], took[:, c, :], ALU.add)
                    if c < NC - 1:
                        link(ins)
                ins.then_inc(took_ready, 1)
                dve.wait_ge(counted, b + 1)
                link(v.tensor_tensor(prod[:, :, :, :], hot[:, :, :, :],
                                     ps_p[:, :].rearrange("p (c e) -> p c e", c=NC).unsqueeze(2).to_broadcast([P, NC, K0, EXPERTS]),
                                     ALU.mult))
                link(v.tensor_copy(earlier[:, 0, :], earlier[:, NC, :]))
                link(v.tensor_reduce(place[:, :, :], prod[:, :, :, :], AX.X, ALU.add))
                link(v.tensor_scalar(full[:, :, :], place[:, :, :], float(CAP), None, ALU.is_lt))
                tile = keep["w_all"][:, bass.ds(b * NC, NC), :]
                link(v.tensor_tensor(tile, t8[:, :, 0:K0], full[:, :, :], ALU.mult))
                link(v.tensor_scalar(full[:, :, :], place[:, :, :], float(CAP), 1e6, ALU.is_ge, ALU.mult))
                link(v.scalar_tensor_tensor(out=slot[:, :, :], in0=idx[:, :, :], scalar=float(CAP), in1=place[:, :, :],
                                            op0=ALU.mult, op1=ALU.add))
                link(v.tensor_tensor(slot[:, :, :], slot[:, :, :], full[:, :, :], ALU.add))
                v.tensor_copy(to[:, :, :], slot[:, :, :]).then_inc(to_ready, 1)
                link(v.tensor_scalar(place[:, :, :], place[:, :, :], float(CAP - 1), None, ALU.min))
                link(v.scalar_tensor_tensor(out=slot_f[:, :, :], in0=idx[:, :, :], scalar=float(CAP), in1=place[:, :, :],
                                            op0=ALU.mult, op1=ALU.add))
                link(v.tensor_copy(keep["slot_all"][:, bass.ds(b * NC, NC), :], slot_f[:, :, :]))
                seen["dve"] = n[0]
        assert seen["dve"] == STEPS, seen


def expert_phase(nc, io, scratch):
    with ExitStack() as ctx:
        def sb(name, shape, dt=F32):
            return ctx.enter_context(nc.sbuf_tensor("e_" + name, shape, dt))

        def sem(name):
            return ctx.enter_context(nc.semaphore("e_" + name))

        PAIRS = EXPERTS // 2
        ident = sb("ident", [P, P])
        wgu = [sb(f"wgu{q}", [P, 2, 2, 2, HID0]) for q in range(2)]
        wd = [sb(f"wd{q}", [P, D]) for q in range(2)]
        xb = [sb(f"xb{q}", [P, D]) for q in range(2)]
        xbT = [sb(f"xbT{q}", [P, 2, P]) for q in range(2)]
        gate = [sb(f"gate{q}", [P, CAP]) for q in range(2)]
        y = [sb(f"y{q}", [P, D]) for q in range(2)]
        ps_x = [ctx.enter_context(nc.psum_tensor(f"e_ps_x{q}", [P, 512], F32)) for q in range(2)]
        ps_h = [ctx.enter_context(nc.psum_tensor(f"e_ps_h{q}", [P, 512], F32)) for q in range(2)]
        ps_y = [ctx.enter_context(nc.psum_tensor(f"e_ps_y{q}", [P, 512], F32)) for q in range(2)]
        loaded, carry = sem("loaded"), sem("carry")
        ready = [sem(f"ready{q}") for q in range(2)]
        stored = [sem(f"stored{q}") for q in range(2)]
        turned, xT_ready, gu_ready, silu_ready, h_ready, y_full, y_ready, used = (
            sem(k) for k in ("turned", "xT_ready", "gu_ready", "silu_ready", "h_ready", "y_full", "y_ready", "used"))
        block = ctx.enter_context(nc.Block())

        @block.sync
        def _(sp):
            sp.dma_start(ident[:, :], io["ident"]).then_inc(loaded, 16)
            with sp.Fori(0, PAIRS // 2) as i:
                for q in range(2):
                    j = i * 2 + q
                    sp.wait_ge(used, j + 1)
                    sp.dma_start(wgu[q][:, :, :, :, :].rearrange("p a e k h -> p (a e k h)"), io["wgu0"][j]).then_inc(ready[q], 16)
                    sp.dma_start(wd[q][:, :], io["wd0"].rearrange("(j p) d -> j p d", p=P)[j]).then_inc(ready[q], 16)
                    sp.dma_start(xb[q][:, :], scratch["xb"].rearrange("(j p) d -> j p d", p=P)[j]).then_inc(ready[q], 16)

        @block.scalar
        def _(act):
            for q in range(2):
                act.sem_inc(stored[q], 16)
            with act.Fori(0, PAIRS // 2) as i:
                for q in range(2):
                    j = i * 2 + q
                    act.wait_ge(gu_ready, j + 1)
                    nc.scalar.activation(gate[q][:, :], ps_h[q][:, 0:CAP], ACT.Silu).then_inc(silu_ready, 1)
                    act.wait_ge(stored[q], i * 16 + 16)
                    act.wait_ge(y_full, j + 1)
                    nc.scalar.activation(y[q][:, :], ps_y[q][:, 0:D], ACT.Copy).then_inc(y_ready, 1)
                    act.wait_ge(y_ready, j + 1)
                    act.dma_start(scratch["yb"].rearrange("(j p) d -> j p d", p=P)[j], y[q][:, :]).then_inc(stored[q], 16)
            for q in range(2):
                act.wait_ge(stored[q], 16 * PAIRS // 2 + 16)

        @block.tensor
        def _(pe):
            pe.sem_inc(used, 2)
            pe.wait_ge(loaded, 16)
            with pe.Fori(0, PAIRS // 2) as i:
                for q in range(2):
                    pe.wait_ge(ready[q], i * 48 + 48)
                    for k in range(2):
                        ins = nc.tensor.transpose(ps_x[q][:, k * P:(k + 1) * P], xb[q][:, k * P:(k + 1) * P], ident[:, :])
                    ins.then_inc(turned, 1)
                for q in range(2):
                    pe.wait_ge(xT_ready, i * 2 + q + 1)
                    for a in range(2):
                        for e in range(2):
                            for k in range(2):
                                ins = nc.tensor.matmul(ps_h[q][e * HID0:(e + 1) * HID0, a * CAP:(a + 1) * CAP], wgu[q][:, a, e, k, :],
                                                       xbT[q][:, k, e * CAP:(e + 1) * CAP], start=(k == 0), stop=(k == 1))
                    ins.then_inc(gu_ready, 1)
                for q in range(2):
                    pe.wait_ge(h_ready, i * 2 + q + 1)
                    pe.sem_inc(carry, 1)
                    for e in range(2):
                        rows = slice(e * HID0, (e + 1) * HID0)
                        ins = nc.tensor.matmul(ps_y[q][rows, 0:D], gate[q][rows, :], wd[q][rows, :], start=True, stop=True)
                    ins.then_inc(y_full, 1)
                    pe.wait_ge(y_full, i * 2 + q + 1)
                    pe.sem_inc(used, 1)

        @block.vector
        def _(dve):
            v = nc.vector
            with dve.Fori(0, PAIRS // 2) as i:
                for q in range(2):
                    dve.wait_ge(turned, i * 2 + q + 1)
                    v.tensor_copy(xbT[q][:, :, :].rearrange("p k t -> p (k t)"), ps_x[q][:, 0:2 * P]).then_inc(xT_ready, 1)
                for q in range(2):
                    dve.wait_ge(silu_ready, i * 2 + q + 1)
                    v.tensor_tensor(gate[q][:, :], gate[q][:, :], ps_h[q][:, CAP:2 * CAP], ALU.mult).then_inc(h_ready, 1)
def attention_constants():
    import numpy as np
    half = DH // 2
    freq = 1.0 / 10000.0 ** (np.arange(0, DH, 2, dtype=np.float32) / np.float32(DH))
    ang = (np.arange(SEQ_LEN, dtype=np.float32)[:, None] * freq[None, :].astype(np.float32)).astype(np.float32).astype(np.float64)
    cos, sin = np.cos(ang).T, np.sin(ang).T
    lam = 2.0 ** (-8.0 * np.arange(1, HQ + 1) / HQ)
    i = np.arange(P)
    v_dec = np.exp(lam[None, :] * (i[:, None] + 1 - P // 2))
    q_dec = np.exp(-lam[:, None] * (i[None, :] + 1 - P // 2))
    half_chunk = np.exp(-lam * (P // 2))
    return {
        "cos": np.concatenate([cos, cos]), "sin": np.concatenate([sin, -sin]),
        "mask": (i[:, None] <= i[None, :]), "v_dec": v_dec,
        "q_dec": np.broadcast_to(q_dec.reshape(1, -1), (P, HQ * P)), "half_chunk": np.broadcast_to(half_chunk[None], (P, HQ)),
    }


def attention_phase(nc, io, scratch, keep):
    with ExitStack() as ctx:
        def sb(name, shape, dt=F32):
            return ctx.enter_context(nc.sbuf_tensor("a_" + name, shape, dt))

        def sem(name):
            return ctx.enter_context(nc.semaphore("a_" + name))

        GR = HQ // HKV
        wq = sb("wq", [P, 2, HQ * DH])
        wk = sb("wk", [P, 2, HKV * DH])
        wv = sb("wv", [P, 2, HKV * DH])
        wo = sb("wo", [P, HQ, D])
        cos = sb("cos", [P, SEQ_LEN])
        sin = sb("sin", [P, SEQ_LEN])
        mask = sb("mask", [P, P])
        v_dec = sb("v_dec", [P, HQ])
        q_dec = sb("q_dec", [P, HQ, P])
        half_chunk = sb("half_chunk", [P, HQ])
        ident = sb("ident", [P, P])
        eps = sb("eps", [P, 1])
        x1 = sb("x1", [P, NB, D])
        x1r = sb("x1r", [P, NB, D])
        slot_now = sb("slot_now", [P, NB, K0], U32)
        w_now = sb("w_now", [P, NB, K0])
        gath = [sb(f"gath{q}", [P, K0, D]) for q in range(2)]
        stats = sb("stats", [P, NB, 6])
        mv = sb("mv", [P, NB, 2])
        lnv = sb("lnv", [P, NB])
        rstd = sb("rstd", [P, NB])
        xn = sb("xn", [P, NB, D])
        xnT = sb("xnT", [P, 2, NB, P])
        qT = sb("qT", [P, HQ, NB, P])
        kT = sb("kT", [P, HKV, NB, P])
        rot = sb("rot", [P, 3, NB, P])
        v = sb("v", [P, 2, HKV, DH])
        vd = sb("vd", [P, 2, HQ, DH])
        ktok = sb("ktok", [P, 2, HKV, DH])
        Sm = sb("Sm", [P, 2, GR, P])
        oT = sb("oT", [P, HQ, P])
        kv = sb("kv", [P, NB, HQ, DH])
        res = sb("res", [P, 2, D])
        NA, ND = 2, 6
        psA = [ctx.enter_context(nc.psum_tensor(f"a_psA{i}", [P, 512], F32)) for i in range(NA)]
        psD = [ctx.enter_context(nc.psum_tensor(f"a_psD{i}", [P, 512], F32)) for i in range(ND)]

        def tile_order():
            for b in range(NB):
                yield ("S", b, 0)
                yield ("S", b, 1)
                if b:
                    yield ("wo", b - 1, 0)
                for g in range(HKV):
                    yield ("o", b, g)
                    yield ("kv", b, g)
                    if g + 2 < HKV:
                        yield ("S", b, g + 2)
                yield ("end", b, 0)
            yield ("wo", NB - 1, 0)

        PREP_AT = 2
        A = [("v", b) for b in range(2)] + [("ktok", 0)]
        A += [x for b in range(1, NB) for x in ([("v", b + 1)] if b + 1 < NB else []) + [("ktok", b)]] + [("xt", 0), ("xt", 1)]
        DJ = [("rope", i) for i in range(HKV + HQ)] + [t for t in tile_order() if t[0] != "end"]
        PA, PD = len(A), len(DJ)
        PRE_A = 2

        def a_bank(*job):
            return psA[A.index(job) % NA]

        def d_bank(*job):
            return psD[DJ.index(job) % ND]

        def done(c, *job):
            return c * PD + DJ.index(job) + 1 + ND

        def adone(c, *job):
            return c * PA + A.index(job) + 1 + NA + PRE_A

        def credit(jobs, n, job):
            j = jobs.index(job)
            before = j - n if j >= n else max(i for i in range(len(jobs)) if i % n == j) - len(jobs)
            return before + 1 + n

        a_full, a_done, d_full, d_done = sem("a_full"), sem("a_done"), sem("d_full"), sem("d_done")
        loaded, setup, x_ready, x1r_ready, x_stored, xnT_stored = (
            sem(k) for k in ("loaded", "setup", "x_ready", "x1r_ready", "x_stored", "xnT_stored"))
        now_ready, stats_ready, mv_ready, lnv_ready, rstd_ready, xn_ready = (
            sem(k) for k in ("now_ready", "stats_ready", "mv_ready", "lnv_ready", "rstd_ready", "xn_ready"))
        gathered = [sem("gathered0"), sem("gathered1")]
        stored = [sem("stored0"), sem("stored1")]
        gath_used, added, roped, vd_ready, decayed, carry, half_decayed = (
            sem(k) for k in ("gath_used", "added", "roped", "vd_ready", "decayed", "carry", "half_decayed"))
        cos_done = sem("cos_done")
        block = ctx.enter_context(nc.Block())
        acc_t = scratch["acc0"].rearrange("(b c t) d -> c t b d", c=NC, t=P)
        x1_t = scratch["x1"].rearrange("(b c t) d -> c t b d", c=NC, t=P)
        acc1_t = scratch["acc1"].rearrange("(b c t) d -> c b t d", c=NC, t=P)
        slot_t = keep["slot_all"][:, :, :].rearrange("p (b c) k -> p c b k", b=NB)
        w_t = keep["w_all"][:, :, :].rearrange("p (b c) k -> p c b k", b=NB)
        N_LOAD = 11

        def steps(eng, body):
            with eng.Fori(0, NC - 1) as c:
                body(c, False)
            body(NC - 1, True)

        @block.sync
        def _(sp):
            for dst, src in (
                (ident[:, :], io["ident"]), (wk[:, :, :], io["wk"]), (wv[:, :, :], io["wv"]), (cos[:, :], io["cos"]),
                (sin[:, :], io["sin"]), (wq[:, :, :], io["wq"]), (mask[:, :], io["mask"]), (v_dec[:, :], io["v_dec"]),
                (q_dec[:, :, :], io["q_dec"].rearrange("p (h i) -> p h i", h=HQ)), (half_chunk[:, :], io["half_chunk"]),
                (wo[:, :, :], io["wo"]),
            ):
                sp.dma_start(dst, src).then_inc(loaded, 16)

            def load(c):
                sp.dma_start(x1[:, :, :], acc_t[c]).then_inc(x_ready, 16)

            def save_prep(c):
                sp.wait_ge(xn_ready, c * NB + NB)
                sp.dma_start(x1_t[c], x1[:, :, :]).then_inc(x_stored, 16)
                sp.wait_ge(a_done, adone(c - 1, "xt", 1))
                sp.dma_start(scratch["xnT1"][c], xnT[:, :, :, :].rearrange("p k b t -> p (k b t)")).then_inc(xnT_stored, 16)

            def body(c, last):
                sp.wait_ge(x_stored, c * 16 + 16)
                if not last:
                    load(c + 1)
                sp.wait_ge(d_done, c * PD + ND)
                sp.dma_start(x1r[:, :, :], x1_t[c]).then_inc(x1r_ready, 16)
                for b in range(NB):
                    if b == NB - 1 and not last:
                        save_prep(c + 1)
                    sp.wait_ge(d_done, done(c, "wo", b, 0))
                    sp.dma_start(acc1_t[c, b], res[:, b % 2, :]).then_inc(stored[b % 2], 16)

            load(0)
            save_prep(0)
            steps(sp, body)
            for s in stored:
                sp.wait_ge(s, 16 * NC * NB // 2 + 16)
            sp.wait_ge(x_stored, 16 * NC)
            sp.wait_ge(xnT_stored, 16 * NC)

        @block.gpsimd
        def _(pool):
            nc.gpsimd.memset(kv[:, :, :, :], 0.0).then_inc(setup, 1)
            nc.gpsimd.memset(eps[:, :], 1e-5).then_inc(setup, 1)
            pool.wait_ge(setup, 2)
            pool.wait_ge(loaded, 16 * N_LOAD)

            def gather(c, b):
                if b == 0:
                    pool.wait_ge(now_ready, c + 1)
                pool.wait_ge(gath_used, c * NB + b + 1)
                pool.sem_inc(carry, 1)
                for k in range(K0):
                    nc.gpsimd.indirect_dma_start(
                        out=gath[b % 2][:, k, :], out_offset=None, in_=scratch["yb"],
                        in_offset=bass.IndirectOffsetOnAxis(ap=slot_now[:, b, k:k + 1], axis=0),
                        bounds_check=EXPERTS * CAP - 1, oob_is_err=False,
                    ).then_inc(gathered[b % 2], 16)

            def values(c, b):
                pool.wait_ge(a_done, adone(c, "v", b))
                nc.gpsimd.tensor_tensor(
                    vd[:, b % 2, :, :].rearrange("p (g r) e -> p g r e", g=HKV),
                    v[:, b % 2, :, :].unsqueeze(2).to_broadcast([P, HKV, GR, DH]),
                    v_dec[:, :].rearrange("p (g r) -> p g r", g=HKV).unsqueeze(3).to_broadcast([P, HKV, GR, DH]),
                    ALU.mult).then_inc(vd_ready, 1)

            def body(c, last):
                for i in range(HKV + HQ):
                    pool.wait_ge(d_done, done(c, "rope", i))
                    dst = kT[:, i, :, :] if i < HKV else qT[:, i - HKV, :, :]
                    nc.gpsimd.tensor_tensor(dst, dst, rot[:, i % 3, :, :], ALU.add).then_inc(roped, 1)
                    if i == HKV - 1:
                        values(c, 0)
                        values(c, 1)
                if not last:
                    gather(c + 1, 0)
                    gather(c + 1, 1)
                for b in range(NB):
                    pool.wait_ge(d_done, done(c, "kv", b, HKV - 1))
                    dec = half_chunk[:, :].unsqueeze(2).to_broadcast([P, HQ, DH])
                    nc.gpsimd.tensor_tensor(kv[:, b, :, :], kv[:, b, :, :], dec, ALU.mult).then_inc(half_decayed, 1)
                    pool.wait_ge(half_decayed, c * NB + b + 1)
                    nc.gpsimd.tensor_tensor(kv[:, b, :, :], kv[:, b, :, :], dec, ALU.mult).then_inc(decayed, 1)
                    if b + 2 < NB:
                        values(c, b + 2)
                    if b == PREP_AT - 1 and not last:
                        gather(c + 1, 2)
                        gather(c + 1, 3)

            for b in range(NB):
                gather(0, b)
            steps(pool, body)

        @block.scalar
        def _(act):
            def A_wait(c, *job):
                act.wait_ge(a_full, c * PA + A.index(job) + 1 + PRE_A)

            def prep(c):
                act.wait_ge(mv_ready, c * NB + NB)
                nc.scalar.activation(lnv[:, :], mv[:, :, 1], ACT.Ln, bias=eps[:, :]).then_inc(lnv_ready, 1)
                act.wait_ge(lnv_ready, c + 1)
                nc.scalar.activation(rstd[:, :], lnv[:, :], ACT.Exp, scale=-0.5).then_inc(rstd_ready, 1)

            def turned(c):
                for i in range(2):
                    A_wait(c - 1, "xt", i)
                    if i == 0:
                        act.wait_ge(xnT_stored, c * 16 + 0) if not isinstance(c, int) or c else None
                    nc.scalar.activation(xnT[:, :, 2 * i:2 * i + 2, :].rearrange("p k b t -> p b k t"),
                                         a_bank("xt", i)[:, :].rearrange("p (b k t) -> p b k t", b=2, k=2),
                                         ACT.Copy).then_inc(a_done, 1)

            def values(c, b):
                A_wait(c, "v", b)
                act.wait_ge(vd_ready, c * NB + b - 2 + 1 + 2)
                nc.scalar.activation(v[:, b % 2, :, :].rearrange("p g e -> p (g e)"), a_bank("v", b)[:, :], ACT.Copy).then_inc(a_done, 1)

            def keys(c, b):
                A_wait(c, "ktok", b)
                nc.scalar.activation(ktok[:, b % 2, :, :].rearrange("p g e -> p (g e)"), a_bank("ktok", b)[:, :], ACT.Copy).then_inc(a_done, 1)

            def body(c, last):
                for kind, b in A:
                    if kind == "v":
                        values(c, b)
                    if kind == "ktok":
                        keys(c, b)
                        if b == PREP_AT and not last:
                            prep(c + 1)
                if not last:
                    turned(c + 1)

            act.sem_inc(a_done, NA)
            act.wait_ge(setup, 2)
            prep(0)
            turned(0)
            steps(act, body)

        @block.tensor
        def _(pe):
            def A_open(c, *job):
                pe.wait_ge(a_done, c * PA + credit(A, NA, job) + PRE_A)

            def D_open(c, *job):
                pe.wait_ge(d_done, c * PD + credit(DJ, ND, job))

            def turn(c):
                pe.wait_ge(xn_ready, c * NB + NB)
                for i in range(2):
                    A_open(c - 1, "xt", i)
                    for b in range(2):
                        for k in range(2):
                            o = (b * 2 + k) * P
                            ins = nc.tensor.transpose(a_bank("xt", i)[:, o:o + P], xn[:, 2 * i + b, k * P:(k + 1) * P], ident[:, :])
                    ins.then_inc(a_full, 1)

            def values(c, b):
                A_open(c, "v", b)
                for k in range(2):
                    ins = nc.tensor.matmul(a_bank("v", b)[:, :], xnT[:, k, b, :], wv[:, k, :], start=(k == 0), stop=(k == 1))
                ins.then_inc(a_full, 1)

            def keys(c, b):
                A_open(c, "ktok", b)
                for g in range(HKV):
                    ins = nc.tensor.transpose(a_bank("ktok", b)[:, g * P:(g + 1) * P], kT[:, g, b, :], ident[:, :])
                ins.then_inc(a_full, 1)

            def body(c, last):
                pe.wait_ge(a_done, adone(c - 1, "xt", 1))
                values(c, 0)
                values(c, 1)
                for i in range(HKV + HQ):
                    D_open(c, "rope", i)
                    w, n = (wk, i) if i < HKV else (wq, i - HKV)
                    for k in range(2):
                        ins = nc.tensor.matmul(d_bank("rope", i)[:, :], w[:, k, n * P:(n + 1) * P],
                                               xnT[:, k, :, :].rearrange("p b t -> p (b t)"), start=(k == 0), stop=(k == 1))
                    ins.then_inc(d_full, 1)
                pe.wait_ge(roped, c * (HKV + HQ) + HKV)
                keys(c, 0)
                pe.wait_ge(roped, (c + 1) * (HKV + HQ))
                for job in tile_order():
                    stage, b, g = job
                    q = b % 2
                    if stage == "end":
                        continue
                    if stage == "S" and g == 0 and b:
                        if b + 1 < NB:
                            values(c, b + 1)
                        keys(c, b)
                    D_open(c, *job)
                    out = d_bank(*job)
                    if stage == "S":
                        nc.tensor.matmul(out[:, :], kT[:, g, b, :], qT[:, GR * g:GR * g + GR, b, :], start=True, stop=True).then_inc(d_full, 1)
                    if stage == "o":
                        if g == 0:
                            pe.wait_ge(vd_ready, c * NB + b + 1 + 2)
                            pe.wait_ge(decayed, c * NB + b + 1)
                        pe.wait_ge(d_done, done(c, "S", b, g))
                        for r in range(GR):
                            h = GR * g + r
                            nc.tensor.matmul(out[:, r * P:(r + 1) * P], vd[:, q, h, :], Sm[:, g % 2, r, :], start=True, stop=False)
                            ins = nc.tensor.matmul(out[:, r * P:(r + 1) * P], kv[:, b, h, :], qT[:, h, b, :], start=False, stop=True)
                        ins.then_inc(d_full, 1)
                    if stage == "kv":
                        pe.wait_ge(a_done, adone(c, "ktok", b))
                        nc.tensor.matmul(out[:, :], ktok[:, q, g, :], vd[:, q, GR * g:GR * g + GR, :], start=True, stop=True).then_inc(d_full, 1)
                    if stage == "wo":
                        if b == NB - 1 and not last:
                            turn(c + 1)
                        pe.wait_ge(d_done, done(c, "o", b, HKV - 1))
                        for h in range(HQ):
                            ins = nc.tensor.matmul(out[:, 0:D], oT[:, h, :], wo[:, h, :], start=(h == 0), stop=(h == HQ - 1))
                        ins.then_inc(d_full, 1)

            pe.sem_inc(vd_ready, 2)
            pe.sem_inc(decayed, NB)
            pe.wait_ge(loaded, 16 * N_LOAD)
            pe.wait_ge(setup, 2)
            turn(0)
            steps(pe, body)

        @block.vector
        def _(dve):
            n = [0]
            vec = nc.vector

            def now(c):
                vec.tensor_copy(slot_now[:, :, :], slot_t[:, c, :, :]).then_inc(now_ready, 1)
                vec.tensor_copy(w_now[:, :, :], w_t[:, c, :, :]).then_inc(added, 1)

            ADDS = 1 + NB * K0

            def combine(c, b):
                q = b % 2
                if b == 0:
                    dve.wait_ge(x_ready, c * 16 + 16)
                dve.wait_ge(gathered[q], (c * 2 + b // 2) * 16 * K0 + 16 * K0)
                for k in range(K0):
                    dve.wait_ge(added, c * ADDS + 1 + b * K0 + k)
                    vec.scalar_tensor_tensor(out=x1[:, b, :], in0=gath[q][:, k, :], scalar=w_now[:, b, k:k + 1],
                                             in1=x1[:, b, :], op0=ALU.mult, op1=ALU.add).then_inc(added, 1)
                dve.wait_ge(added, c * ADDS + 1 + b * K0 + K0)
                dve.sem_inc(gath_used, 1)

            def norm(c):
                for b in range(NB):
                    ins = vec.bn_stats(stats[:, b, :], x1[:, b, :])
                ins.then_inc(stats_ready, 1)
                dve.wait_ge(stats_ready, c + 1)
                dve.sem_inc(carry, 1)
                for b in range(NB):
                    vec.bn_aggr(mv[:, b, :], stats[:, b, :]).then_inc(mv_ready, 1)
                dve.wait_ge(rstd_ready, c + 1)
                for b in range(NB):
                    vec.tensor_scalar(xn[:, b, :], x1[:, b, :], mv[:, b, 0:1], rstd[:, b:b + 1], ALU.subtract,
                                      ALU.mult).then_inc(xn_ready, 1)

            def body(c, last):
                at = cos[:, bass.ds(c * P, P)], sin[:, bass.ds(c * P, P)]
                for i in range(HKV + HQ):
                    dve.wait_ge(d_full, c * PD + DJ.index(("rope", i)) + 1)
                    if i >= 3:
                        dve.wait_ge(roped, c * (HKV + HQ) + i - 2)
                    src = d_bank("rope", i)
                    dst = kT[:, i, :, :] if i < HKV else qT[:, i - HKV, :, :]
                    vec.tensor_tensor(dst, src[:, :].rearrange("p (b t) -> p b t", b=NB),
                                      at[0].unsqueeze(1).to_broadcast([P, NB, P]), ALU.mult)
                    for lo, hi in ((0, 64), (64, 0)):
                        ins = vec.tensor_tensor(rot[lo:lo + 64, i % 3, :, :], src[hi:hi + 64, :].rearrange("p (b t) -> p b t", b=NB),
                                                at[1][hi:hi + 64, :].unsqueeze(1).to_broadcast([64, NB, P]), ALU.mult)
                    ins.then_inc(d_done, 1)
                if not last:
                    now(c + 1)
                for job in tile_order():
                    stage, b, g = job
                    if stage == "end":
                        if not last and b == PREP_AT - 1:
                            combine(c + 1, 0)
                            combine(c + 1, 1)
                        if not last and b == PREP_AT:
                            combine(c + 1, 2)
                            combine(c + 1, 3)
                            norm(c + 1)
                        continue
                    dve.wait_ge(d_full, c * PD + DJ.index(job) + 1)
                    src = d_bank(*job)
                    if stage == "S":
                        vec.tensor_tensor(Sm[:, g % 2, :, :], src[:, :].rearrange("p (r i) -> p r i", r=GR),
                                          mask[:, :].unsqueeze(1).to_broadcast([P, GR, P]), ALU.mult).then_inc(d_done, 1)
                    if stage == "o":
                        vec.tensor_tensor(oT[:, GR * g:GR * g + GR, :], src[:, :].rearrange("p (r i) -> p r i", r=GR),
                                          q_dec[:, GR * g:GR * g + GR, :], ALU.mult).then_inc(d_done, 1)
                    if stage == "kv":
                        part = kv[:, b, GR * g:GR * g + GR, :]
                        vec.tensor_tensor(part, part, src[:, :].rearrange("p (r i) -> p r i", r=GR), ALU.add).then_inc(d_done, 1)
                    if stage == "wo":
                        if b == 0:
                            dve.wait_ge(x1r_ready, c * 16 + 16)
                        dve.wait_ge(stored[b % 2], c * 32 + b // 2 * 16 + 16)
                        vec.tensor_tensor(res[:, b % 2, :], src[:, 0:D], x1r[:, b, :], ALU.add).then_inc(d_done, 1)

            dve.sem_inc(d_done, ND)
            dve.sem_inc(gath_used, 2)
            for s in stored:
                dve.sem_inc(s, 16)
            dve.wait_ge(loaded, 16 * N_LOAD)
            dve.wait_ge(setup, 2)
            now(0)
            for b in range(NB):
                combine(0, b)
            norm(0)
            steps(dve, body)


def ffn_phase(nc, io, scratch, out):
    with ExitStack() as ctx:
        def sb(name, shape, dt=F32):
            return ctx.enter_context(nc.sbuf_tensor("f_" + name, shape, dt))

        def sem(name):
            return ctx.enter_context(nc.semaphore("f_" + name))

        NE = E1 + 1
        wg = sb("wg", [P, 2, NE, P])
        wu = sb("wu", [P, 2, NE, P])
        wd = sb("wd", [P, NE, D])
        gw = sb("gw", [P, 2, E1])
        bias = sb("bias", [P, E1])
        iota = sb("iota", [P, E1])
        xT = sb("xT", [P, 2, 2, NB, P])
        acc = sb("acc", [P, 2, NB, D])
        score = sb("score", [P, NB, E1])
        picked = sb("picked", [P, NB, E1])
        t8 = sb("t8", [P, NB, 8])
        i8 = sb("i8", [P, NB, 8], U32)
        idx = sb("idx", [P, NB, 4])
        hot = sb("hot", [P, NB, 4, E1])
        tot = sb("tot", [P, NB])
        cw = sb("cw", [P, 2, NB, NE])
        h = sb("h", [P, 2, NB * P])
        NG = 2
        psG = [ctx.enter_context(nc.psum_tensor(f"f_psG{i}", [P, 512], F32)) for i in range(NG)]
        psU = [ctx.enter_context(nc.psum_tensor(f"f_psU{i}", [P, 512], F32)) for i in range(NG)]
        psY = [ctx.enter_context(nc.psum_tensor(f"f_psY{i}", [P, 512], F32)) for i in range(4)]
        loaded, setup, carry = sem("loaded"), sem("setup"), sem("carry")
        ready = [sem("ready0"), sem("ready1")]
        stored = [sem("stored0"), sem("stored1")]
        logit, scored, step, cw_ready, g_full, u_full, silu, h_ready, y_full, y_used = (
            sem(k) for k in ("logit", "scored", "step", "cw_ready", "g_full", "u_full", "silu", "h_ready", "y_full", "y_used"))
        block = ctx.enter_context(nc.Block())
        acc1_t = scratch["acc1"].rearrange("(b c t) d -> c t b d", c=NC, t=P)
        out_t = out.rearrange("b (c t) d -> c t b d", t=P)
        STEPS = GATE_STEPS
        seen = {}

        def at(q, e):
            return (q * NE + e) % 2

        def pairs(eng, body):
            with eng.Fori(0, NC // 2) as i:
                for q in range(2):
                    body(i * 2 + q, i, q)

        @block.sync
        def _(sp):
            for dst, src in ((gw[:, :, :], io["gw1"]), (bias[:, :], io["bias1"].rearrange("(a n) -> a n", a=1).to_broadcast([P, E1])),
                             (wg[:, :, :, :], io["wg1"]), (wu[:, :, :, :], io["wu1"]), (wd[:, :, :], io["wd1"])):
                sp.dma_start(dst, src).then_inc(loaded, 16)

            def body(c, i, q):
                sp.wait_ge(stored[q], i * 16 + 16)
                sp.dma_start(xT[:, q, :, :, :].rearrange("p k b t -> p (k b t)"), scratch["xnT1"][c]).then_inc(ready[q], 16)
                sp.dma_start(acc[:, q, :, :], acc1_t[c]).then_inc(ready[q], 16)

            pairs(sp, body)

        @block.gpsimd
        def _(pool):
            nc.gpsimd.iota(iota[:, :], [[1, E1]], base=0, channel_multiplier=0,
                           allow_small_or_imprecise_dtypes=True).then_inc(setup, 1)
            nc.gpsimd.memset(cw[:, :, :, :], 1.0).then_inc(setup, 1)

        @block.scalar
        def _(act):
            def body(c, i, q):
                act.wait_ge(logit, c + 1)
                nc.scalar.activation(score[:, :, :], psG[0][:, 0:NB * E1].rearrange("p (b e) -> p b e", b=NB), ACT.Sigmoid).then_inc(scored, 1)
                for e in range(NE):
                    m = c * NE + e
                    act.wait_ge(g_full, m + 1)
                    act.wait_ge(y_full, (m - 2) * 2 + 2 + 4)
                    nc.scalar.activation(h[:, at(q, e), :], psG[at(q, e)][:, :], ACT.Silu).then_inc(silu, 1)
                act.wait_ge(y_used, (c * NE + NE) * 2 + 4)
                act.dma_start(out_t[c], acc[:, q, :, :]).then_inc(stored[q], 16)

            act.sem_inc(stored[0], 16)
            act.sem_inc(stored[1], 16)
            act.sem_inc(y_full, 4)
            act.wait_ge(setup, 2)
            pairs(act, body)
            for s in stored:
                act.wait_ge(s, 16 * NC // 2 + 16)

        @block.tensor
        def _(pe):
            pe.wait_ge(loaded, 16 * 5)

            def up(c, q, e):
                m = c * NE + e
                pe.wait_ge(silu, m - NG + 1 + NG)
                for k in range(2):
                    ins = nc.tensor.matmul(psG[at(q, e)][:, :], wg[:, k, e, :], xT[:, q, k, :, :].rearrange("p b t -> p (b t)"),
                                           start=(k == 0), stop=(k == 1))
                ins.then_inc(g_full, 1)
                pe.wait_ge(h_ready, m - NG + 1 + NG)
                for k in range(2):
                    ins = nc.tensor.matmul(psU[at(q, e)][:, :], wu[:, k, e, :], xT[:, q, k, :, :].rearrange("p b t -> p (b t)"),
                                           start=(k == 0), stop=(k == 1))
                ins.then_inc(u_full, 1)

            def down(c, q, e):
                m = c * NE + e
                pe.wait_ge(h_ready, m + 1 + NG)
                for j in range(2):
                    y = m * 2 + j
                    pe.wait_ge(y_used, y - 4 + 1 + 4)
                    dst = psY[((q * NE + e) * 2 + j) % 4]
                    for r in range(2):
                        b = 2 * j + r
                        ins = nc.tensor.matmul(dst[:, r * D:(r + 1) * D], h[:, at(q, e), b * P:(b + 1) * P], wd[:, e, :], start=True, stop=True)
                    ins.then_inc(y_full, 1)

            def body(c, i, q):
                pe.wait_ge(ready[q], i * 32 + 32)
                pe.wait_ge(silu, c * NE + NG)
                for b in range(NB):
                    for k in range(2):
                        ins = nc.tensor.matmul(psG[0][:, b * E1:(b + 1) * E1], xT[:, q, k, b, :], gw[:, k, :], start=(k == 0), stop=(k == 1))
                ins.then_inc(logit, 1)
                pe.wait_ge(scored, c + 1)
                up(c, q, 0)
                for e in range(NE):
                    if e + 1 < NE:
                        up(c, q, e + 1)
                    down(c, q, e)

            pe.sem_inc(silu, NG)
            pe.sem_inc(h_ready, NG)
            pe.sem_inc(y_used, 4)
            pairs(pe, body)

        @block.vector
        def _(dve):
            n = [0]
            v = nc.vector

            def body(c, i, q):
                n[0] = 0

                def link(ins):
                    n[0] += 1
                    ins.then_inc(step, 1)
                    dve.wait_ge(step, c * STEPS + n[0])

                def gates():
                    dve.wait_ge(scored, c + 1)
                    link(v.tensor_tensor(picked[:, :, :], score[:, :, :], bias[:, :].unsqueeze(1).to_broadcast([P, NB, E1]), ALU.add))
                    dve.sem_inc(carry, 1)
                    for b in range(NB):
                        ins = v.max(t8[:, b, :], picked[:, b, :])
                    link(ins)
                    dve.sem_inc(carry, 1)
                    for b in range(NB):
                        ins = v.max_index(i8[:, b, :], t8[:, b, :], picked[:, b, :])
                    link(ins)
                    link(v.tensor_copy(idx[:, :, :], i8[:, :, 0:4]))
                    link(v.tensor_tensor(hot[:, :, :, :], iota[:, :].unsqueeze(1).unsqueeze(1).to_broadcast([P, NB, 4, E1]),
                                         idx[:, :, :].unsqueeze(3).to_broadcast([P, NB, 4, E1]), ALU.is_equal))
                    link(v.tensor_reduce(picked[:, :, :], hot[:, :, :, :].rearrange("p b k e -> p b e k"), AX.X, ALU.add))
                    link(v.tensor_tensor(picked[:, :, :], picked[:, :, :], score[:, :, :], ALU.mult))
                    link(v.tensor_reduce(tot[:, :], picked[:, :, :], AX.X, ALU.add))
                    link(v.reciprocal(tot[:, :], tot[:, :]))
                    link(v.tensor_tensor(cw[:, q, :, 0:E1], picked[:, :, :], tot[:, :].unsqueeze(2).to_broadcast([P, NB, E1]), ALU.mult))

                def product(e):
                    m = c * NE + e
                    dve.wait_ge(u_full, m + 1)
                    dve.wait_ge(silu, m + 1 + NG)
                    v.tensor_tensor(h[:, at(q, e), :], h[:, at(q, e), :], psU[at(q, e)][:, :], ALU.mult).then_inc(h_ready, 1)

                def gather(e):
                    m = c * NE + e
                    for j in range(2):
                        y = m * 2 + j
                        dve.wait_ge(y_full, y + 1 + 4)
                        for r in range(2):
                            b = 2 * j + r
                            ins = v.scalar_tensor_tensor(out=acc[:, q, b, :], in0=psY[((q * NE + e) * 2 + j) % 4][:, r * D:(r + 1) * D],
                                                         scalar=cw[:, q, b, e:e + 1], in1=acc[:, q, b, :], op0=ALU.mult, op1=ALU.add)
                        ins.then_inc(y_used, 1)

                product(0)
                gates()
                dve.wait_ge(ready[q], i * 32 + 32)
                for e in range(NE):
                    if e + 1 < NE:
                        product(e + 1)
                    if e:
                        dve.wait_ge(y_used, (c * NE + e) * 2 + 4)
                    gather(e)
                seen["dve"] = n[0]

            dve.wait_ge(setup, 2)
            dve.wait_ge(loaded, 16 * 5)
            pairs(dve, body)
        assert seen["dve"] == STEPS, seen

def kernel(**inputs):
    import numpy as np
    import concourse.bacc as bacc
    from concourse.bass_utils import run_bass_kernel_spmd as run

    nc = bacc.Bacc("TRN2", target_bir_lowering=False, num_devices=1)
    arrays, io = {}, {}

    def give(name, a):
        arrays["in_" + name] = np.ascontiguousarray(a)
        io[name] = nc.dram_tensor("in_" + name, arrays["in_" + name].shape, F32, kind="ExternalInput").ap()

    I = {k: np.asarray(v) for k, v in inputs.items()}
    m = "L0_attn_"
    give("x", I[m + "x"])
    give("W_in", I[m + "W_in"])
    give("b_in", I[m + "b_in"])
    give("b_xbc", I[m + "b_in"][INNER:2 * INNER + 2 * D_STATE].reshape(6, P).T)
    give("b_z", I[m + "b_in"][:INNER].reshape(4, P).T)
    give("conv_w", I[m + "conv_w"].reshape(4, 6, P).transpose(2, 1, 0))
    give("conv_b", I[m + "conv_b"].reshape(6, P).T)
    give("norm_w", I[m + "norm_w"].reshape(4, P).T)
    for n in ("A_log", "dt_bias", "D_param", "W_out", "b_out"):
        give(n, I[m + n])
    give("Sg", I["L0_ffn_Sg"].reshape(2, 2, P, 256).transpose(2, 1, 0, 3))
    give("Su", I["L0_ffn_Su"].reshape(2, 2, P, 256).transpose(2, 1, 0, 3))
    give("Sd", I["L0_ffn_Sd"])
    sums, pairs = level_constants()
    give("sums", sums)
    give("pairs", pairs)
    give("ident", np.eye(P, dtype=np.float32))
    give("Wr", I["L0_ffn_Wr"])
    give("r_bias", I["L0_ffn_router_bias"])
    give("before", np.triu(np.ones((P, P), np.float32), 1))
    gu = np.stack([I["L0_ffn_Wg"], I["L0_ffn_Wu"]]).reshape(2, EXPERTS // 2, 2, 2, P, HID0)
    give("wgu0", gu.transpose(1, 4, 0, 2, 3, 5).reshape(EXPERTS // 2, P, 8 * HID0))
    give("wd0", I["L0_ffn_Wd"].reshape(EXPERTS * HID0, D))
    n = "L1_attn_"
    for w in ("wq", "wk", "wv"):
        a = I[n + w]
        give(w, a.T.reshape(2, P, a.shape[0]).transpose(1, 0, 2))
    give("wo", I[n + "wo"].T.reshape(HQ, P, D).transpose(1, 0, 2))
    for k, a in attention_constants().items():
        give(k, a.astype(np.float32))
    f = "L1_ffn_"
    for k, w in (("wg1", "gate"), ("wu1", "up")):
        a = np.concatenate([I[f + "w_" + w], I[f + "sw_" + w][None]])
        give(k, a.reshape(E1 + 1, P, 2, P).transpose(3, 2, 0, 1))
    give("wd1", np.concatenate([I[f + "w_down"], I[f + "sw_down"][None]]).transpose(2, 0, 1))
    give("gw1", I[f + "gate_w"].T.reshape(2, P, E1).transpose(1, 0, 2))
    give("bias1", I[f + "expert_bias"])
    scratch = {}
    kind = "ExternalOutput" if DEBUG else "Internal"
    for n, shape in (("acc0", (N_TOK, D)), ("xb", (EXPERTS * CAP, D)), ("yb", (EXPERTS * CAP, D)), ("xn", (N_TOK, D)), ("xnT", (NC, P, 2 * NB * P)), ("x1", (N_TOK, D)), ("acc1", (N_TOK, D)),
                     ("xnT1", (NC, P, 2 * NB * P))):
        scratch[n] = nc.dram_tensor("s_" + n, shape, F32, kind=kind).ap()
    out = nc.dram_tensor("out", (NB, SEQ_LEN, D), F32, kind="ExternalOutput").ap()
    mixer_phase(nc, io, scratch)
    with ExitStack() as ctx:
        keep = {"w_all": ctx.enter_context(nc.sbuf_tensor("w_all", [P, NB * NC, K0], F32)),
                "slot_all": ctx.enter_context(nc.sbuf_tensor("slot_all", [P, NB * NC, K0], U32))}
        router_phase(nc, io, scratch, keep)
        expert_phase(nc, io, scratch)
        attention_phase(nc, io, scratch, keep)
    ffn_phase(nc, io, scratch, out)
    r = run(nc, [arrays], core_ids=[0])
    return r.results[0]["out"]
```

```python
from contextlib import ExitStack

import concourse.bass as bass
from concourse import mybir

ALU = mybir.AluOpType
ACT = mybir.ActivationFunctionType
F32 = mybir.dt.float32
FR = mybir.dt.float32r
U32 = mybir.dt.uint32
AX = mybir.AxisListType
P = 128
NB, SEQ_LEN, D = 4, 1024, 256
NC = SEQ_LEN // P
N_TOK = NB * SEQ_LEN
INNER, HEADS, D_STATE = 512, 64, 128
D_PROJ = 2 * INNER + 2 * D_STATE + HEADS
LEVELS = 7
HQ, HKV, DH = 16, 4, 128
E1 = 16
GATE_STEPS = 10
EXPERTS, K0, CAP, HID0 = 64, 4, 64, 64
ROUTER_STEPS = 31
SUM_END, SUM_POST, SUM_START, SUM_ALL = LEVELS, LEVELS + 1, 2 * LEVELS, 2 * LEVELS + 1
N_SUMS = 2 * LEVELS + 2
PRE_D = 4
POOL_ADDS = [1, "off", 4, 6]
MIX_STEPS = (33, 4, 0)


def h1(ap):
    return ap.rearrange("p (h e) -> p h e", e=8)


def h8(ap, n):
    return ap.rearrange("p k (h e) -> p k h e", e=8)


def h8b(ap, n):
    return h1(ap).unsqueeze(1).to_broadcast([P, n, HEADS, 8])

DEBUG = False
def level_constants():
    import numpy as np
    t = np.arange(128)
    sums = np.zeros((N_SUMS, 128, 128), np.float32)
    pairs = np.zeros((LEVELS, 128, 128), np.float32)
    for k in range(LEVELS):
        for m in range(128):
            mid = ((m >> (k + 1)) << (k + 1)) + (1 << k)
            if m < mid:
                sums[k, :, m] = (t > m) & (t <= (mid if k == 0 else mid - 1))
                pairs[k, m, :] = (t >= mid) & (t < mid + (1 << k))
            elif k > 0:
                sums[SUM_POST + k - 1, :, m] = (t >= mid) & (t <= m)
    for m in range(128):
        sums[SUM_END, :, m] = t > m
        sums[SUM_START, :, m] = t <= m
    sums[SUM_ALL] = 1.0
    return np.ascontiguousarray(sums.transpose(1, 0, 2)), np.ascontiguousarray(pairs.transpose(1, 0, 2))


def mixer_phase(nc, io, scratch):
    with ExitStack() as ctx:
        def sb(name, shape, dt=F32):
            return ctx.enter_context(nc.sbuf_tensor("m_" + name, shape, dt))

        def sem(name):
            return ctx.enter_context(nc.semaphore("m_" + name))

        w_in = sb("w_in", [P, 2, D_PROJ])
        w_out = sb("w_out", [P, 4, D])
        s_gate = sb("s_gate", [P, 2, 512])
        s_up = sb("s_up", [P, 2, 512])
        s_down = sb("s_down", [P, 4, D])
        b_xbc = sb("b_xbc", [P, 6])
        b_z = sb("b_z", [P, 4])
        cw = sb("cw", [P, 6, 4])
        cb = sb("cb", [P, 6])
        normw = sb("normw", [P, 4])
        dt_add = sb("dt_add", [P, HEADS])
        dt_add2 = sb("dt_add2", [P, HEADS])
        a_exp = sb("a_exp", [P, HEADS])
        d_par = sb("d_par", [P, HEADS])
        b_out = sb("b_out", [P, D])
        sums = sb("sums", [P, N_SUMS, P])
        pairs = sb("pairs", [P, LEVELS, P])
        ident = sb("ident", [P, P])
        ones = sb("ones", [P, 2])
        eps = sb("eps", [P, 2])
        x_ln = sb("x_ln", [P, NB, D])
        x_res = sb("x_res", [P, NB, D])
        xn = sb("xn", [P, NB, D])
        stats = sb("stats", [P, NB, 6])
        mv = sb("mv", [P, NB, 2])
        lnv = sb("lnv", [P, NB])
        rstd = sb("rstd", [P, NB])
        xnT = sb("xnT", [P, 2, NB, P])
        xin = sb("xin", [P, 6, NB, P + 3])
        xc = sb("xc", [P, 6, NB, P])
        zs = sb("zs", [P, 4, NB, P])
        hs = sb("hs", [P, 4, NB, P])
        E = sb("E", [P, N_SUMS, NB, HEADS])
        dtr = sb("dtr", [P, NB, HEADS])
        dtu = sb("dtu", [P, NB, HEADS])
        dtw = sb("dtw", [P, NB, HEADS])
        dtl = sb("dtl", [P, NB, HEADS])
        dtd = sb("dtd", [P, NB, HEADS])
        dtc = sb("dtc", [P, NB, HEADS])
        adt = sb("adt", [P, NB, HEADS])
        d_over = sb("d_over", [P, NB, HEADS])
        Xd = sb("Xd", [P, 2, 512])
        Xp = sb("Xp", [P, 2, 8, 512])
        Gm = sb("Gm", [P, 2, LEVELS, P])
        gj = sb("gj", [P, P])
        gd = sb("gd", [P, 2])
        coef = sb("coef", [P, 2, HEADS])
        Btok = sb("Btok", [P, 2, P])
        Yd = sb("Yd", [P, 2, 512])
        Yp = sb("Yp", [P, 2, 512])
        T = sb("T", [P, 4, 512])
        S = sb("S", [P, NB, 512])
        yg = sb("yg", [P, 2, 4, P])
        y2 = sb("y2", [P, 2, 4, P])
        lss = sb("lss", [P, 2])
        rss = sb("rss", [P, 2])
        res = sb("res", [P, 2, D])
        NA, ND = 2, 6
        psA = [ctx.enter_context(nc.psum_tensor(f"m_psA{i}", [P, 512], F32)) for i in range(NA)]
        psD = [ctx.enter_context(nc.psum_tensor(f"m_psD{i}", [P, 512], F32)) for i in range(ND)]

        SEQ = [1, 2, 0, "off", 3, 4, 5, 6]
        LATE = [("T4", 2), ("T3", 3), ("T4", 3)]
        ORDER = [("dt", 0), ("xbc", 0), ("xbc", 1), ("xbc", 2), ("T4", 2), ("xbc", 3), ("T3", 3), ("xbc", 4), ("xbc", 5),
                 ("z", 0), ("z", 1), ("z", 2), ("z", 3), ("T4", 3)] + [("E", i) for i in range(8)] \
            + [("gu", 0), ("gu", 1), ("T1", 0), ("gu", 2), ("gu", 3), ("T1", 1), ("T2", 0), ("T1", 2), ("T2", 1), ("T3", 0),
               ("T1", 3), ("T2", 2), ("T4", 0), ("T3", 1), ("T2", 3), ("xt", 0), ("T4", 1), ("T3", 2)]
        TAIL = ORDER[:ORDER.index(("T4", 3)) + 1]

        def a_jobs(stage, b):
            return {"xbc": [("xbc", b)], "z": [("z", b)], "E": [("E", b)], "gu": [("g", b)], "T1": [("btok", b)], "T4": [("ss", b)],
                    "xt": [("xt", 0), ("xt", 1)]}.get(stage, [])

        def d_jobs(stage, b):
            return {"dt": [("dt", 0)], "gu": [("u", b)], "T1": [("xtok", b), ("G", b)],
                    "T2": [("L", b, k) for k in SEQ] + [("snew", b)], "T3": [("yT", b)], "T4": [("out", b)]}.get(stage, [])

        A = [j for s in ORDER for j in a_jobs(*s)]
        DJ = [j for s in ORDER for j in d_jobs(*s)]
        PA, PD = len(A), len(DJ)
        PRE_A = PA - A.index(("xt", 0))

        def bank(jobs, ring, job):
            return ring[jobs.index(job) % len(ring)]

        def a_bank(*job):
            return bank(A, psA, job)

        def d_bank(*job):
            return bank(DJ, psD, job)

        def done(c, *job):
            return c * PD + DJ.index(job) + 1 + ND

        def adone(c, *job):
            return c * PA + A.index(job) + 1 + NA + PRE_A

        def credit(jobs, n, job):
            j = jobs.index(job)
            before = j - n if j >= n else max(i for i in range(len(jobs)) if i % n == j) - len(jobs)
            return before + 1 + n

        def skip(eng, full_or_done, jobs, n, stage_jobs, c):
            for job in stage_jobs:
                if c * len(jobs) + jobs.index(job) + n > 0:
                    eng.wait_ge(full_or_done, c * len(jobs) + jobs.index(job) + n)
                eng.sem_inc(full_or_done, 1)

        def steps(eng, body):
            body(0, ORDER, True, False)
            with eng.Fori(1, NC - 1) as c:
                body(c, ORDER, False, False)
            body(NC - 1, ORDER, False, True)
            body(NC, TAIL, False, True)

        def absent(c, order, first, stage, b):
            return (first and (stage, b) in LATE) or (order is TAIL and (stage, b) not in LATE)

        a_full, a_done = sem("a_full"), sem("a_done")
        d_full, d_done = sem("d_full"), sem("d_done")
        loaded, x_ready, xres_ready = sem("loaded"), sem("x_ready"), sem("xres_ready")
        x_used, xres_used = sem("x_used"), sem("xres_used")
        stored, xn_stored, xnT_stored = [sem("stored0"), sem("stored1")], sem("xn_stored"), sem("xnT_stored")
        setup, zeroed = sem("setup"), sem("zeroed")
        mv_ready, rstd_ready, xn_ready = sem("mv_ready"), sem("rstd_ready"), sem("xn_ready")
        act_step, dve_step, pool_step = sem("act_step"), sem("dve_step"), sem("pool_step")
        conv_ready, xc_ready, hist = sem("conv_ready"), sem("xc_ready"), sem("hist")
        dt_in, dtu_ready, dtw_ready, dtl_ready, adt_ready = (sem(k) for k in ("dt_in", "dtu_ready", "dtw_ready", "dtl_ready", "adt_ready"))
        Gm_ready, XpD_ready, XpP_ready, coef_ready = sem("Gm_ready"), sem("XpD_ready"), sem("XpP_ready"), sem("coef_ready")
        T_used, S_decayed, Y_ready, y2_ready, rss_ready = (sem(k) for k in ("T_used", "S_decayed", "Y_ready", "y2_ready", "rss_ready"))
        xb_ready, stats_ready = sem("xb_ready"), sem("stats_ready")
        carry, res_half = sem("carry"), sem("res_half")
        DVE_STEPS, POOL_STEPS, ACT_STEPS = MIX_STEPS
        seen = {}

        block = ctx.enter_context(nc.Block())
        x_t = io["x"].rearrange("b (c t) d -> c t b d", t=P)
        acc_t = scratch["acc0"].rearrange("(b c t) d -> c b t d", c=NC, t=P)
        xn_t = scratch["xn"].rearrange("(b c t) d -> c t b d", c=NC, t=P)

        @block.sync
        def _(sp):
            sp.dma_start(x_ln[:, :, :], x_t[0]).then_inc(x_ready, 16)
            rows = lambda v, n: v.rearrange("(a n) -> a n", a=1).to_broadcast([P, n])
            for dst, src in (
                (ident[:, :], io["ident"]), (w_in[:, :, :], io["W_in"].rearrange("(k p) n -> p k n", p=P)),
                (dt_add[:, :], rows(io["b_in"][D_PROJ - HEADS:D_PROJ], HEADS)), (dt_add2[:, :], rows(io["dt_bias"], HEADS)),
                (a_exp[:, :], rows(io["A_log"], HEADS)), (d_par[:, :], rows(io["D_param"], HEADS)),
                (b_out[:, :], rows(io["b_out"], D)), (b_xbc[:, :], io["b_xbc"]), (b_z[:, :], io["b_z"]),
                (cw[:, :, :], io["conv_w"]), (cb[:, :], io["conv_b"]), (normw[:, :], io["norm_w"]),
                (sums[:, :, :], io["sums"]), (pairs[:, :, :], io["pairs"]),
                (w_out[:, :, :], io["W_out"].rearrange("(g p) n -> p g n", p=P)),
                (s_gate[:, :, :].rearrange("p k (s h) -> p k s h", s=2), io["Sg"]),
                (s_up[:, :, :].rearrange("p k (s h) -> p k s h", s=2), io["Su"]),
                (s_down[:, :, :], io["Sd"].rearrange("s (q p) d -> p (s q) d", p=P)),
            ):
                sp.dma_start(dst, src).then_inc(loaded, 16)
            def save(c, own, b):
                sp.wait_ge(d_done, done(c, "out", b))
                sp.dma_start(acc_t[own, b], res[:, b % 2, :]).then_inc(stored[b % 2], 16)

            def body(c, order, first, last):
                if order is TAIL:
                    save(c, c - 1, 2)
                    save(c, c - 1, 3)
                    return
                sp.wait_ge(xn_ready, c * NB + NB)
                sp.dma_start(xn_t[c], xn[:, :, :]).then_inc(xn_stored, 16)
                sp.wait_ge(a_done, adone(c - 1, "xt", 1))
                sp.dma_start(scratch["xnT"][c], xnT[:, :, :, :].rearrange("p k b t -> p (k b t)")).then_inc(xnT_stored, 16)
                if not last:
                    sp.wait_ge(x_used, c + 1)
                    sp.dma_start(x_ln[:, :, :], x_t[c + 1]).then_inc(x_ready, 16)
                if not first:
                    save(c, c - 1, 2)
                    save(c, c - 1, 3)
                sp.wait_ge(xres_used, c + 1)
                sp.dma_start(x_res[:, :, :], x_t[c]).then_inc(xres_ready, 16)
                save(c, c, 0)
                save(c, c, 1)

            steps(sp, body)
            for s in stored:
                sp.wait_ge(s, 16 * NC * NB // 2 + 16)
            sp.wait_ge(xn_stored, 16 * NC)
            sp.wait_ge(xnT_stored, 16 * NC)

        @block.gpsimd
        def _(pool):
            n = [0]
            nc.gpsimd.memset(xin[:, :, :, 0:3], 0.0).then_inc(zeroed, 1)
            nc.gpsimd.memset(S[:, :, :], 0.0).then_inc(zeroed, 1)
            nc.gpsimd.memset(ones[:, :], 1.0).then_inc(zeroed, 1)
            nc.gpsimd.memset(eps[:, 0:1], 1e-5).then_inc(zeroed, 1)
            nc.gpsimd.memset(eps[:, 1:2], 1e-6).then_inc(zeroed, 1)
            pool.wait_ge(zeroed, 5)

            def body(c, order, first, last):
                def link(ins):
                    n[0] += 1
                    ins.then_inc(pool_step, 1)
                    pool.wait_ge(pool_step, c * POOL_STEPS + n[0])

                if order is TAIL:
                    return
                n[0] = 0
                for stage, b in order:
                    q, m = b % 2, c * NB + b
                    if stage == "gu" and b == 0:
                        pool.wait_ge(xres_ready, c * 16 + 16)
                        nc.gpsimd.tensor_tensor(x_res[:, :, :], x_res[:, :, :], b_out[:, :].unsqueeze(1).to_broadcast([P, NB, D]),
                                                ALU.add).then_inc(xb_ready, 1)
                    if stage == "T1":
                        pool.wait_ge(a_done, adone(c, "E", 7))
                        pool.wait_ge(d_done, done(c, "xtok", b))
                        nc.gpsimd.tensor_tensor(h8(Xp[:, q, PRE_D:8, :], 8 - PRE_D), h8b(Xd[:, q, :], 8 - PRE_D),
                                                E[:, PRE_D:8, b, :].unsqueeze(3).to_broadcast([P, 8 - PRE_D, HEADS, 8]),
                                                ALU.mult).then_inc(XpP_ready, 1)
                        pool.wait_ge(coef_ready, m + 1)
                        link(nc.gpsimd.tensor_tensor(h1(Yp[:, q, :]), h1(Xd[:, q, :]),
                                                     coef[:, q, :].unsqueeze(2).to_broadcast([P, HEADS, 8]), ALU.mult))
                    if stage == "T2":
                        for k in SEQ:
                            if k in POOL_ADDS:
                                j = POOL_ADDS.index(k)
                                pool.wait_ge(d_done, done(c, "L", b, k))
                                ins = nc.gpsimd.tensor_tensor(Yp[:, q, :], Yp[:, q, :], T[:, j % 2, :], ALU.add)
                                ins.then_inc(T_used, 1)
                                pool.wait_ge(T_used, m * 4 + j + 1 + 2)
                            if k == "off":
                                pool.wait_ge(d_full, c * PD + DJ.index(("L", b, "off")) + 1)
                                nc.gpsimd.tensor_tensor(h1(S[:, b, :]), h1(S[:, b, :]),
                                                        E[:, SUM_ALL, b, :].unsqueeze(2).to_broadcast([P, HEADS, 8]),
                                                        ALU.mult).then_inc(S_decayed, 1)
                seen["pool"] = n[0]

            steps(pool, body)

        @block.scalar
        def _(act):
            def A_wait(c, *job):
                act.wait_ge(a_full, c * PA + A.index(job) + 1 + PRE_A)

            def norm(c):
                act.wait_ge(mv_ready, c * NB + NB)
                nc.scalar.activation(lnv[:, :], mv[:, :, 1], ACT.Ln, bias=eps[:, 0:1]).then_inc(act_step, 1)
                act.wait_ge(act_step, c + 1)
                nc.scalar.activation(rstd[:, :], lnv[:, :], ACT.Exp, scale=-0.5).then_inc(rstd_ready, 1)

            def turned(c, first=False):
                for i in range(2):
                    A_wait(c - 1, "xt", i)
                    if i == 0 and not first:
                        act.wait_ge(xnT_stored, c * 16)
                    nc.scalar.activation(xnT[:, :, 2 * i:2 * i + 2, :].rearrange("p k b t -> p b k t"),
                                         a_bank("xt", i)[:, :].rearrange("p (b k t) -> p b k t", b=2, k=2),
                                         ACT.Copy).then_inc(a_done, 1)

            def square(c, own, b):
                act.wait_ge(d_done, done(c, "yT", b))
                nc.scalar.activation(y2[:, b % 2, :, :], yg[:, b % 2, :, :], ACT.Square).then_inc(y2_ready, 1)

            def rms(c, b):
                q = b % 2
                A_wait(c, "ss", b)
                nc.scalar.activation(lss[:, q:q + 1], a_bank("ss", b)[:, 0:1], ACT.Ln, scale=1.0 / INNER,
                                     bias=eps[:, 1:2]).then_inc(a_done, 1)
                act.wait_ge(a_done, adone(c, "ss", b))
                nc.scalar.activation(rss[:, q:q + 1], lss[:, q:q + 1], ACT.Exp, scale=-0.5).then_inc(rss_ready, 1)

            def body(c, order, first, last):
                for stage, b in order:
                    own = c - 1 if (stage, b) in LATE else c
                    if stage == "T4" and b == 2 and order is not TAIL:
                        act.wait_ge(dtw_ready, c + 1)
                        nc.scalar.activation(dtl[:, :, :], dtw[:, :, :], ACT.Ln).then_inc(dtl_ready, 1)
                    if stage == "z" and b == 0:
                        if first:
                            act.wait_ge(d_done, done(c, "yT", 3))
                        else:
                            square(c, c - 1, 3)
                    if absent(c, order, first, stage, b) or (stage == "xt" and last):
                        skip(act, a_done, A, NA + PRE_A, a_jobs(stage, b), c)
                        continue
                    if stage == "xbc":
                        A_wait(c, "xbc", b)
                        if b == 0:
                            act.wait_ge(hist, c + 1)
                        nc.scalar.activation(xin[:, b, :, 3:3 + P], a_bank("xbc", b)[:, :].rearrange("p (b t) -> p b t", b=NB),
                                             ACT.Identity, bias=b_xbc[:, b:b + 1]).then_inc(a_done, 1)
                        if b == 1:
                            act.wait_ge(dt_in, c + 1)
                            nc.scalar.activation(dtu[:, :, :], dtr[:, :, :], ACT.Exp).then_inc(dtu_ready, 1)
                    if stage == "z":
                        A_wait(c, "z", b)
                        nc.scalar.activation(zs[:, b, :, :].rearrange("p b t -> p (b t)"), a_bank("z", b)[:, :], ACT.Silu,
                                             bias=b_z[:, b:b + 1]).then_inc(a_done, 1)
                    if stage == "E":
                        A_wait(c, "E", b)
                        nc.scalar.activation(E[:, 2 * b:2 * b + 2, :, :].rearrange("p s b h -> p (s b h)"), a_bank("E", b)[:, :],
                                             ACT.Exp).then_inc(a_done, 1)
                        if b == 7:
                            for g in range(6):
                                act.wait_ge(conv_ready, c * 6 + g + 1)
                                nc.scalar.activation(xc[:, g, :, :], xc[:, g, :, :], ACT.Silu).then_inc(xc_ready, 1)
                    if stage == "gu":
                        A_wait(c, "g", b)
                        nc.scalar.activation(hs[:, b, :, :].rearrange("p b t -> p (b t)"), a_bank("g", b)[:, :],
                                             ACT.Silu).then_inc(a_done, 1)
                    if stage == "T1":
                        A_wait(c, "btok", b)
                        nc.scalar.activation(Btok[:, b % 2, :], a_bank("btok", b)[:, 0:P], ACT.Copy).then_inc(a_done, 1)
                    if stage == "T2" and b == 1 and not last:
                        norm(c + 1)
                    if stage == "T3" and b != 3:
                        square(c, own, b)
                    if stage == "T4":
                        rms(c, b)
                    if stage == "xt":
                        turned(c + 1)

            act.sem_inc(a_done, NA)
            act.wait_ge(zeroed, 5)
            norm(0)
            act.wait_ge(loaded, 16 * 18)
            nc.scalar.activation(a_exp[:, :], a_exp[:, :], ACT.Exp).then_inc(setup, 1)
            turned(0, True)
            skip(act, a_done, A, NA + PRE_A, A[A.index(("xt", 1)) + 1:], -1)
            steps(act, body)

        @block.tensor
        def _(pe):
            def A_open(c, *job):
                pe.wait_ge(a_done, c * PA + credit(A, NA, job) + PRE_A)

            def D_open(c, *job):
                pe.wait_ge(d_done, c * PD + credit(DJ, ND, job))

            def turn(c, first=False):
                pe.wait_ge(xn_ready, c * NB + NB)
                for i in range(2):
                    if not first:
                        A_open(c - 1, "xt", i)
                    for b in range(2):
                        for k in range(2):
                            o = (b * 2 + k) * P
                            ins = nc.tensor.transpose(a_bank("xt", i)[:, o:o + P], xn[:, 2 * i + b, k * P:(k + 1) * P], ident[:, :])
                    ins.then_inc(a_full, 1)

            def project(dst, w, col, full):
                for k in range(2):
                    ins = nc.tensor.matmul(dst[:, :], w[:, k, col:col + P], xnT[:, k, :, :].rearrange("p b t -> p (b t)"),
                                           start=(k == 0), stop=(k == 1))
                ins.then_inc(full, 1)

            def body(c, order, first, last):
                for stage, b in order:
                    own = c - 1 if (stage, b) in LATE else c
                    q, m = b % 2, own * NB + b
                    if absent(c, order, first, stage, b) or (stage == "xt" and last):
                        skip(pe, a_full, A, PRE_A, a_jobs(stage, b), c)
                        skip(pe, d_full, DJ, 0, d_jobs(stage, b), c)
                        continue
                    if stage == "dt":
                        pe.wait_ge(a_done, adone(c - 1, "xt", 1))
                        D_open(c, "dt", 0)
                        for i in range(NB):
                            for k in range(2):
                                ins = nc.tensor.matmul(d_bank("dt", 0)[:, i * HEADS:(i + 1) * HEADS], xnT[:, k, i, :],
                                                       w_in[:, k, D_PROJ - HEADS:D_PROJ], start=(k == 0), stop=(k == 1))
                        ins.then_inc(d_full, 1)
                    if stage == "xbc":
                        A_open(c, "xbc", b)
                        project(a_bank("xbc", b), w_in, INNER + b * P, a_full)
                    if stage == "z":
                        A_open(c, "z", b)
                        project(a_bank("z", b), w_in, b * P, a_full)
                    if stage == "gu":
                        A_open(c, "g", b)
                        project(a_bank("g", b), s_gate, b * P, a_full)
                        D_open(c, "u", b)
                        project(d_bank("u", b), s_up, b * P, d_full)
                    if stage == "E":
                        if b == 0:
                            pe.wait_ge(adt_ready, c + 1)
                        A_open(c, "E", b)
                        for s in range(2):
                            ins = nc.tensor.matmul(a_bank("E", b)[:, s * 256:(s + 1) * 256], sums[:, 2 * b + s, :],
                                                   adt[:, :, :].rearrange("p b h -> p (b h)"), start=True, stop=True)
                        ins.then_inc(a_full, 1)
                    if stage == "T1":
                        pe.wait_ge(xc_ready, c * 6 + 6)
                        D_open(c, "xtok", b)
                        for g in range(4):
                            ins = nc.tensor.transpose(d_bank("xtok", b)[:, g * P:(g + 1) * P], xc[:, g, b, :], ident[:, :])
                        ins.then_inc(d_full, 1)
                        A_open(c, "btok", b)
                        nc.tensor.transpose(a_bank("btok", b)[:, 0:P], xc[:, 4, b, :], ident[:, :]).then_inc(a_full, 1)
                        D_open(c, "G", b)
                        nc.tensor.matmul(d_bank("G", b)[:, 0:P], xc[:, 4, b, :], xc[:, 5, b, :], start=True, stop=True).then_inc(d_full, 1)
                    if stage == "T2":
                        pe.wait_ge(Gm_ready, m + 1)
                        pe.wait_ge(XpD_ready, m + 1)
                        pe.wait_ge(XpP_ready, m + 1)
                        for k in SEQ:
                            D_open(c, "L", b, k)
                            if k == "off":
                                nc.tensor.matmul(d_bank("L", b, k)[:, :], xc[:, 5, b, :], S[:, b, :], start=True, stop=True).then_inc(d_full, 1)
                            else:
                                nc.tensor.matmul(d_bank("L", b, k)[:, :], Gm[:, q, k, :], Xp[:, q, k, :], start=True, stop=True).then_inc(d_full, 1)
                        pe.wait_ge(a_done, adone(c, "btok", b))
                        D_open(c, "snew", b)
                        nc.tensor.matmul(d_bank("snew", b)[:, :], Btok[:, q, :], Xp[:, q, 7, :], start=True, stop=True).then_inc(d_full, 1)
                    if stage == "T3":
                        pe.wait_ge(Y_ready, m + 1)
                        D_open(c, "yT", b)
                        for g in range(4):
                            ins = nc.tensor.transpose(d_bank("yT", b)[:, g * P:(g + 1) * P], Yd[:, q, g * P:(g + 1) * P], ident[:, :])
                        ins.then_inc(d_full, 1)
                    if stage == "T4":
                        pe.wait_ge(y2_ready, m + 1)
                        A_open(c, "ss", b)
                        for g in range(4):
                            ins = nc.tensor.matmul(a_bank("ss", b)[:, 0:2], y2[:, q, g, :], ones[:, :], start=(g == 0), stop=(g == 3))
                        ins.then_inc(a_full, 1)
                        pe.wait_ge(d_done, done(own, "u", 3))
                        D_open(c, "out", b)
                        for g in range(4):
                            nc.tensor.matmul(d_bank("out", b)[:, 0:D], yg[:, q, g, :], w_out[:, g, :], start=(g == 0), stop=(g == 3))
                        for g in range(4):
                            ins = nc.tensor.matmul(d_bank("out", b)[:, D:2 * D], hs[:, g, b, :], s_down[:, g, :], start=(g == 0), stop=(g == 3))
                        ins.then_inc(d_full, 1)
                    if stage == "xt":
                        turn(c + 1)

            pe.wait_ge(loaded, 16 * 18)
            pe.wait_ge(zeroed, 5)
            pe.wait_ge(setup, 1)
            turn(0, True)
            skip(pe, a_full, A, PRE_A, A[A.index(("xt", 1)) + 1:], -1)
            steps(pe, body)

        @block.vector
        def _(dve):
            n = [0]
            v = nc.vector

            def D_wait(c, *job):
                dve.wait_ge(d_full, c * PD + DJ.index(job) + 1)

            def norm_stats(c):
                dve.wait_ge(x_ready, c * 16 + 16)
                for b in range(NB):
                    ins = v.bn_stats(stats[:, b, :], x_ln[:, b, :])
                ins.then_inc(stats_ready, 1)
                dve.wait_ge(stats_ready, c + 1)
                dve.sem_inc(carry, 1)
                for b in range(NB):
                    v.bn_aggr(mv[:, b, :], stats[:, b, :]).then_inc(mv_ready, 1)

            def norm(c, first=False):
                dve.wait_ge(rstd_ready, c + 1)
                if not first:
                    dve.wait_ge(xn_stored, c * 16)
                for b in range(NB):
                    v.tensor_scalar(xn[:, b, :], x_ln[:, b, :], mv[:, b, 0:1], rstd[:, b:b + 1], ALU.subtract,
                                    ALU.mult).then_inc(xn_ready, 1)
                dve.wait_ge(xn_ready, c * NB + NB)
                dve.sem_inc(x_used, 1)

            def conv(c, g, link):
                dve.wait_ge(a_done, adone(c, "xbc", g))
                link(v.tensor_scalar(xc[:, g, :, :], xin[:, g, :, 0:P], cw[:, g, 0:1], cb[:, g:g + 1], ALU.mult, ALU.add))
                for t in range(1, 4):
                    ins = v.scalar_tensor_tensor(out=xc[:, g, :, :], in0=xin[:, g, :, t:t + P], scalar=cw[:, g, t:t + 1],
                                                 in1=xc[:, g, :, :], op0=ALU.mult, op1=ALU.add)
                    if t < 3:
                        link(ins)
                    else:
                        ins.then_inc(conv_ready, 1)

            def body(c, order, first, last):
                n[0] = 0

                def link(ins):
                    n[0] += 1
                    ins.then_inc(dve_step, 1)
                    dve.wait_ge(dve_step, c * DVE_STEPS + n[0] + 6)

                def D_done(ins, *job):
                    ins.then_inc(d_done, 1)
                    dve.wait_ge(d_done, done(c, *job))

                for stage, b in order:
                    own = c - 1 if (stage, b) in LATE else c
                    q, m = b % 2, own * NB + b
                    if absent(c, order, first, stage, b):
                        skip(dve, d_done, DJ, ND, d_jobs(stage, b), c)
                    elif stage == "dt":
                        D_wait(c, "dt", 0)
                        ins = v.tensor_tensor(dtr[:, :, :], d_bank("dt", 0)[:, 0:NB * HEADS].rearrange("p (b h) -> p b h", b=NB),
                                              dt_add[:, :].unsqueeze(1).to_broadcast([P, NB, HEADS]), ALU.add)
                        D_done(ins, "dt", 0)
                        v.tensor_scalar(dtr[:, :, :], dtr[:, :, :], 30.0, None, ALU.min).then_inc(dt_in, 1)
                    elif stage == "xbc":
                        if b == 1:
                            dve.wait_ge(dtu_ready, c + 1)
                            v.tensor_scalar(dtw[:, :, :], dtu[:, :, :], 1.0, None, ALU.add).then_inc(dtw_ready, 1)
                        if b == 2:
                            dve.wait_ge(dtw_ready, c + 1)
                            link(v.tensor_scalar(dtd[:, :, :], dtw[:, :, :], -1.0, 1e-30, ALU.add, ALU.max))
                            link(v.reciprocal(dtd[:, :, :], dtd[:, :, :]))
                            link(v.tensor_tensor(dtd[:, :, :], dtd[:, :, :], dtu[:, :, :], ALU.mult))
                        if b == 3:
                            dve.wait_ge(dtl_ready, c + 1)
                            link(v.tensor_tensor(dtc[:, :, :], dtl[:, :, :], dtd[:, :, :], ALU.mult))
                            link(v.tensor_scalar(dtc[:, :, :], dtc[:, :, :], 0.001, 0.1, ALU.max, ALU.min))
                            v.scalar_tensor_tensor(out=adt[:, :, :], in0=dtc[:, :, :], scalar=-1.0,
                                                   in1=a_exp[:, :].unsqueeze(1).to_broadcast([P, NB, HEADS]), op0=ALU.mult,
                                                   op1=ALU.mult).then_inc(adt_ready, 1)
                        if b == 5:
                            link(v.reciprocal(d_over[:, :, :], dtc[:, :, :]))
                            link(v.tensor_tensor(d_over[:, :, :], d_over[:, :, :], d_par[:, :].unsqueeze(1).to_broadcast([P, NB, HEADS]), ALU.mult))
                        conv(c, b, link)
                        if b == 5:
                            dve.wait_ge(conv_ready, c * 6 + 6)
                            v.tensor_copy(xin[:, :, :, 0:3], xin[:, :, :, P:P + 3]).then_inc(hist, 1)
                    elif stage == "gu":
                        D_wait(c, "u", b)
                        dve.wait_ge(a_done, adone(c, "g", b))
                        v.tensor_tensor(hs[:, b, :, :].rearrange("p b t -> p (b t)"), hs[:, b, :, :].rearrange("p b t -> p (b t)"),
                                        d_bank("u", b)[:, :], ALU.mult).then_inc(d_done, 1)
                    elif stage == "T1":
                        D_wait(c, "xtok", b)
                        ins = v.tensor_tensor(h1(Xd[:, q, :]), h1(d_bank("xtok", b)[:, :]),
                                              dtc[:, b, :].unsqueeze(2).to_broadcast([P, HEADS, 8]), ALU.mult)
                        D_done(ins, "xtok", b)
                        dve.wait_ge(a_done, adone(c, "E", 7))
                        v.tensor_tensor(h8(Xp[:, q, 0:PRE_D, :], PRE_D), h8b(Xd[:, q, :], PRE_D),
                                        E[:, 0:PRE_D, b, :].unsqueeze(3).to_broadcast([P, PRE_D, HEADS, 8]),
                                        ALU.mult).then_inc(XpD_ready, 1)
                        D_wait(c, "G", b)
                        v.tensor_tensor(Gm[:, q, :, :], d_bank("G", b)[:, 0:P].unsqueeze(1).to_broadcast([P, LEVELS, P]),
                                        pairs[:, :, :], ALU.mult).then_inc(Gm_ready, 1)
                        D_done(v.tensor_tensor_reduce(gj[:, :], d_bank("G", b)[:, 0:P], ident[:, :], 1.0, 0.0, ALU.mult, ALU.add,
                                                      gd[:, q:q + 1]), "G", b)
                        v.tensor_scalar(coef[:, q, :], d_over[:, b, :], gd[:, q:q + 1], None, ALU.add).then_inc(coef_ready, 1)
                    elif stage == "T2":
                        for k in SEQ:
                            D_wait(c, "L", b, k)
                            src = d_bank("L", b, k)
                            if k == 0:
                                D_done(v.tensor_tensor(Yd[:, q, :], Yd[:, q, :], src[:, :], ALU.add), "L", b, k)
                                continue
                            e = SUM_START if k == "off" else SUM_POST + k - 1
                            post = E[:, e, b, :].unsqueeze(2).to_broadcast([P, HEADS, 8])
                            if k in POOL_ADDS:
                                j = POOL_ADDS.index(k)
                                dve.wait_ge(T_used, m * 4 + j + 1)
                                v.tensor_tensor(h1(T[:, j % 2, :]), h1(src[:, :]), post, ALU.mult).then_inc(d_done, 1)
                            elif k == 2:
                                D_done(v.tensor_tensor(h1(Yd[:, q, :]), h1(src[:, :]), post, ALU.mult), "L", b, k)
                            else:
                                D_done(v.tensor_tensor(h1(T[:, 2, :]), h1(src[:, :]), post, ALU.mult), "L", b, k)
                                link(v.tensor_tensor(Yd[:, q, :], Yd[:, q, :], T[:, 2, :], ALU.add))
                        D_wait(c, "snew", b)
                        dve.wait_ge(S_decayed, m + 1)
                        v.tensor_tensor(S[:, b, :], S[:, b, :], d_bank("snew", b)[:, :], ALU.add).then_inc(d_done, 1)
                        dve.wait_ge(T_used, m * 4 + 4 + 2)
                        v.tensor_tensor(Yd[:, q, :], Yd[:, q, :], Yp[:, q, :], ALU.add).then_inc(Y_ready, 1)
                        if b == 0 and not last:
                            norm_stats(c + 1)
                        if b == 1 and not last:
                            norm(c + 1)
                    elif stage == "T3":
                        D_wait(c, "yT", b)
                        dve.wait_ge(a_done, adone(own, "z", 3))
                        v.tensor_tensor(yg[:, q, :, :], d_bank("yT", b)[:, :].rearrange("p (g t) -> p g t", g=4),
                                        zs[:, :, b, :], ALU.mult).then_inc(d_done, 1)
                    elif stage == "T4":
                        D_wait(c, "out", b)
                        dve.wait_ge(rss_ready, m + 1)
                        dve.wait_ge(xb_ready, own + 1)
                        dve.wait_ge(stored[q], own * 32 + b // 2 * 16 + 16)
                        v.scalar_tensor_tensor(out=res[:, q, :], in0=d_bank("out", b)[:, 0:D], scalar=rss[:, q:q + 1],
                                               in1=x_res[:, b, :], op0=ALU.mult, op1=ALU.add).then_inc(res_half, 1)
                        dve.wait_ge(res_half, m + 1)
                        v.tensor_tensor(res[:, q, :], res[:, q, :], d_bank("out", b)[:, D:2 * D], ALU.add).then_inc(d_done, 1)
                    if stage == "T4" and b == 3:
                        dve.wait_ge(d_done, done(c, "out", 3))
                        dve.sem_inc(xres_used, 1)
                if order is ORDER:
                    seen["dve"] = n[0]

            dve.sem_inc(d_done, ND)
            dve.sem_inc(T_used, 2)
            dve.sem_inc(hist, 1)
            dve.sem_inc(stored[0], 16)
            dve.sem_inc(stored[1], 16)
            norm_stats(0)
            norm(0, True)
            dve.wait_ge(loaded, 16 * 18)
            dve.wait_ge(zeroed, 5)
            for g in range(4):
                v.tensor_scalar(w_out[:, g, :], w_out[:, g, :], normw[:, g:g + 1], None, ALU.mult).then_inc(dve_step, 1)
            v.tensor_tensor(dt_add[:, :], dt_add[:, :], dt_add2[:, :], ALU.add).then_inc(dve_step, 1)
            v.memset(lss[:, :], 0.0).then_inc(dve_step, 1)
            dve.wait_ge(dve_step, 6)
            dve.wait_ge(setup, 1)
            dve.sem_inc(setup, 1)
            steps(dve, body)
        assert (seen["dve"], seen["pool"]) == (DVE_STEPS, POOL_STEPS), seen
def router_phase(nc, io, scratch, keep):
    with ExitStack() as ctx:
        def sb(name, shape, dt=F32):
            return ctx.enter_context(nc.sbuf_tensor("r_" + name, shape, dt))

        def sem(name):
            return ctx.enter_context(nc.semaphore("r_" + name))

        wr = sb("wr", [P, 2, EXPERTS])
        rb = sb("rb", [P, EXPERTS])
        iota = sb("iota", [P, EXPERTS])
        before = sb("before", [P, P])
        ones = sb("ones", [P, P])
        zero = sb("zero", [P, 2048])
        xT = sb("xT", [P, NC, 2, P])
        xr = sb("xr", [P, NC, D])
        sc = sb("sc", [P, NC, EXPERTS])
        mx = sb("mx", [P, NC])
        t8 = sb("t8", [P, NC, 8])
        i8 = sb("i8", [P, NC, 8], U32)
        idx = sb("idx", [P, NC, K0])
        hot = sb("hot", [P, NC, K0, EXPERTS])
        prod = sb("prod", [P, NC, K0, EXPERTS])
        took = sb("took", [P, NC, EXPERTS])
        earlier = sb("earlier", [P, NC + 1, EXPERTS])
        place = sb("place", [P, NC, K0])
        full = sb("full", [P, NC, K0])
        slot = sb("slot", [P, NC, K0])
        slot_f = sb("slot_f", [P, NC, K0])
        to = sb("to", [P, NC, K0], U32)
        ps_l = ctx.enter_context(nc.psum_tensor("r_ps_l", [P, 512], F32))
        ps_p = ctx.enter_context(nc.psum_tensor("r_ps_p", [P, 512], F32))
        loaded, ready, cleared, zeroed = sem("loaded"), sem("ready"), sem("cleared"), sem("zeroed")
        logits, exped, counted, to_ready, scattered = sem("logits"), sem("exped"), sem("counted"), sem("to_ready"), sem("scattered")
        carry = sem("carry")
        shifted, took_ready, step, scat_all = sem("shifted"), sem("took_ready"), sem("step"), sem("scat_all")
        block = ctx.enter_context(nc.Block())
        xT_t = scratch["xnT"].rearrange("c p (k b t) -> b k p c t", k=2, b=NB)
        xr_t = scratch["xn"].rearrange("(b c t) d -> b t c d", c=NC, t=P)
        STEPS = ROUTER_STEPS
        seen = {}

        @block.sync
        def _(sp):
            sp.dma_start(wr[:, :, :], io["Wr"].rearrange("(k p) e -> p k e", p=P)).then_inc(loaded, 16)
            sp.dma_start(rb[:, :], io["r_bias"].rearrange("(a n) -> a n", a=1).to_broadcast([P, EXPERTS])).then_inc(loaded, 16)
            sp.dma_start(before[:, :], io["before"]).then_inc(loaded, 16)
            sp.wait_ge(zeroed, 1)
            for i in range(4):
                sp.dma_start(scratch["xb"].rearrange("(i p r) d -> i p (r d)", i=4, p=P)[i], zero[:, :]).then_inc(cleared, 16)
            with sp.Fori(0, NB) as b:
                sp.wait_ge(scattered, b + 1)
                for k in range(2):
                    sp.dma_start(xT[:, :, k, :], xT_t[b, k]).then_inc(ready, 16)
                sp.dma_start(xr[:, :, :], xr_t[b]).then_inc(ready, 16)

        @block.gpsimd
        def _(pool):
            nc.gpsimd.memset(zero[:, :], 0.0).then_inc(zeroed, 1)
            nc.gpsimd.iota(iota[:, :], [[1, EXPERTS]], base=0, channel_multiplier=0,
                           allow_small_or_imprecise_dtypes=True).then_inc(zeroed, 1)
            nc.gpsimd.memset(ones[:, :], 1.0).then_inc(zeroed, 1)
            nc.gpsimd.memset(earlier[:, :, :], 0.0).then_inc(zeroed, 1)
            pool.sem_inc(scattered, 1)
            pool.wait_ge(cleared, 64)
            with pool.Fori(0, NB) as b:
                pool.wait_ge(to_ready, b + 1)
                pool.sem_inc(carry, 1)
                for c in range(NC):
                    for k in range(K0):
                        nc.gpsimd.indirect_dma_start(
                            out=scratch["xb"], out_offset=bass.IndirectOffsetOnAxis(ap=to[:, c, k:k + 1], axis=0),
                            in_=xr[:, c, :], in_offset=None, bounds_check=EXPERTS * CAP - 1, oob_is_err=False,
                        ).then_inc(scat_all, 16)
                pool.wait_ge(scat_all, b * 16 * NC * K0 + 16 * NC * K0)
                pool.sem_inc(scattered, 1)

        @block.scalar
        def _(act):
            with act.Fori(0, NB) as b:
                act.wait_ge(shifted, b + 1)
                nc.scalar.activation(sc[:, :, :], sc[:, :, :], ACT.Exp).then_inc(exped, 1)

        @block.tensor
        def _(pe):
            pe.wait_ge(loaded, 48)
            pe.wait_ge(zeroed, 4)
            with pe.Fori(0, NB) as b:
                pe.wait_ge(ready, b * 48 + 48)
                for c in range(NC):
                    for k in range(2):
                        ins = nc.tensor.matmul(ps_l[:, c * EXPERTS:(c + 1) * EXPERTS], xT[:, c, k, :], wr[:, k, :],
                                               start=(k == 0), stop=(k == 1))
                ins.then_inc(logits, 1)
                pe.wait_ge(took_ready, b + 1)
                nc.tensor.matmul(ps_p[:, :], before[:, :], took[:, :, :].rearrange("p c e -> p (c e)"), start=True, stop=False)
                nc.tensor.matmul(ps_p[:, :], ones[:, :], earlier[:, 0:NC, :].rearrange("p c e -> p (c e)"),
                                 start=False, stop=True).then_inc(counted, 1)

        @block.vector
        def _(dve):
            n = [0]
            v = nc.vector

            def link(ins):
                n[0] += 1
                ins.then_inc(step, 1)
                dve.wait_ge(step, b * STEPS + n[0])

            def wide(ap):
                return ap.unsqueeze(2).to_broadcast([P, NC, EXPERTS])

            dve.wait_ge(loaded, 48)
            dve.wait_ge(zeroed, 4)
            with dve.Fori(0, NB) as b:
                dve.wait_ge(logits, b + 1)
                link(v.tensor_tensor(sc[:, :, :], ps_l[:, :].rearrange("p (c e) -> p c e", c=NC),
                                     rb[:, :].unsqueeze(1).to_broadcast([P, NC, EXPERTS]), ALU.add))
                link(v.tensor_reduce(mx[:, :], sc[:, :, :], AX.X, ALU.max))
                v.tensor_tensor(sc[:, :, :], sc[:, :, :], wide(mx[:, :]), ALU.subtract).then_inc(shifted, 1)
                dve.wait_ge(exped, b + 1)
                link(v.tensor_reduce(mx[:, :], sc[:, :, :], AX.X, ALU.add))
                link(v.reciprocal(mx[:, :], mx[:, :]))
                link(v.tensor_tensor(sc[:, :, :], sc[:, :, :], wide(mx[:, :]), ALU.mult))
                dve.sem_inc(carry, 1)
                for c in range(NC):
                    ins = v.max(t8[:, c, :], sc[:, c, :])
                link(ins)
                dve.sem_inc(carry, 1)
                for c in range(NC):
                    ins = v.max_index(i8[:, c, :], t8[:, c, :], sc[:, c, :])
                link(ins)
                link(v.tensor_copy(idx[:, :, :], i8[:, :, 0:K0]))
                link(v.tensor_reduce(mx[:, :], t8[:, :, 0:K0], AX.X, ALU.add))
                link(v.reciprocal(mx[:, :], mx[:, :]))
                link(v.tensor_tensor(t8[:, :, 0:K0], t8[:, :, 0:K0], mx[:, :].unsqueeze(2).to_broadcast([P, NC, K0]), ALU.mult))
                link(v.tensor_tensor(hot[:, :, :, :], iota[:, :].unsqueeze(1).unsqueeze(1).to_broadcast([P, NC, K0, EXPERTS]),
                                     idx[:, :, :].unsqueeze(3).to_broadcast([P, NC, K0, EXPERTS]), ALU.is_equal))
                link(v.tensor_reduce(took[:, :, :], hot[:, :, :, :].rearrange("p c k e -> p c e k"), AX.X, ALU.add))
                for c in range(NC):
                    ins = v.tensor_tensor(earlier[:, c + 1, :], earlier[:, c, :], took[:, c, :], ALU.add)
                    if c < NC - 1:
                        link(ins)
                ins.then_inc(took_ready, 1)
                dve.wait_ge(counted, b + 1)
                link(v.tensor_tensor(prod[:, :, :, :], hot[:, :, :, :],
                                     ps_p[:, :].rearrange("p (c e) -> p c e", c=NC).unsqueeze(2).to_broadcast([P, NC, K0, EXPERTS]),
                                     ALU.mult))
                link(v.tensor_copy(earlier[:, 0, :], earlier[:, NC, :]))
                link(v.tensor_reduce(place[:, :, :], prod[:, :, :, :], AX.X, ALU.add))
                link(v.tensor_scalar(full[:, :, :], place[:, :, :], float(CAP), None, ALU.is_lt))
                tile = keep["w_all"][:, bass.ds(b * NC, NC), :]
                link(v.tensor_tensor(tile, t8[:, :, 0:K0], full[:, :, :], ALU.mult))
                link(v.tensor_scalar(full[:, :, :], place[:, :, :], float(CAP), 1e6, ALU.is_ge, ALU.mult))
                link(v.scalar_tensor_tensor(out=slot[:, :, :], in0=idx[:, :, :], scalar=float(CAP), in1=place[:, :, :],
                                            op0=ALU.mult, op1=ALU.add))
                link(v.tensor_tensor(slot[:, :, :], slot[:, :, :], full[:, :, :], ALU.add))
                v.tensor_copy(to[:, :, :], slot[:, :, :]).then_inc(to_ready, 1)
                link(v.tensor_scalar(place[:, :, :], place[:, :, :], float(CAP - 1), None, ALU.min))
                link(v.scalar_tensor_tensor(out=slot_f[:, :, :], in0=idx[:, :, :], scalar=float(CAP), in1=place[:, :, :],
                                            op0=ALU.mult, op1=ALU.add))
                link(v.tensor_copy(keep["slot_all"][:, bass.ds(b * NC, NC), :], slot_f[:, :, :]))
                seen["dve"] = n[0]
        assert seen["dve"] == STEPS, seen


def expert_phase(nc, io, scratch):
    with ExitStack() as ctx:
        def sb(name, shape, dt=F32):
            return ctx.enter_context(nc.sbuf_tensor("e_" + name, shape, dt))

        def sem(name):
            return ctx.enter_context(nc.semaphore("e_" + name))

        PAIRS = EXPERTS // 2
        ident = sb("ident", [P, P])
        wgu = [sb(f"wgu{q}", [P, 2, 2, 2, HID0]) for q in range(2)]
        wd = [sb(f"wd{q}", [P, D]) for q in range(2)]
        xb = [sb(f"xb{q}", [P, D]) for q in range(2)]
        xbT = [sb(f"xbT{q}", [P, 2, P]) for q in range(2)]
        gate = [sb(f"gate{q}", [P, CAP]) for q in range(2)]
        y = [sb(f"y{q}", [P, D]) for q in range(2)]
        ps_x = [ctx.enter_context(nc.psum_tensor(f"e_ps_x{q}", [P, 512], F32)) for q in range(2)]
        ps_h = [ctx.enter_context(nc.psum_tensor(f"e_ps_h{q}", [P, 512], F32)) for q in range(2)]
        ps_y = [ctx.enter_context(nc.psum_tensor(f"e_ps_y{q}", [P, 512], F32)) for q in range(2)]
        loaded, carry = sem("loaded"), sem("carry")
        ready = [sem(f"ready{q}") for q in range(2)]
        stored = [sem(f"stored{q}") for q in range(2)]
        turned, xT_ready, gu_ready, silu_ready, h_ready, y_full, y_ready, used = (
            sem(k) for k in ("turned", "xT_ready", "gu_ready", "silu_ready", "h_ready", "y_full", "y_ready", "used"))
        block = ctx.enter_context(nc.Block())

        @block.sync
        def _(sp):
            sp.dma_start(ident[:, :], io["ident"]).then_inc(loaded, 16)
            with sp.Fori(0, PAIRS // 2) as i:
                for q in range(2):
                    j = i * 2 + q
                    sp.wait_ge(used, j + 1)
                    sp.dma_start(wgu[q][:, :, :, :, :].rearrange("p a e k h -> p (a e k h)"), io["wgu0"][j]).then_inc(ready[q], 16)
                    sp.dma_start(wd[q][:, :], io["wd0"].rearrange("(j p) d -> j p d", p=P)[j]).then_inc(ready[q], 16)
                    sp.dma_start(xb[q][:, :], scratch["xb"].rearrange("(j p) d -> j p d", p=P)[j]).then_inc(ready[q], 16)

        @block.scalar
        def _(act):
            for q in range(2):
                act.sem_inc(stored[q], 16)
            with act.Fori(0, PAIRS // 2) as i:
                for q in range(2):
                    j = i * 2 + q
                    act.wait_ge(gu_ready, j + 1)
                    nc.scalar.activation(gate[q][:, :], ps_h[q][:, 0:CAP], ACT.Silu).then_inc(silu_ready, 1)
                    act.wait_ge(stored[q], i * 16 + 16)
                    act.wait_ge(y_full, j + 1)
                    nc.scalar.activation(y[q][:, :], ps_y[q][:, 0:D], ACT.Copy).then_inc(y_ready, 1)
                    act.wait_ge(y_ready, j + 1)
                    act.dma_start(scratch["yb"].rearrange("(j p) d -> j p d", p=P)[j], y[q][:, :]).then_inc(stored[q], 16)
            for q in range(2):
                act.wait_ge(stored[q], 16 * PAIRS // 2 + 16)

        @block.tensor
        def _(pe):
            pe.sem_inc(used, 2)
            pe.wait_ge(loaded, 16)
            with pe.Fori(0, PAIRS // 2) as i:
                for q in range(2):
                    pe.wait_ge(ready[q], i * 48 + 48)
                    for k in range(2):
                        ins = nc.tensor.transpose(ps_x[q][:, k * P:(k + 1) * P], xb[q][:, k * P:(k + 1) * P], ident[:, :])
                    ins.then_inc(turned, 1)
                for q in range(2):
                    pe.wait_ge(xT_ready, i * 2 + q + 1)
                    for a in range(2):
                        for e in range(2):
                            for k in range(2):
                                ins = nc.tensor.matmul(ps_h[q][e * HID0:(e + 1) * HID0, a * CAP:(a + 1) * CAP], wgu[q][:, a, e, k, :],
                                                       xbT[q][:, k, e * CAP:(e + 1) * CAP], start=(k == 0), stop=(k == 1))
                    ins.then_inc(gu_ready, 1)
                for q in range(2):
                    pe.wait_ge(h_ready, i * 2 + q + 1)
                    pe.sem_inc(carry, 1)
                    for e in range(2):
                        rows = slice(e * HID0, (e + 1) * HID0)
                        ins = nc.tensor.matmul(ps_y[q][rows, 0:D], gate[q][rows, :], wd[q][rows, :], start=True, stop=True)
                    ins.then_inc(y_full, 1)
                    pe.wait_ge(y_full, i * 2 + q + 1)
                    pe.sem_inc(used, 1)

        @block.vector
        def _(dve):
            v = nc.vector
            with dve.Fori(0, PAIRS // 2) as i:
                for q in range(2):
                    dve.wait_ge(turned, i * 2 + q + 1)
                    v.tensor_copy(xbT[q][:, :, :].rearrange("p k t -> p (k t)"), ps_x[q][:, 0:2 * P]).then_inc(xT_ready, 1)
                for q in range(2):
                    dve.wait_ge(silu_ready, i * 2 + q + 1)
                    v.tensor_tensor(gate[q][:, :], gate[q][:, :], ps_h[q][:, CAP:2 * CAP], ALU.mult).then_inc(h_ready, 1)
def attention_constants():
    import numpy as np
    half = DH // 2
    freq = 1.0 / 10000.0 ** (np.arange(0, DH, 2, dtype=np.float32) / np.float32(DH))
    ang = (np.arange(SEQ_LEN, dtype=np.float32)[:, None] * freq[None, :].astype(np.float32)).astype(np.float32).astype(np.float64)
    cos, sin = np.cos(ang).T, np.sin(ang).T
    lam = 2.0 ** (-8.0 * np.arange(1, HQ + 1) / HQ)
    i = np.arange(P)
    v_dec = np.exp(lam[None, :] * (i[:, None] + 1 - P // 2))
    q_dec = np.exp(-lam[:, None] * (i[None, :] + 1 - P // 2))
    half_chunk = np.exp(-lam * (P // 2))
    return {
        "cos": np.concatenate([cos, cos]), "sin": np.concatenate([sin, -sin]),
        "mask": (i[:, None] <= i[None, :]), "v_dec": v_dec,
        "q_dec": np.broadcast_to(q_dec.reshape(1, -1), (P, HQ * P)), "half_chunk": np.broadcast_to(half_chunk[None], (P, HQ)),
    }


def attention_phase(nc, io, scratch, keep):
    with ExitStack() as ctx:
        def sb(name, shape, dt=F32):
            return ctx.enter_context(nc.sbuf_tensor("a_" + name, shape, dt))

        def sem(name):
            return ctx.enter_context(nc.semaphore("a_" + name))

        GR = HQ // HKV
        wq = sb("wq", [P, 2, HQ * DH])
        wk = sb("wk", [P, 2, HKV * DH])
        wv = sb("wv", [P, 2, HKV * DH])
        wo = sb("wo", [P, HQ, D])
        cos = sb("cos", [P, SEQ_LEN])
        sin = sb("sin", [P, SEQ_LEN])
        mask = sb("mask", [P, P])
        v_dec = sb("v_dec", [P, HQ])
        q_dec = sb("q_dec", [P, HQ, P])
        half_chunk = sb("half_chunk", [P, HQ])
        ident = sb("ident", [P, P])
        eps = sb("eps", [P, 1])
        x1 = sb("x1", [P, NB, D])
        x1r = sb("x1r", [P, NB, D])
        slot_now = sb("slot_now", [P, NB, K0], U32)
        w_now = sb("w_now", [P, NB, K0])
        gath = [sb(f"gath{q}", [P, K0, D]) for q in range(2)]
        stats = sb("stats", [P, NB, 6])
        mv = sb("mv", [P, NB, 2])
        lnv = sb("lnv", [P, NB])
        rstd = sb("rstd", [P, NB])
        xn = sb("xn", [P, NB, D])
        xnT = sb("xnT", [P, 2, NB, P])
        qT = sb("qT", [P, HQ, NB, P])
        kT = sb("kT", [P, HKV, NB, P])
        rot = sb("rot", [P, 3, NB, P])
        v = sb("v", [P, 2, HKV, DH])
        vd = sb("vd", [P, 2, HQ, DH])
        ktok = sb("ktok", [P, 2, HKV, DH])
        Sm = sb("Sm", [P, 2, GR, P])
        oT = sb("oT", [P, HQ, P])
        kv = sb("kv", [P, NB, HQ, DH])
        res = sb("res", [P, 2, D])
        NA, ND = 2, 6
        psA = [ctx.enter_context(nc.psum_tensor(f"a_psA{i}", [P, 512], F32)) for i in range(NA)]
        psD = [ctx.enter_context(nc.psum_tensor(f"a_psD{i}", [P, 512], F32)) for i in range(ND)]

        def tile_order():
            for b in range(NB):
                yield ("S", b, 0)
                yield ("S", b, 1)
                if b:
                    yield ("wo", b - 1, 0)
                for g in range(HKV):
                    yield ("o", b, g)
                    yield ("kv", b, g)
                    if g + 2 < HKV:
                        yield ("S", b, g + 2)
                yield ("end", b, 0)
            yield ("wo", NB - 1, 0)

        PREP_AT = 2
        A = [("v", b) for b in range(2)] + [("ktok", 0)]
        A += [x for b in range(1, NB) for x in ([("v", b + 1)] if b + 1 < NB else []) + [("ktok", b)]] + [("xt", 0), ("xt", 1)]
        DJ = [("rope", i) for i in range(HKV + HQ)] + [t for t in tile_order() if t[0] != "end"]
        PA, PD = len(A), len(DJ)
        PRE_A = 2

        def a_bank(*job):
            return psA[A.index(job) % NA]

        def d_bank(*job):
            return psD[DJ.index(job) % ND]

        def done(c, *job):
            return c * PD + DJ.index(job) + 1 + ND

        def adone(c, *job):
            return c * PA + A.index(job) + 1 + NA + PRE_A

        def credit(jobs, n, job):
            j = jobs.index(job)
            before = j - n if j >= n else max(i for i in range(len(jobs)) if i % n == j) - len(jobs)
            return before + 1 + n

        a_full, a_done, d_full, d_done = sem("a_full"), sem("a_done"), sem("d_full"), sem("d_done")
        loaded, setup, x_ready, x1r_ready, x_stored, xnT_stored = (
            sem(k) for k in ("loaded", "setup", "x_ready", "x1r_ready", "x_stored", "xnT_stored"))
        now_ready, stats_ready, mv_ready, lnv_ready, rstd_ready, xn_ready = (
            sem(k) for k in ("now_ready", "stats_ready", "mv_ready", "lnv_ready", "rstd_ready", "xn_ready"))
        gathered = [sem("gathered0"), sem("gathered1")]
        stored = [sem("stored0"), sem("stored1")]
        gath_used, added, roped, vd_ready, decayed, carry, half_decayed = (
            sem(k) for k in ("gath_used", "added", "roped", "vd_ready", "decayed", "carry", "half_decayed"))
        cos_done = sem("cos_done")
        block = ctx.enter_context(nc.Block())
        acc_t = scratch["acc0"].rearrange("(b c t) d -> c t b d", c=NC, t=P)
        x1_t = scratch["x1"].rearrange("(b c t) d -> c t b d", c=NC, t=P)
        acc1_t = scratch["acc1"].rearrange("(b c t) d -> c b t d", c=NC, t=P)
        slot_t = keep["slot_all"][:, :, :].rearrange("p (b c) k -> p c b k", b=NB)
        w_t = keep["w_all"][:, :, :].rearrange("p (b c) k -> p c b k", b=NB)
        N_LOAD = 11

        def steps(eng, body):
            with eng.Fori(0, NC - 1) as c:
                body(c, False)
            body(NC - 1, True)

        @block.sync
        def _(sp):
            for dst, src in (
                (ident[:, :], io["ident"]), (wk[:, :, :], io["wk"]), (wv[:, :, :], io["wv"]), (cos[:, :], io["cos"]),
                (sin[:, :], io["sin"]), (wq[:, :, :], io["wq"]), (mask[:, :], io["mask"]), (v_dec[:, :], io["v_dec"]),
                (q_dec[:, :, :], io["q_dec"].rearrange("p (h i) -> p h i", h=HQ)), (half_chunk[:, :], io["half_chunk"]),
                (wo[:, :, :], io["wo"]),
            ):
                sp.dma_start(dst, src).then_inc(loaded, 16)

            def load(c):
                sp.dma_start(x1[:, :, :], acc_t[c]).then_inc(x_ready, 16)

            def save_prep(c):
                sp.wait_ge(xn_ready, c * NB + NB)
                sp.dma_start(x1_t[c], x1[:, :, :]).then_inc(x_stored, 16)
                sp.wait_ge(a_done, adone(c - 1, "xt", 1))
                sp.dma_start(scratch["xnT1"][c], xnT[:, :, :, :].rearrange("p k b t -> p (k b t)")).then_inc(xnT_stored, 16)

            def body(c, last):
                sp.wait_ge(x_stored, c * 16 + 16)
                if not last:
                    load(c + 1)
                sp.wait_ge(d_done, c * PD + ND)
                sp.dma_start(x1r[:, :, :], x1_t[c]).then_inc(x1r_ready, 16)
                for b in range(NB):
                    if b == NB - 1 and not last:
                        save_prep(c + 1)
                    sp.wait_ge(d_done, done(c, "wo", b, 0))
                    sp.dma_start(acc1_t[c, b], res[:, b % 2, :]).then_inc(stored[b % 2], 16)

            load(0)
            save_prep(0)
            steps(sp, body)
            for s in stored:
                sp.wait_ge(s, 16 * NC * NB // 2 + 16)
            sp.wait_ge(x_stored, 16 * NC)
            sp.wait_ge(xnT_stored, 16 * NC)

        @block.gpsimd
        def _(pool):
            nc.gpsimd.memset(kv[:, :, :, :], 0.0).then_inc(setup, 1)
            nc.gpsimd.memset(eps[:, :], 1e-5).then_inc(setup, 1)
            pool.wait_ge(setup, 2)
            pool.wait_ge(loaded, 16 * N_LOAD)

            def gather(c, b):
                if b == 0:
                    pool.wait_ge(now_ready, c + 1)
                pool.wait_ge(gath_used, c * NB + b + 1)
                pool.sem_inc(carry, 1)
                for k in range(K0):
                    nc.gpsimd.indirect_dma_start(
                        out=gath[b % 2][:, k, :], out_offset=None, in_=scratch["yb"],
                        in_offset=bass.IndirectOffsetOnAxis(ap=slot_now[:, b, k:k + 1], axis=0),
                        bounds_check=EXPERTS * CAP - 1, oob_is_err=False,
                    ).then_inc(gathered[b % 2], 16)

            def values(c, b):
                pool.wait_ge(a_done, adone(c, "v", b))
                nc.gpsimd.tensor_tensor(
                    vd[:, b % 2, :, :].rearrange("p (g r) e -> p g r e", g=HKV),
                    v[:, b % 2, :, :].unsqueeze(2).to_broadcast([P, HKV, GR, DH]),
                    v_dec[:, :].rearrange("p (g r) -> p g r", g=HKV).unsqueeze(3).to_broadcast([P, HKV, GR, DH]),
                    ALU.mult).then_inc(vd_ready, 1)

            def body(c, last):
                for i in range(HKV + HQ):
                    pool.wait_ge(d_done, done(c, "rope", i))
                    dst = kT[:, i, :, :] if i < HKV else qT[:, i - HKV, :, :]
                    nc.gpsimd.tensor_tensor(dst, dst, rot[:, i % 3, :, :], ALU.add).then_inc(roped, 1)
                    if i == HKV - 1:
                        values(c, 0)
                        values(c, 1)
                if not last:
                    gather(c + 1, 0)
                    gather(c + 1, 1)
                for b in range(NB):
                    pool.wait_ge(d_done, done(c, "kv", b, HKV - 1))
                    dec = half_chunk[:, :].unsqueeze(2).to_broadcast([P, HQ, DH])
                    nc.gpsimd.tensor_tensor(kv[:, b, :, :], kv[:, b, :, :], dec, ALU.mult).then_inc(half_decayed, 1)
                    pool.wait_ge(half_decayed, c * NB + b + 1)
                    nc.gpsimd.tensor_tensor(kv[:, b, :, :], kv[:, b, :, :], dec, ALU.mult).then_inc(decayed, 1)
                    if b + 2 < NB:
                        values(c, b + 2)
                    if b == PREP_AT - 1 and not last:
                        gather(c + 1, 2)
                        gather(c + 1, 3)

            for b in range(NB):
                gather(0, b)
            steps(pool, body)

        @block.scalar
        def _(act):
            def A_wait(c, *job):
                act.wait_ge(a_full, c * PA + A.index(job) + 1 + PRE_A)

            def prep(c):
                act.wait_ge(mv_ready, c * NB + NB)
                nc.scalar.activation(lnv[:, :], mv[:, :, 1], ACT.Ln, bias=eps[:, :]).then_inc(lnv_ready, 1)
                act.wait_ge(lnv_ready, c + 1)
                nc.scalar.activation(rstd[:, :], lnv[:, :], ACT.Exp, scale=-0.5).then_inc(rstd_ready, 1)

            def turned(c):
                for i in range(2):
                    A_wait(c - 1, "xt", i)
                    if i == 0:
                        act.wait_ge(xnT_stored, c * 16 + 0) if not isinstance(c, int) or c else None
                    nc.scalar.activation(xnT[:, :, 2 * i:2 * i + 2, :].rearrange("p k b t -> p b k t"),
                                         a_bank("xt", i)[:, :].rearrange("p (b k t) -> p b k t", b=2, k=2),
                                         ACT.Copy).then_inc(a_done, 1)

            def values(c, b):
                A_wait(c, "v", b)
                act.wait_ge(vd_ready, c * NB + b - 2 + 1 + 2)
                nc.scalar.activation(v[:, b % 2, :, :].rearrange("p g e -> p (g e)"), a_bank("v", b)[:, :], ACT.Copy).then_inc(a_done, 1)

            def keys(c, b):
                A_wait(c, "ktok", b)
                nc.scalar.activation(ktok[:, b % 2, :, :].rearrange("p g e -> p (g e)"), a_bank("ktok", b)[:, :], ACT.Copy).then_inc(a_done, 1)

            def body(c, last):
                for kind, b in A:
                    if kind == "v":
                        values(c, b)
                    if kind == "ktok":
                        keys(c, b)
                        if b == PREP_AT and not last:
                            prep(c + 1)
                if not last:
                    turned(c + 1)

            act.sem_inc(a_done, NA)
            act.wait_ge(setup, 2)
            prep(0)
            turned(0)
            steps(act, body)

        @block.tensor
        def _(pe):
            def A_open(c, *job):
                pe.wait_ge(a_done, c * PA + credit(A, NA, job) + PRE_A)

            def D_open(c, *job):
                pe.wait_ge(d_done, c * PD + credit(DJ, ND, job))

            def turn(c):
                pe.wait_ge(xn_ready, c * NB + NB)
                for i in range(2):
                    A_open(c - 1, "xt", i)
                    for b in range(2):
                        for k in range(2):
                            o = (b * 2 + k) * P
                            ins = nc.tensor.transpose(a_bank("xt", i)[:, o:o + P], xn[:, 2 * i + b, k * P:(k + 1) * P], ident[:, :])
                    ins.then_inc(a_full, 1)

            def values(c, b):
                A_open(c, "v", b)
                for k in range(2):
                    ins = nc.tensor.matmul(a_bank("v", b)[:, :], xnT[:, k, b, :], wv[:, k, :], start=(k == 0), stop=(k == 1))
                ins.then_inc(a_full, 1)

            def keys(c, b):
                A_open(c, "ktok", b)
                for g in range(HKV):
                    ins = nc.tensor.transpose(a_bank("ktok", b)[:, g * P:(g + 1) * P], kT[:, g, b, :], ident[:, :])
                ins.then_inc(a_full, 1)

            def body(c, last):
                pe.wait_ge(a_done, adone(c - 1, "xt", 1))
                values(c, 0)
                values(c, 1)
                for i in range(HKV + HQ):
                    D_open(c, "rope", i)
                    w, n = (wk, i) if i < HKV else (wq, i - HKV)
                    for k in range(2):
                        ins = nc.tensor.matmul(d_bank("rope", i)[:, :], w[:, k, n * P:(n + 1) * P],
                                               xnT[:, k, :, :].rearrange("p b t -> p (b t)"), start=(k == 0), stop=(k == 1))
                    ins.then_inc(d_full, 1)
                pe.wait_ge(roped, c * (HKV + HQ) + HKV)
                keys(c, 0)
                pe.wait_ge(roped, (c + 1) * (HKV + HQ))
                for job in tile_order():
                    stage, b, g = job
                    q = b % 2
                    if stage == "end":
                        continue
                    if stage == "S" and g == 0 and b:
                        if b + 1 < NB:
                            values(c, b + 1)
                        keys(c, b)
                    D_open(c, *job)
                    out = d_bank(*job)
                    if stage == "S":
                        nc.tensor.matmul(out[:, :], kT[:, g, b, :], qT[:, GR * g:GR * g + GR, b, :], start=True, stop=True).then_inc(d_full, 1)
                    if stage == "o":
                        if g == 0:
                            pe.wait_ge(vd_ready, c * NB + b + 1 + 2)
                            pe.wait_ge(decayed, c * NB + b + 1)
                        pe.wait_ge(d_done, done(c, "S", b, g))
                        for r in range(GR):
                            h = GR * g + r
                            nc.tensor.matmul(out[:, r * P:(r + 1) * P], vd[:, q, h, :], Sm[:, g % 2, r, :], start=True, stop=False)
                            ins = nc.tensor.matmul(out[:, r * P:(r + 1) * P], kv[:, b, h, :], qT[:, h, b, :], start=False, stop=True)
                        ins.then_inc(d_full, 1)
                    if stage == "kv":
                        pe.wait_ge(a_done, adone(c, "ktok", b))
                        nc.tensor.matmul(out[:, :], ktok[:, q, g, :], vd[:, q, GR * g:GR * g + GR, :], start=True, stop=True).then_inc(d_full, 1)
                    if stage == "wo":
                        if b == NB - 1 and not last:
                            turn(c + 1)
                        pe.wait_ge(d_done, done(c, "o", b, HKV - 1))
                        for h in range(HQ):
                            ins = nc.tensor.matmul(out[:, 0:D], oT[:, h, :], wo[:, h, :], start=(h == 0), stop=(h == HQ - 1))
                        ins.then_inc(d_full, 1)

            pe.sem_inc(vd_ready, 2)
            pe.sem_inc(decayed, NB)
            pe.wait_ge(loaded, 16 * N_LOAD)
            pe.wait_ge(setup, 2)
            turn(0)
            steps(pe, body)

        @block.vector
        def _(dve):
            n = [0]
            vec = nc.vector

            def now(c):
                vec.tensor_copy(slot_now[:, :, :], slot_t[:, c, :, :]).then_inc(now_ready, 1)
                vec.tensor_copy(w_now[:, :, :], w_t[:, c, :, :]).then_inc(added, 1)

            ADDS = 1 + NB * K0

            def combine(c, b):
                q = b % 2
                if b == 0:
                    dve.wait_ge(x_ready, c * 16 + 16)
                dve.wait_ge(gathered[q], (c * 2 + b // 2) * 16 * K0 + 16 * K0)
                for k in range(K0):
                    dve.wait_ge(added, c * ADDS + 1 + b * K0 + k)
                    vec.scalar_tensor_tensor(out=x1[:, b, :], in0=gath[q][:, k, :], scalar=w_now[:, b, k:k + 1],
                                             in1=x1[:, b, :], op0=ALU.mult, op1=ALU.add).then_inc(added, 1)
                dve.wait_ge(added, c * ADDS + 1 + b * K0 + K0)
                dve.sem_inc(gath_used, 1)

            def norm(c):
                for b in range(NB):
                    ins = vec.bn_stats(stats[:, b, :], x1[:, b, :])
                ins.then_inc(stats_ready, 1)
                dve.wait_ge(stats_ready, c + 1)
                dve.sem_inc(carry, 1)
                for b in range(NB):
                    vec.bn_aggr(mv[:, b, :], stats[:, b, :]).then_inc(mv_ready, 1)
                dve.wait_ge(rstd_ready, c + 1)
                for b in range(NB):
                    vec.tensor_scalar(xn[:, b, :], x1[:, b, :], mv[:, b, 0:1], rstd[:, b:b + 1], ALU.subtract,
                                      ALU.mult).then_inc(xn_ready, 1)

            def body(c, last):
                at = cos[:, bass.ds(c * P, P)], sin[:, bass.ds(c * P, P)]
                for i in range(HKV + HQ):
                    dve.wait_ge(d_full, c * PD + DJ.index(("rope", i)) + 1)
                    if i >= 3:
                        dve.wait_ge(roped, c * (HKV + HQ) + i - 2)
                    src = d_bank("rope", i)
                    dst = kT[:, i, :, :] if i < HKV else qT[:, i - HKV, :, :]
                    vec.tensor_tensor(dst, src[:, :].rearrange("p (b t) -> p b t", b=NB),
                                      at[0].unsqueeze(1).to_broadcast([P, NB, P]), ALU.mult)
                    for lo, hi in ((0, 64), (64, 0)):
                        ins = vec.tensor_tensor(rot[lo:lo + 64, i % 3, :, :], src[hi:hi + 64, :].rearrange("p (b t) -> p b t", b=NB),
                                                at[1][hi:hi + 64, :].unsqueeze(1).to_broadcast([64, NB, P]), ALU.mult)
                    ins.then_inc(d_done, 1)
                if not last:
                    now(c + 1)
                for job in tile_order():
                    stage, b, g = job
                    if stage == "end":
                        if not last and b == PREP_AT - 1:
                            combine(c + 1, 0)
                            combine(c + 1, 1)
                        if not last and b == PREP_AT:
                            combine(c + 1, 2)
                            combine(c + 1, 3)
                            norm(c + 1)
                        continue
                    dve.wait_ge(d_full, c * PD + DJ.index(job) + 1)
                    src = d_bank(*job)
                    if stage == "S":
                        vec.tensor_tensor(Sm[:, g % 2, :, :], src[:, :].rearrange("p (r i) -> p r i", r=GR),
                                          mask[:, :].unsqueeze(1).to_broadcast([P, GR, P]), ALU.mult).then_inc(d_done, 1)
                    if stage == "o":
                        vec.tensor_tensor(oT[:, GR * g:GR * g + GR, :], src[:, :].rearrange("p (r i) -> p r i", r=GR),
                                          q_dec[:, GR * g:GR * g + GR, :], ALU.mult).then_inc(d_done, 1)
                    if stage == "kv":
                        part = kv[:, b, GR * g:GR * g + GR, :]
                        vec.tensor_tensor(part, part, src[:, :].rearrange("p (r i) -> p r i", r=GR), ALU.add).then_inc(d_done, 1)
                    if stage == "wo":
                        if b == 0:
                            dve.wait_ge(x1r_ready, c * 16 + 16)
                        dve.wait_ge(stored[b % 2], c * 32 + b // 2 * 16 + 16)
                        vec.tensor_tensor(res[:, b % 2, :], src[:, 0:D], x1r[:, b, :], ALU.add).then_inc(d_done, 1)

            dve.sem_inc(d_done, ND)
            dve.sem_inc(gath_used, 2)
            for s in stored:
                dve.sem_inc(s, 16)
            dve.wait_ge(loaded, 16 * N_LOAD)
            dve.wait_ge(setup, 2)
            now(0)
            for b in range(NB):
                combine(0, b)
            norm(0)
            steps(dve, body)


def ffn_phase(nc, io, scratch, out):
    with ExitStack() as ctx:
        def sb(name, shape, dt=F32):
            return ctx.enter_context(nc.sbuf_tensor("f_" + name, shape, dt))

        def sem(name):
            return ctx.enter_context(nc.semaphore("f_" + name))

        NE = E1 + 1
        W1 = 2 * P + 2 * P + D
        w_f = sb("w_f", [P, 3, W1])
        w_hi = sb("w_hi", [P, NE, W1], FR)
        w_lo = sb("w_lo", [P, NE, W1], FR)
        gw = sb("gw", [P, 2, E1])
        bias = sb("bias", [P, E1])
        iota = sb("iota", [P, E1])
        x_f = sb("x_f", [P, 2, 2, NB, P])
        x_hi = sb("x_hi", [P, 2, 2, NB * P], FR)
        x_lo = sb("x_lo", [P, 2, 2, NB * P], FR)
        acc = sb("acc", [P, 2, NB, D])
        score = sb("score", [P, NB, E1])
        picked = sb("picked", [P, NB, E1])
        t8 = sb("t8", [P, NB, 8])
        i8 = sb("i8", [P, NB, 8], U32)
        idx = sb("idx", [P, NB, 4])
        hot = sb("hot", [P, NB, 4, E1])
        tot = sb("tot", [P, NB])
        cw = sb("cw", [P, 2, NB, NE])
        h_f = sb("h_f", [P, 2, NB * P])
        h_hi = sb("h_hi", [P, 2, NB * P], FR)
        h_lo = sb("h_lo", [P, 2, NB * P], FR)
        psG = [ctx.enter_context(nc.psum_tensor(f"f_psG{i}", [P, 512], F32)) for i in range(2)]
        psU = [ctx.enter_context(nc.psum_tensor(f"f_psU{i}", [P, 512], F32)) for i in range(2)]
        psY = [ctx.enter_context(nc.psum_tensor(f"f_psY{i}", [P, 512], F32)) for i in range(4)]
        loaded, setup, carry = sem("loaded"), sem("setup"), sem("carry")
        w_ready = [sem(f"w_ready{i}") for i in range(3)]
        ready = [sem("ready0"), sem("ready1")]
        stored = [sem("stored0"), sem("stored1")]
        w_cut, w_done, x_cut, x_done = sem("w_cut"), sem("w_done"), sem("x_cut"), sem("x_done")
        logit, scored, step, g_full, u_full, silu, h_ready, hi_ready, lo_ready, y_full, y_used = (
            sem(k) for k in ("logit", "scored", "step", "g_full", "u_full", "silu", "h_ready", "hi_ready", "lo_ready",
                             "y_full", "y_used"))
        block = ctx.enter_context(nc.Block())
        acc1_t = scratch["acc1"].rearrange("(b c t) d -> c t b d", c=NC, t=P)
        out_t = out.rearrange("b (c t) d -> c t b d", t=P)
        STEPS = GATE_STEPS
        seen = {}
        SLOTS = 2 * NE + 2
        LOGIT_SLOT = 2 * (NE - 2)
        assert SLOTS % 4 == 0

        def slot(e, j):
            return 2 * e + j + (2 if e >= NE - 2 else 0)

        def at(q, e):
            return (q * NE + e) % 2

        def steps(eng, body):
            with eng.Fori(0, NC // 2 - 1) as i:
                body(i * 2, i, 0, False)
                body(i * 2 + 1, i, 1, False)
            body(NC - 2, NC // 2 - 1, 0, False)
            body(NC - 1, NC // 2 - 1, 1, True)

        def after(c, q, e, last):
            return (c, q, e + 1) if e + 1 < NE else None if last else (c + 1, 1 - q, 0)

        @block.sync
        def _(sp):
            sp.dma_start(gw[:, :, :], io["gw1"]).then_inc(loaded, 16)
            sp.dma_start(bias[:, :], io["bias1"].rearrange("(a n) -> a n", a=1).to_broadcast([P, E1])).then_inc(loaded, 16)

            def x_load(c, i, q):
                sp.wait_ge(stored[q], i * 16 + 16)
                sp.dma_start(x_f[:, q, :, :, :].rearrange("p k b t -> p (k b t)"), scratch["xnT1"][c]).then_inc(ready[q], 16)
                sp.dma_start(acc[:, q, :, :], acc1_t[c]).then_inc(ready[q], 16)

            for e in range(NE):
                if e == 2:
                    x_load(0, 0, 0)
                if e >= 3:
                    sp.wait_ge(w_done, e - 2)
                sp.dma_start(w_f[:, e % 3, :], io["w1"][e]).then_inc(w_ready[e % 3], 16)
            x_load(1, 0, 1)
            with sp.Fori(1, NC // 2) as i:
                for q in range(2):
                    x_load(i * 2 + q, i, q)

        @block.gpsimd
        def _(pool):
            nc.gpsimd.iota(iota[:, :], [[1, E1]], base=0, channel_multiplier=0,
                           allow_small_or_imprecise_dtypes=True).then_inc(setup, 1)
            nc.gpsimd.memset(cw[:, :, :, :], 1.0).then_inc(setup, 1)

            def body(c, i, q, last):
                for e in range(NE):
                    pool.wait_ge(hi_ready, c * NE + e + 1)
                    n = at(q, e)
                    nc.gpsimd.tensor_tensor(h_lo[:, n, :], h_f[:, n, :], h_hi[:, n, :].bitcast(F32), ALU.subtract).then_inc(lo_ready, 1)

            pool.sem_inc(lo_ready, 2)
            steps(pool, body)

        @block.scalar
        def _(act):
            def cut_x(c, i, q):
                act.wait_ge(ready[q], i * 32 + 32)
                nc.scalar.activation(x_hi[:, q, :, :].rearrange("p k n -> p (k n)"),
                                     x_f[:, q, :, :, :].rearrange("p k b t -> p (k b t)"), ACT.Copy).then_inc(x_cut, 1)

            def cut_w(e):
                act.wait_ge(w_ready[e % 3], e // 3 * 16 + 16)
                nc.scalar.activation(w_hi[:, e, :], w_f[:, e % 3, :], ACT.Copy).then_inc(w_cut, 1)

            def gate(c, q, e):
                m = c * NE + e
                act.wait_ge(g_full, m + 1)
                act.wait_ge(lo_ready, m - 2 + 1 + 2)
                nc.scalar.activation(h_f[:, at(q, e), :], psG[at(q, e)][:, :], ACT.Silu).then_inc(silu, 1)

            def high(c, q, e):
                m = c * NE + e
                act.wait_ge(h_ready, m + 1 + 2)
                act.wait_ge(y_full, (m - 2) * 2 + 2 + 4)
                nc.scalar.activation(h_hi[:, at(q, e), :], h_f[:, at(q, e), :], ACT.Copy).then_inc(hi_ready, 1)

            def sigmoid(c):
                act.wait_ge(logit, c + 1)
                nc.scalar.activation(score[:, :, :], psY[LOGIT_SLOT % 4][:, 0:NB * E1].rearrange("p (b e) -> p b e", b=NB),
                                     ACT.Sigmoid).then_inc(scored, 1)

            def body(c, i, q, last):
                for e in range(NE):
                    if e == NE // 2 and not last:
                        cut_x(c + 1, i + q, 1 - q)
                    if e == NE - 2 and not last:
                        sigmoid(c + 1)
                    nxt = after(c, q, e, last)
                    if nxt:
                        gate(*nxt)
                    high(c, q, e)
                act.wait_ge(y_used, c * SLOTS + SLOTS + 4)
                act.dma_start(out_t[c], acc[:, q, :, :]).then_inc(stored[q], 16)

            act.sem_inc(stored[0], 16)
            act.sem_inc(stored[1], 16)
            act.wait_ge(setup, 2)
            for e in range(2):
                cut_w(e)
            cut_x(0, 0, 0)
            for e in range(2, NE):
                cut_w(e)
            sigmoid(0)
            gate(0, 0, 0)
            steps(act, body)
            for s in stored:
                act.wait_ge(s, 16 * NC // 2 + 16)

        @block.tensor
        def _(pe):
            def exact(dst, pairs, start, stop):
                terms = [(w[i], x[j]) for w, x in pairs for i, j in ((0, 0), (0, 1), (1, 0))]
                for n, (w, x) in enumerate(terms):
                    ins = nc.tensor.matmul(dst, w, x, start=start and n == 0, stop=stop and n == len(terms) - 1)
                return ins

            def project(dst, q, e, col):
                return exact(dst[:, :], [((w_hi[:, e, col + k * P:col + k * P + P], w_lo[:, e, col + k * P:col + k * P + P]),
                                          (x_hi[:, q, k, :], x_lo[:, q, k, :])) for k in range(2)], True, True)

            def up(c, q, e):
                m = c * NE + e
                if isinstance(c, int) and c == 0:
                    pe.wait_ge(w_done, e + 1)
                pe.wait_ge(silu, m - 2 + 1 + 2)
                project(psG[at(q, e)], q, e, 0).then_inc(g_full, 1)
                pe.wait_ge(h_ready, m - 2 + 1 + 2)
                project(psU[at(q, e)], q, e, 2 * P).then_inc(u_full, 1)

            def down(c, q, e):
                pe.wait_ge(lo_ready, c * NE + e + 1 + 2)
                for j in range(2):
                    s = slot(e, j)
                    pe.wait_ge(y_used, c * SLOTS + s - 3 + 4)
                    for r in range(2):
                        cols = slice((2 * j + r) * P, (2 * j + r + 1) * P)
                        n = at(q, e)
                        ins = exact(psY[s % 4][:, r * D:(r + 1) * D],
                                    [((h_hi[:, n, cols], h_lo[:, n, cols]), (w_hi[:, e, 4 * P:W1], w_lo[:, e, 4 * P:W1]))], True, True)
                    ins.then_inc(y_full, 1)

            def logits(c, q, first=False):
                pe.wait_ge(x_done, c + 1)
                if not first:
                    pe.wait_ge(y_used, (c - 1) * SLOTS + LOGIT_SLOT + 1 - 3 + 4)
                for b in range(NB):
                    for k in range(2):
                        ins = nc.tensor.matmul(psY[LOGIT_SLOT % 4][:, b * E1:(b + 1) * E1], x_f[:, q, k, b, :], gw[:, k, :],
                                               start=(k == 0), stop=(k == 1))
                ins.then_inc(logit, 1)

            def body(c, i, q, last):
                for e in range(NE):
                    if e == NE - 2 and not last:
                        logits(c + 1, 1 - q)
                    n1 = after(c, q, e, last)
                    n2 = after(*n1, last) if n1 else None
                    if n2:
                        up(*n2)
                    down(c, q, e)

            pe.sem_inc(silu, 2)
            pe.sem_inc(y_full, 4)
            pe.wait_ge(loaded, 32)
            logits(0, 0, True)
            for e in range(2):
                up(0, 0, e)
            pe.wait_ge(w_done, NE)
            steps(pe, body)

        @block.vector
        def _(dve):
            v = nc.vector

            def cut_x(c, q):
                dve.wait_ge(x_cut, c + 1)
                v.tensor_tensor(x_lo[:, q, :, :].rearrange("p k n -> p (k n)"), x_f[:, q, :, :, :].rearrange("p k b t -> p (k b t)"),
                                x_hi[:, q, :, :].rearrange("p k n -> p (k n)").bitcast(F32), ALU.subtract).then_inc(x_done, 1)

            def cut_w(e):
                dve.wait_ge(w_cut, e + 1)
                v.tensor_tensor(w_lo[:, e, :], w_f[:, e % 3, :], w_hi[:, e, :].bitcast(F32), ALU.subtract).then_inc(w_done, 1)

            def gates(c, q):
                n = [0]

                def link(ins):
                    n[0] += 1
                    ins.then_inc(step, 1)
                    dve.wait_ge(step, c * STEPS + n[0])

                dve.wait_ge(scored, c + 1)
                link(v.tensor_tensor(picked[:, :, :], score[:, :, :], bias[:, :].unsqueeze(1).to_broadcast([P, NB, E1]), ALU.add))
                dve.sem_inc(carry, 1)
                for b in range(NB):
                    ins = v.max(t8[:, b, :], picked[:, b, :])
                link(ins)
                dve.sem_inc(carry, 1)
                for b in range(NB):
                    ins = v.max_index(i8[:, b, :], t8[:, b, :], picked[:, b, :])
                link(ins)
                link(v.tensor_copy(idx[:, :, :], i8[:, :, 0:4]))
                link(v.tensor_tensor(hot[:, :, :, :], iota[:, :].unsqueeze(1).unsqueeze(1).to_broadcast([P, NB, 4, E1]),
                                     idx[:, :, :].unsqueeze(3).to_broadcast([P, NB, 4, E1]), ALU.is_equal))
                link(v.tensor_reduce(picked[:, :, :], hot[:, :, :, :].rearrange("p b k e -> p b e k"), AX.X, ALU.add))
                link(v.tensor_tensor(picked[:, :, :], picked[:, :, :], score[:, :, :], ALU.mult))
                link(v.tensor_reduce(tot[:, :], picked[:, :, :], AX.X, ALU.add))
                link(v.reciprocal(tot[:, :], tot[:, :]))
                link(v.tensor_tensor(cw[:, q, :, 0:E1], picked[:, :, :], tot[:, :].unsqueeze(2).to_broadcast([P, NB, E1]), ALU.mult))
                dve.sem_inc(y_used, 2)
                seen["gates"] = n[0]

            def product(c, q, e):
                m = c * NE + e
                n = at(q, e)
                dve.wait_ge(u_full, m + 1)
                dve.wait_ge(silu, m + 1 + 2)
                v.tensor_tensor(h_f[:, n, :], h_f[:, n, :], psU[n][:, :], ALU.mult).then_inc(h_ready, 1)

            def collect(c, q, e):
                for j in range(2):
                    dve.wait_ge(y_full, (c * NE + e) * 2 + j + 1 + 4)
                    for r in range(2):
                        b = 2 * j + r
                        ins = v.scalar_tensor_tensor(out=acc[:, q, b, :], in0=psY[slot(e, j) % 4][:, r * D:(r + 1) * D],
                                                     scalar=cw[:, q, b, e:e + 1], in1=acc[:, q, b, :], op0=ALU.mult, op1=ALU.add)
                    ins.then_inc(y_used, 1)

            def body(c, i, q, last):
                dve.wait_ge(ready[q], i * 32 + 32)
                for e in range(NE):
                    if e == NE // 2 and not last:
                        cut_x(c + 1, 1 - q)
                    if e == NE - 2 and not last:
                        gates(c + 1, 1 - q)
                    if e == NE - 2 and last:
                        dve.wait_ge(y_used, c * SLOTS + LOGIT_SLOT + 4)
                        dve.sem_inc(y_used, 2)
                    nxt = after(c, q, e, last)
                    if nxt:
                        product(*nxt)
                    if e:
                        s = slot(e, 0)
                        dve.wait_ge(y_used, c * SLOTS + s + 4)
                    collect(c, q, e)

            dve.sem_inc(h_ready, 2)
            dve.sem_inc(y_used, 2)
            dve.wait_ge(setup, 2)
            dve.wait_ge(loaded, 32)
            for e in range(2):
                cut_w(e)
            cut_x(0, 0)
            for e in range(2, NE):
                cut_w(e)
            gates(0, 0)
            product(0, 0, 0)
            steps(dve, body)
        assert seen["gates"] == STEPS, seen

def kernel(**inputs):
    import numpy as np
    import concourse.bacc as bacc
    from concourse.bass_utils import run_bass_kernel_spmd as run

    nc = bacc.Bacc("TRN2", target_bir_lowering=False, num_devices=1)
    arrays, io = {}, {}

    def give(name, a):
        arrays["in_" + name] = np.ascontiguousarray(a)
        io[name] = nc.dram_tensor("in_" + name, arrays["in_" + name].shape, F32, kind="ExternalInput").ap()

    I = {k: np.asarray(v) for k, v in inputs.items()}
    m = "L0_attn_"
    give("x", I[m + "x"])
    give("W_in", I[m + "W_in"])
    give("b_in", I[m + "b_in"])
    give("b_xbc", I[m + "b_in"][INNER:2 * INNER + 2 * D_STATE].reshape(6, P).T)
    give("b_z", I[m + "b_in"][:INNER].reshape(4, P).T)
    give("conv_w", I[m + "conv_w"].reshape(4, 6, P).transpose(2, 1, 0))
    give("conv_b", I[m + "conv_b"].reshape(6, P).T)
    give("norm_w", I[m + "norm_w"].reshape(4, P).T)
    for n in ("A_log", "dt_bias", "D_param", "W_out", "b_out"):
        give(n, I[m + n])
    give("Sg", I["L0_ffn_Sg"].reshape(2, 2, P, 256).transpose(2, 1, 0, 3))
    give("Su", I["L0_ffn_Su"].reshape(2, 2, P, 256).transpose(2, 1, 0, 3))
    give("Sd", I["L0_ffn_Sd"])
    sums, pairs = level_constants()
    give("sums", sums)
    give("pairs", pairs)
    give("ident", np.eye(P, dtype=np.float32))
    give("Wr", I["L0_ffn_Wr"])
    give("r_bias", I["L0_ffn_router_bias"])
    give("before", np.triu(np.ones((P, P), np.float32), 1))
    gu = np.stack([I["L0_ffn_Wg"], I["L0_ffn_Wu"]]).reshape(2, EXPERTS // 2, 2, 2, P, HID0)
    give("wgu0", gu.transpose(1, 4, 0, 2, 3, 5).reshape(EXPERTS // 2, P, 8 * HID0))
    give("wd0", I["L0_ffn_Wd"].reshape(EXPERTS * HID0, D))
    n = "L1_attn_"
    for w in ("wq", "wk", "wv"):
        a = I[n + w]
        give(w, a.T.reshape(2, P, a.shape[0]).transpose(1, 0, 2))
    give("wo", I[n + "wo"].T.reshape(HQ, P, D).transpose(1, 0, 2))
    for k, a in attention_constants().items():
        give(k, a.astype(np.float32))
    f = "L1_ffn_"
    gate, up = (np.concatenate([I[f + "w_" + w], I[f + "sw_" + w][None]]).reshape(E1 + 1, P, 2, P).transpose(0, 3, 2, 1)
                for w in ("gate", "up"))
    down = np.concatenate([I[f + "w_down"], I[f + "sw_down"][None]]).transpose(0, 2, 1)
    give("w1", np.concatenate([gate.reshape(E1 + 1, P, 2 * P), up.reshape(E1 + 1, P, 2 * P), down], axis=2))
    give("gw1", I[f + "gate_w"].T.reshape(2, P, E1).transpose(1, 0, 2))
    give("bias1", I[f + "expert_bias"])
    scratch = {}
    kind = "ExternalOutput" if DEBUG else "Internal"
    for n, shape in (("acc0", (N_TOK, D)), ("xb", (EXPERTS * CAP, D)), ("yb", (EXPERTS * CAP, D)), ("xn", (N_TOK, D)), ("xnT", (NC, P, 2 * NB * P)), ("x1", (N_TOK, D)), ("acc1", (N_TOK, D)),
                     ("xnT1", (NC, P, 2 * NB * P))):
        scratch[n] = nc.dram_tensor("s_" + n, shape, F32, kind=kind).ap()
    out = nc.dram_tensor("out", (NB, SEQ_LEN, D), F32, kind="ExternalOutput").ap()
    mixer_phase(nc, io, scratch)
    with ExitStack() as ctx:
        keep = {"w_all": ctx.enter_context(nc.sbuf_tensor("w_all", [P, NB * NC, K0], F32)),
                "slot_all": ctx.enter_context(nc.sbuf_tensor("slot_all", [P, NB * NC, K0], U32))}
        router_phase(nc, io, scratch, keep)
        expert_phase(nc, io, scratch)
        attention_phase(nc, io, scratch, keep)
    ffn_phase(nc, io, scratch, out)
    r = run(nc, [arrays], core_ids=[0])
    return r.results[0]["out"]
```

```python
from contextlib import ExitStack

import concourse.bass as bass
from concourse import mybir

ALU = mybir.AluOpType
ACT = mybir.ActivationFunctionType
F32 = mybir.dt.float32
FR = mybir.dt.float32r
U32 = mybir.dt.uint32
AX = mybir.AxisListType
P = 128
NB, SEQ_LEN, D = 4, 1024, 256
NC = SEQ_LEN // P
N_TOK = NB * SEQ_LEN
INNER, HEADS, D_STATE = 512, 64, 128
D_PROJ = 2 * INNER + 2 * D_STATE + HEADS
LEVELS = 7
HQ, HKV, DH = 16, 4, 128
CUT_HEADS = 7
E1 = 16
GATE_STEPS = 10
EXPERTS, K0, CAP, HID0 = 64, 4, 64, 64
W0 = 8 * HID0 + D
ROUTER_STEPS = 31
SUM_END, SUM_POST, SUM_START, SUM_ALL = LEVELS, LEVELS + 1, 2 * LEVELS, 2 * LEVELS + 1
N_SUMS = 2 * LEVELS + 2
PRE_D = 3
POOL_ADDS = [1, "off", 4, 6]
MIX_STEPS = (33, 4)


def h1(ap):
    return ap.rearrange("p (h e) -> p h e", e=8)


def h8(ap, n):
    return ap.rearrange("p k (h e) -> p k h e", e=8)


def h8b(ap, n):
    return h1(ap).unsqueeze(1).to_broadcast([P, n, HEADS, 8])

def level_constants():
    import numpy as np
    t = np.arange(128)
    sums = np.zeros((N_SUMS, 128, 128), np.float32)
    pairs = np.zeros((LEVELS, 128, 128), np.float32)
    for k in range(LEVELS):
        for m in range(128):
            mid = ((m >> (k + 1)) << (k + 1)) + (1 << k)
            if m < mid:
                sums[k, :, m] = (t > m) & (t <= (mid if k == 0 else mid - 1))
                pairs[k, m, :] = (t >= mid) & (t < mid + (1 << k))
            elif k > 0:
                sums[SUM_POST + k - 1, :, m] = (t >= mid) & (t <= m)
    for m in range(128):
        sums[SUM_END, :, m] = t > m
        sums[SUM_START, :, m] = t <= m
    sums[SUM_ALL] = 1.0
    return np.ascontiguousarray(sums.transpose(1, 0, 2)), np.ascontiguousarray(pairs.transpose(1, 0, 2))


def mixer_phase(nc, io, scratch):
    with ExitStack() as ctx:
        def sb(name, shape, dt=F32):
            return ctx.enter_context(nc.sbuf_tensor("m_" + name, shape, dt))

        def sem(name):
            return ctx.enter_context(nc.semaphore("m_" + name))

        w_in = sb("w_in", [P, 2, D_PROJ])
        w_out = sb("w_out", [P, 4, D])
        s_gate = sb("s_gate", [P, 2, 512])
        s_up = sb("s_up", [P, 2, 512])
        s_down = sb("s_down", [P, 4, D])
        b_xbc = sb("b_xbc", [P, 6])
        b_z = sb("b_z", [P, 4])
        cw = sb("cw", [P, 6, 4])
        cb = sb("cb", [P, 6])
        normw = sb("normw", [P, 4])
        dt_add = sb("dt_add", [P, HEADS])
        dt_add2 = sb("dt_add2", [P, HEADS])
        a_exp = sb("a_exp", [P, HEADS])
        d_par = sb("d_par", [P, HEADS])
        b_out = sb("b_out", [P, D])
        sums = sb("sums", [P, N_SUMS, P], FR)
        pairs = sb("pairs", [P, LEVELS, P])
        ident = sb("ident", [P, P])
        ones = sb("ones", [P, 2])
        eps = sb("eps", [P, 2])
        x_ln = sb("x_ln", [P, NB, D])
        x_res = sb("x_res", [P, NB, D])
        xn = sb("xn", [P, NB, D])
        stats = sb("stats", [P, NB, 6])
        mv = sb("mv", [P, NB, 2])
        lnv = sb("lnv", [P, NB])
        rstd = sb("rstd", [P, NB])
        xnT = sb("xnT", [P, 2, NB, P])
        xin = sb("xin", [P, 6, NB, P + 3])
        xc = sb("xc", [P, 6, NB, P])
        zs = sb("zs", [P, 4, NB, P])
        hs = sb("hs", [P, 4, NB, P])
        E = sb("E", [P, N_SUMS, NB, HEADS])
        dtr = sb("dtr", [P, NB, HEADS])
        dtu = sb("dtu", [P, NB, HEADS])
        dtw = sb("dtw", [P, NB, HEADS])
        dtl = sb("dtl", [P, NB, HEADS])
        dtd = sb("dtd", [P, NB, HEADS])
        dtc = sb("dtc", [P, NB, HEADS])
        adt = sb("adt", [P, NB, HEADS])
        adt_hi = sb("adt_hi", [P, NB, HEADS], FR)
        adt_lo = sb("adt_lo", [P, NB, HEADS], FR)
        d_over = sb("d_over", [P, NB, HEADS])
        Xd = sb("Xd", [P, 2, 512])
        Xp = sb("Xp", [P, 2, 8, 512])
        Gm = sb("Gm", [P, 2, LEVELS, P])
        gj = sb("gj", [P, P])
        gd = sb("gd", [P, 2])
        coef = sb("coef", [P, 2, HEADS])
        Btok = sb("Btok", [P, 2, P])
        Yd = sb("Yd", [P, 2, 512])
        Yp = sb("Yp", [P, 2, 512])
        T = sb("T", [P, 3, 512])
        S = sb("S", [P, NB, 512])
        yg = sb("yg", [P, 2, 4, P])
        y2 = sb("y2", [P, 2, 4, P])
        lss = sb("lss", [P, 2])
        rss = sb("rss", [P, 2])
        res = sb("res", [P, 2, D])
        NA, ND = 2, 6
        psA = [ctx.enter_context(nc.psum_tensor(f"m_psA{i}", [P, 512], F32)) for i in range(NA)]
        psD = [ctx.enter_context(nc.psum_tensor(f"m_psD{i}", [P, 512], F32)) for i in range(ND)]

        SEQ = [1, 2, 0, "off", 3, 4, 5, 6]
        LATE = [("T4", 2), ("T3", 3), ("T4", 3)]
        ORDER = [("dt", 0), ("xbc", 0), ("xbc", 1), ("T3", 3), ("xbc", 2), ("T4", 2), ("xbc", 3), ("xbc", 4), ("xbc", 5),
                 ("z", 0), ("z", 1), ("z", 2), ("z", 3), ("T4", 3)] + [("E", i) for i in range(8)] \
            + [("gu", 0), ("gu", 1), ("T1", 0), ("gu", 2), ("gu", 3), ("T1", 1), ("T2", 0), ("T1", 2), ("T2", 1), ("T3", 0),
               ("T1", 3), ("T2", 2), ("T4", 0), ("T3", 1), ("T2", 3), ("xt", 0), ("T4", 1), ("T3", 2)]
        TAIL = ORDER[:ORDER.index(("T4", 3)) + 1]

        def a_jobs(stage, b):
            return {"xbc": [("xbc", b)], "z": [("z", b)], "E": [("E", b)], "gu": [("g", b)], "T1": [("btok", b)], "T4": [("ss", b)],
                    "xt": [("xt", 0), ("xt", 1)]}.get(stage, [])

        def d_jobs(stage, b):
            return {"dt": [("dt", 0)], "gu": [("u", b)], "T1": [("xtok", b), ("G", b)],
                    "T2": [("L", b, k) for k in SEQ] + [("snew", b)], "T3": [("yT", b)], "T4": [("out", b)]}.get(stage, [])

        A = [j for s in ORDER for j in a_jobs(*s)]
        DJ = [j for s in ORDER for j in d_jobs(*s)]
        PA, PD = len(A), len(DJ)
        PRE_A = PA - A.index(("xt", 0))

        def bank(jobs, ring, job):
            return ring[jobs.index(job) % len(ring)]

        def a_bank(*job):
            return bank(A, psA, job)

        def d_bank(*job):
            return bank(DJ, psD, job)

        def done(c, *job):
            return c * PD + DJ.index(job) + 1 + ND

        def adone(c, *job):
            return c * PA + A.index(job) + 1 + NA + PRE_A

        def credit(jobs, n, job):
            j = jobs.index(job)
            before = j - n if j >= n else max(i for i in range(len(jobs)) if i % n == j) - len(jobs)
            return before + 1 + n

        def skip(eng, full_or_done, jobs, n, stage_jobs, c):
            for job in stage_jobs:
                if c * len(jobs) + jobs.index(job) + n > 0:
                    eng.wait_ge(full_or_done, c * len(jobs) + jobs.index(job) + n)
                eng.sem_inc(full_or_done, 1)

        def steps(eng, body):
            body(0, ORDER, True, False)
            with eng.Fori(1, NC - 1) as c:
                body(c, ORDER, False, False)
            body(NC - 1, ORDER, False, True)
            body(NC, TAIL, False, True)

        def absent(c, order, first, stage, b):
            return (first and (stage, b) in LATE) or (order is TAIL and (stage, b) not in LATE)

        a_full, a_done = sem("a_full"), sem("a_done")
        d_full, d_done = sem("d_full"), sem("d_done")
        loaded, x_ready, xres_ready = sem("loaded"), sem("x_ready"), sem("xres_ready")
        x_used, xres_used = sem("x_used"), sem("xres_used")
        stored, xn_stored, xnT_stored = [sem("stored0"), sem("stored1")], sem("xn_stored"), sem("xnT_stored")
        setup, zeroed = sem("setup"), sem("zeroed")
        mv_ready, rstd_ready, xn_ready = sem("mv_ready"), sem("rstd_ready"), sem("xn_ready")
        lnv_ready, dve_step, pool_step = sem("lnv_ready"), sem("dve_step"), sem("pool_step")
        conv_ready, xc_ready, hist = sem("conv_ready"), sem("xc_ready"), sem("hist")
        dt_in, dtu_ready, dtw_ready, dtl_ready, adt_ready = (sem(k) for k in ("dt_in", "dtu_ready", "dtw_ready", "dtl_ready", "adt_ready"))
        Gm_ready, XpD_ready, XpP_ready, coef_ready = sem("Gm_ready"), sem("XpD_ready"), sem("XpP_ready"), sem("coef_ready")
        T_used, S_decayed, Y_ready, y2_ready, rss_ready = (sem(k) for k in ("T_used", "S_decayed", "Y_ready", "y2_ready", "rss_ready"))
        xb_ready, stats_ready = sem("xb_ready"), sem("stats_ready")
        adt_cut, adt_done = sem("adt_cut"), sem("adt_done")
        ident_ready, loaded_late, w_out_ready = sem("ident_ready"), sem("loaded_late"), sem("w_out_ready")
        N_LOAD, N_LATE = 11, 6
        carry, res_half, cleared = sem("carry"), sem("res_half"), sem("cleared")
        DVE_STEPS, POOL_STEPS = MIX_STEPS
        seen = {}

        block = ctx.enter_context(nc.Block())
        x_t = io["x"].rearrange("b (c t) d -> c t b d", t=P)
        acc_t = scratch["acc0"].rearrange("(b c t) d -> c b t d", c=NC, t=P)
        xn_t = scratch["xn"].rearrange("(b c t) d -> c t b d", c=NC, t=P)

        @block.sync
        def _(sp):
            sp.dma_start(x_ln[:, :, :], x_t[0]).then_inc(x_ready, 16)
            sp.dma_start(ident[:, :], io["ident"]).then_inc(ident_ready, 16)

            def rows(v, n):
                return v.rearrange("(a n) -> a n", a=1).to_broadcast([P, n])

            for dst, src in (
                (w_in[:, :, :], io["W_in"].rearrange("(k p) n -> p k n", p=P)),
                (dt_add[:, :], rows(io["b_in"][D_PROJ - HEADS:D_PROJ], HEADS)), (dt_add2[:, :], rows(io["dt_bias"], HEADS)),
                (a_exp[:, :], rows(io["A_log"], HEADS)), (d_par[:, :], rows(io["D_param"], HEADS)),
                (b_out[:, :], rows(io["b_out"], D)), (b_xbc[:, :], io["b_xbc"]), (b_z[:, :], io["b_z"]),
                (cw[:, :, :], io["conv_w"]), (cb[:, :], io["conv_b"]), (normw[:, :], io["norm_w"]),
            ):
                sp.dma_start(dst, src).then_inc(loaded, 16)
            sp.wait_ge(x_used, 1)
            sp.dma_start(x_ln[:, :, :], x_t[1]).then_inc(x_ready, 16)
            for dst, src in (
                (E[:, :, 0:2, :], io["sums"].rearrange("p s (b h) -> p s b h", b=2)), (pairs[:, :, :], io["pairs"]),
                (w_out[:, :, :], io["W_out"].rearrange("(g p) n -> p g n", p=P)),
                (s_gate[:, :, :].rearrange("p k (s h) -> p k s h", s=2), io["Sg"]),
                (s_up[:, :, :].rearrange("p k (s h) -> p k s h", s=2), io["Su"]),
                (s_down[:, :, :], io["Sd"].rearrange("s (q p) d -> p (s q) d", p=P)),
            ):
                sp.dma_start(dst, src).then_inc(loaded_late, 16)
            sp.wait_ge(zeroed, 5)
            for i in range(4):
                sp.dma_start(scratch["xb"].rearrange("(i p r) d -> i p (r d)", i=4, p=P)[i],
                             S[:, :, :].rearrange("p b n -> p (b n)")).then_inc(cleared, 16)
            def save(c, own, b):
                sp.wait_ge(d_done, done(c, "out", b))
                sp.dma_start(acc_t[own, b], res[:, b % 2, :]).then_inc(stored[b % 2], 16)

            def body(c, order, first, last):
                if order is TAIL:
                    save(c, c - 1, 2)
                    save(c, c - 1, 3)
                    return
                if not first and not last:
                    sp.wait_ge(x_used, c + 1)
                    sp.dma_start(x_ln[:, :, :], x_t[c + 1]).then_inc(x_ready, 16)
                sp.wait_ge(xn_ready, c * NB + NB)
                sp.dma_start(xn_t[c], xn[:, :, :]).then_inc(xn_stored, 16)
                sp.wait_ge(a_done, adone(c - 1, "xt", 1))
                sp.dma_start(scratch["xnT"][c], xnT[:, :, :, :].rearrange("p k b t -> p (k b t)")).then_inc(xnT_stored, 16)
                if not first:
                    save(c, c - 1, 2)
                    save(c, c - 1, 3)
                sp.wait_ge(xres_used, c + 1)
                sp.dma_start(x_res[:, :, :], x_t[c]).then_inc(xres_ready, 16)
                save(c, c, 0)
                save(c, c, 1)

            steps(sp, body)
            for s in stored:
                sp.wait_ge(s, 16 * NC * NB // 2 + 16)
            sp.wait_ge(xn_stored, 16 * NC)
            sp.wait_ge(xnT_stored, 16 * NC)

        @block.gpsimd
        def _(pool):
            n = [0]
            nc.gpsimd.memset(xin[:, :, :, 0:3], 0.0).then_inc(zeroed, 1)
            nc.gpsimd.memset(S[:, :, :], 0.0).then_inc(zeroed, 1)
            nc.gpsimd.memset(ones[:, :], 1.0).then_inc(zeroed, 1)
            nc.gpsimd.memset(eps[:, 0:1], 1e-5).then_inc(zeroed, 1)
            nc.gpsimd.memset(eps[:, 1:2], 1e-6).then_inc(zeroed, 1)
            pool.wait_ge(zeroed, 5)

            def body(c, order, first, last):
                def link(ins):
                    n[0] += 1
                    ins.then_inc(pool_step, 1)
                    pool.wait_ge(pool_step, c * POOL_STEPS + n[0])

                if order is TAIL:
                    return
                n[0] = 0
                for stage, b in order:
                    q, m = b % 2, c * NB + b
                    if stage == "gu" and b == 0:
                        pool.wait_ge(xres_ready, c * 16 + 16)
                        nc.gpsimd.tensor_tensor(x_res[:, :, :], x_res[:, :, :], b_out[:, :].unsqueeze(1).to_broadcast([P, NB, D]),
                                                ALU.add).then_inc(xb_ready, 1)
                    if stage == "T1":
                        pool.wait_ge(a_done, adone(c, "E", 7))
                        pool.wait_ge(d_done, done(c, "xtok", b))
                        nc.gpsimd.tensor_tensor(h8(Xp[:, q, PRE_D:8, :], 8 - PRE_D), h8b(Xd[:, q, :], 8 - PRE_D),
                                                E[:, PRE_D:8, b, :].unsqueeze(3).to_broadcast([P, 8 - PRE_D, HEADS, 8]),
                                                ALU.mult).then_inc(XpP_ready, 1)
                        pool.wait_ge(coef_ready, m + 1)
                        link(nc.gpsimd.tensor_tensor(h1(Yp[:, q, :]), h1(Xd[:, q, :]),
                                                     coef[:, q, :].unsqueeze(2).to_broadcast([P, HEADS, 8]), ALU.mult))
                    if stage == "T2":
                        for k in SEQ:
                            if k in POOL_ADDS:
                                j = POOL_ADDS.index(k)
                                pool.wait_ge(d_done, done(c, "L", b, k))
                                ins = nc.gpsimd.tensor_tensor(Yp[:, q, :], Yp[:, q, :], T[:, j % 2, :], ALU.add)
                                ins.then_inc(T_used, 1)
                                pool.wait_ge(T_used, m * 4 + j + 1 + 2)
                            if k == "off":
                                if first and b == 0:
                                    pool.wait_ge(cleared, 64)
                                pool.wait_ge(d_full, c * PD + DJ.index(("L", b, "off")) + 1)
                                nc.gpsimd.tensor_tensor(h1(S[:, b, :]), h1(S[:, b, :]),
                                                        E[:, SUM_ALL, b, :].unsqueeze(2).to_broadcast([P, HEADS, 8]),
                                                        ALU.mult).then_inc(S_decayed, 1)
                seen["pool"] = n[0]

            steps(pool, body)

        @block.scalar
        def _(act):
            def A_wait(c, *job):
                act.wait_ge(a_full, c * PA + A.index(job) + 1 + PRE_A)

            def norm_log(c):
                act.wait_ge(mv_ready, c * NB + NB)
                nc.scalar.activation(lnv[:, :], mv[:, :, 1], ACT.Ln, bias=eps[:, 0:1]).then_inc(lnv_ready, 1)

            def norm_scale(c):
                act.wait_ge(lnv_ready, c + 1)
                nc.scalar.activation(rstd[:, :], lnv[:, :], ACT.Exp, scale=-0.5).then_inc(rstd_ready, 1)

            def turned(c, first=False):
                for i in range(2):
                    A_wait(c - 1, "xt", i)
                    if i == 0 and not first:
                        act.wait_ge(xnT_stored, c * 16)
                    nc.scalar.activation(xnT[:, :, 2 * i:2 * i + 2, :].rearrange("p k b t -> p b k t"),
                                         a_bank("xt", i)[:, :].rearrange("p (b k t) -> p b k t", b=2, k=2),
                                         ACT.Copy).then_inc(a_done, 1)

            def square(c, b):
                act.wait_ge(d_done, done(c, "yT", b))
                nc.scalar.activation(y2[:, b % 2, :, :], yg[:, b % 2, :, :], ACT.Square).then_inc(y2_ready, 1)

            def rms(c, b):
                q = b % 2
                A_wait(c, "ss", b)
                nc.scalar.activation(lss[:, q:q + 1], a_bank("ss", b)[:, 0:1], ACT.Ln, scale=1.0 / INNER,
                                     bias=eps[:, 1:2]).then_inc(a_done, 1)
                act.wait_ge(a_done, adone(c, "ss", b))
                nc.scalar.activation(rss[:, q:q + 1], lss[:, q:q + 1], ACT.Exp, scale=-0.5).then_inc(rss_ready, 1)

            def body(c, order, first, last):
                for stage, b in order:
                    if stage == "T4" and b == 2 and order is not TAIL:
                        act.wait_ge(dtw_ready, c + 1)
                        nc.scalar.activation(dtl[:, :, :], dtw[:, :, :], ACT.Ln).then_inc(dtl_ready, 1)
                        if not last:
                            norm_log(c + 1)
                    if stage == "xbc" and b == 3 and not last:
                        norm_scale(c + 1)
                    if stage == "z" and b == 0:
                        if first:
                            act.wait_ge(d_done, done(c, "yT", 3))
                        else:
                            square(c, 3)
                    if first and (stage, b) == ("E", 0):
                        act.wait_ge(loaded_late, 16 * N_LATE)
                        nc.scalar.activation(sums[:, :, :].rearrange("p s (b h) -> p s b h", b=2), E[:, :, 0:2, :], ACT.Copy).then_inc(setup, 1)
                    if absent(c, order, first, stage, b) or (stage == "xt" and last):
                        skip(act, a_done, A, NA + PRE_A, a_jobs(stage, b), c)
                        continue
                    if stage == "xbc":
                        A_wait(c, "xbc", b)
                        if b == 0:
                            act.wait_ge(hist, c + 1)
                        nc.scalar.activation(xin[:, b, :, 3:3 + P], a_bank("xbc", b)[:, :].rearrange("p (b t) -> p b t", b=NB),
                                             ACT.Identity, bias=b_xbc[:, b:b + 1]).then_inc(a_done, 1)
                        if b == 1:
                            act.wait_ge(dt_in, c + 1)
                            nc.scalar.activation(dtu[:, :, :], dtr[:, :, :], ACT.Exp).then_inc(dtu_ready, 1)
                    if stage == "z" and b == 0:
                        act.wait_ge(adt_ready, c + 1)
                        nc.scalar.activation(adt_hi[:, :, :], adt[:, :, :], ACT.Copy).then_inc(adt_cut, 1)
                    if stage == "z":
                        A_wait(c, "z", b)
                        nc.scalar.activation(zs[:, b, :, :].rearrange("p b t -> p (b t)"), a_bank("z", b)[:, :], ACT.Silu,
                                             bias=b_z[:, b:b + 1]).then_inc(a_done, 1)
                    if stage == "E":
                        A_wait(c, "E", b)
                        nc.scalar.activation(E[:, 2 * b:2 * b + 2, :, :].rearrange("p s b h -> p (s b h)"), a_bank("E", b)[:, :],
                                             ACT.Exp).then_inc(a_done, 1)
                        if b == 7:
                            for g in range(6):
                                act.wait_ge(conv_ready, c * 6 + g + 1)
                                nc.scalar.activation(xc[:, g, :, :], xc[:, g, :, :], ACT.Silu).then_inc(xc_ready, 1)
                    if stage == "gu":
                        A_wait(c, "g", b)
                        nc.scalar.activation(hs[:, b, :, :].rearrange("p b t -> p (b t)"), a_bank("g", b)[:, :],
                                             ACT.Silu).then_inc(a_done, 1)
                    if stage == "T1":
                        A_wait(c, "btok", b)
                        nc.scalar.activation(Btok[:, b % 2, :], a_bank("btok", b)[:, 0:P], ACT.Copy).then_inc(a_done, 1)
                    if stage == "T3" and b != 3:
                        square(c, b)
                    if stage == "T4":
                        rms(c, b)
                    if stage == "xt":
                        turned(c + 1)

            act.sem_inc(a_done, NA)
            act.wait_ge(zeroed, 5)
            norm_log(0)
            norm_scale(0)
            turned(0, True)
            act.wait_ge(loaded, 16 * N_LOAD)
            nc.scalar.activation(a_exp[:, :], a_exp[:, :], ACT.Exp).then_inc(setup, 1)
            skip(act, a_done, A, NA + PRE_A, A[A.index(("xt", 1)) + 1:], -1)
            steps(act, body)

        @block.tensor
        def _(pe):
            def A_open(c, *job):
                pe.wait_ge(a_done, c * PA + credit(A, NA, job) + PRE_A)

            def D_open(c, *job):
                pe.wait_ge(d_done, c * PD + credit(DJ, ND, job))

            def turn(c, first=False):
                pe.wait_ge(xn_ready, c * NB + NB)
                for i in range(2):
                    if not first:
                        A_open(c - 1, "xt", i)
                    for b in range(2):
                        for k in range(2):
                            o = (b * 2 + k) * P
                            ins = nc.tensor.transpose(a_bank("xt", i)[:, o:o + P], xn[:, 2 * i + b, k * P:(k + 1) * P], ident[:, :])
                    ins.then_inc(a_full, 1)

            def project(dst, w, col, full):
                for k in range(2):
                    ins = nc.tensor.matmul(dst[:, :], w[:, k, col:col + P], xnT[:, k, :, :].rearrange("p b t -> p (b t)"),
                                           start=(k == 0), stop=(k == 1))
                ins.then_inc(full, 1)

            def body(c, order, first, last):
                for stage, b in order:
                    own = c - 1 if (stage, b) in LATE else c
                    q, m = b % 2, own * NB + b
                    if absent(c, order, first, stage, b) or (stage == "xt" and last):
                        skip(pe, a_full, A, PRE_A, a_jobs(stage, b), c)
                        skip(pe, d_full, DJ, 0, d_jobs(stage, b), c)
                        continue
                    if stage == "dt":
                        pe.wait_ge(a_done, adone(c - 1, "xt", 1))
                        D_open(c, "dt", 0)
                        for i in range(NB):
                            for k in range(2):
                                ins = nc.tensor.matmul(d_bank("dt", 0)[:, i * HEADS:(i + 1) * HEADS], xnT[:, k, i, :],
                                                       w_in[:, k, D_PROJ - HEADS:D_PROJ], start=(k == 0), stop=(k == 1))
                        ins.then_inc(d_full, 1)
                    if stage == "xbc":
                        A_open(c, "xbc", b)
                        project(a_bank("xbc", b), w_in, INNER + b * P, a_full)
                    if stage == "z":
                        A_open(c, "z", b)
                        project(a_bank("z", b), w_in, b * P, a_full)
                    if stage == "gu":
                        pe.wait_ge(loaded_late, 16 * N_LATE)
                        A_open(c, "g", b)
                        project(a_bank("g", b), s_gate, b * P, a_full)
                        D_open(c, "u", b)
                        project(d_bank("u", b), s_up, b * P, d_full)
                    if stage == "E":
                        if b == 0:
                            pe.wait_ge(adt_done, c + 1)
                            pe.wait_ge(setup, 2)
                        A_open(c, "E", b)
                        for s in range(2):
                            for part in (adt_hi, adt_lo):
                                ins = nc.tensor.matmul(a_bank("E", b)[:, s * 256:(s + 1) * 256], sums[:, 2 * b + s, :],
                                                       part[:, :, :].rearrange("p b h -> p (b h)"), start=(part is adt_hi), stop=(part is adt_lo))
                        ins.then_inc(a_full, 1)
                    if stage == "T1":
                        pe.wait_ge(xc_ready, c * 6 + 6)
                        D_open(c, "xtok", b)
                        for g in range(4):
                            ins = nc.tensor.transpose(d_bank("xtok", b)[:, g * P:(g + 1) * P], xc[:, g, b, :], ident[:, :])
                        ins.then_inc(d_full, 1)
                        A_open(c, "btok", b)
                        nc.tensor.transpose(a_bank("btok", b)[:, 0:P], xc[:, 4, b, :], ident[:, :]).then_inc(a_full, 1)
                        D_open(c, "G", b)
                        nc.tensor.matmul(d_bank("G", b)[:, 0:P], xc[:, 4, b, :], xc[:, 5, b, :], start=True, stop=True).then_inc(d_full, 1)
                    if stage == "T2":
                        pe.wait_ge(Gm_ready, m + 1)
                        pe.wait_ge(XpD_ready, m + 1)
                        pe.wait_ge(XpP_ready, m + 1)
                        for k in SEQ:
                            D_open(c, "L", b, k)
                            if k == "off":
                                nc.tensor.matmul(d_bank("L", b, k)[:, :], xc[:, 5, b, :], S[:, b, :], start=True, stop=True).then_inc(d_full, 1)
                            else:
                                nc.tensor.matmul(d_bank("L", b, k)[:, :], Gm[:, q, k, :], Xp[:, q, k, :], start=True, stop=True).then_inc(d_full, 1)
                        pe.wait_ge(a_done, adone(c, "btok", b))
                        D_open(c, "snew", b)
                        nc.tensor.matmul(d_bank("snew", b)[:, :], Btok[:, q, :], Xp[:, q, 7, :], start=True, stop=True).then_inc(d_full, 1)
                    if stage == "T3":
                        pe.wait_ge(Y_ready, m + 1)
                        D_open(c, "yT", b)
                        for g in range(4):
                            ins = nc.tensor.transpose(d_bank("yT", b)[:, g * P:(g + 1) * P], Yd[:, q, g * P:(g + 1) * P], ident[:, :])
                        ins.then_inc(d_full, 1)
                    if stage == "T4":
                        pe.wait_ge(y2_ready, m + 1)
                        A_open(c, "ss", b)
                        for g in range(4):
                            ins = nc.tensor.matmul(a_bank("ss", b)[:, 0:2], y2[:, q, g, :], ones[:, :], start=(g == 0), stop=(g == 3))
                        ins.then_inc(a_full, 1)
                        pe.wait_ge(w_out_ready, 4)
                        pe.wait_ge(d_done, done(own, "u", 3))
                        D_open(c, "out", b)
                        for g in range(4):
                            nc.tensor.matmul(d_bank("out", b)[:, 0:D], yg[:, q, g, :], w_out[:, g, :], start=(g == 0), stop=(g == 3))
                        for g in range(4):
                            ins = nc.tensor.matmul(d_bank("out", b)[:, D:2 * D], hs[:, g, b, :], s_down[:, g, :], start=(g == 0), stop=(g == 3))
                        ins.then_inc(d_full, 1)
                    if stage == "xt":
                        turn(c + 1)

            pe.wait_ge(ident_ready, 16)
            turn(0, True)
            skip(pe, a_full, A, PRE_A, A[A.index(("xt", 1)) + 1:], -1)
            pe.wait_ge(loaded, 16 * N_LOAD)
            pe.wait_ge(zeroed, 5)
            steps(pe, body)

        @block.vector
        def _(dve):
            n = [0]
            v = nc.vector

            def D_wait(c, *job):
                dve.wait_ge(d_full, c * PD + DJ.index(job) + 1)

            def norm_stats(c):
                dve.wait_ge(x_ready, c * 16 + 16)
                for b in range(NB):
                    ins = v.bn_stats(stats[:, b, :], x_ln[:, b, :])
                ins.then_inc(stats_ready, 1)
                dve.wait_ge(stats_ready, c + 1)
                dve.sem_inc(carry, 1)
                for b in range(NB):
                    v.bn_aggr(mv[:, b, :], stats[:, b, :]).then_inc(mv_ready, 1)

            def norm(c, first=False):
                dve.wait_ge(rstd_ready, c + 1)
                if not first:
                    dve.wait_ge(xn_stored, c * 16)
                for b in range(NB):
                    v.tensor_scalar(xn[:, b, :], x_ln[:, b, :], mv[:, b, 0:1], rstd[:, b:b + 1], ALU.subtract,
                                    ALU.mult).then_inc(xn_ready, 1)
                dve.wait_ge(xn_ready, c * NB + NB)
                dve.sem_inc(x_used, 1)

            def conv(c, g, link):
                dve.wait_ge(a_done, adone(c, "xbc", g))
                link(v.tensor_scalar(xc[:, g, :, :], xin[:, g, :, 0:P], cw[:, g, 0:1], cb[:, g:g + 1], ALU.mult, ALU.add))
                for t in range(1, 4):
                    ins = v.scalar_tensor_tensor(out=xc[:, g, :, :], in0=xin[:, g, :, t:t + P], scalar=cw[:, g, t:t + 1],
                                                 in1=xc[:, g, :, :], op0=ALU.mult, op1=ALU.add)
                    if t < 3:
                        link(ins)
                    else:
                        ins.then_inc(conv_ready, 1)

            def body(c, order, first, last):
                n[0] = 0

                def link(ins):
                    n[0] += 1
                    ins.then_inc(dve_step, 1)
                    dve.wait_ge(dve_step, c * DVE_STEPS + n[0] + 2)

                def D_done(ins, *job):
                    ins.then_inc(d_done, 1)
                    dve.wait_ge(d_done, done(c, *job))

                for stage, b in order:
                    own = c - 1 if (stage, b) in LATE else c
                    q, m = b % 2, own * NB + b
                    if absent(c, order, first, stage, b):
                        skip(dve, d_done, DJ, ND, d_jobs(stage, b), c)
                    elif stage == "dt":
                        D_wait(c, "dt", 0)
                        ins = v.tensor_tensor(dtr[:, :, :], d_bank("dt", 0)[:, 0:NB * HEADS].rearrange("p (b h) -> p b h", b=NB),
                                              dt_add[:, :].unsqueeze(1).to_broadcast([P, NB, HEADS]), ALU.add)
                        D_done(ins, "dt", 0)
                        v.tensor_scalar(dtr[:, :, :], dtr[:, :, :], 30.0, None, ALU.min).then_inc(dt_in, 1)
                    elif stage == "xbc":
                        if b == 1:
                            dve.wait_ge(dtu_ready, c + 1)
                            v.tensor_scalar(dtw[:, :, :], dtu[:, :, :], 1.0, None, ALU.add).then_inc(dtw_ready, 1)
                            if not last:
                                norm_stats(c + 1)
                        if b == 2:
                            dve.wait_ge(dtw_ready, c + 1)
                            link(v.tensor_scalar(dtd[:, :, :], dtw[:, :, :], -1.0, 1e-30, ALU.add, ALU.max))
                            link(v.reciprocal(dtd[:, :, :], dtd[:, :, :]))
                            link(v.tensor_tensor(dtd[:, :, :], dtd[:, :, :], dtu[:, :, :], ALU.mult))
                        if b == 3:
                            dve.wait_ge(dtl_ready, c + 1)
                            link(v.tensor_tensor(dtc[:, :, :], dtl[:, :, :], dtd[:, :, :], ALU.mult))
                            link(v.tensor_scalar(dtc[:, :, :], dtc[:, :, :], 0.001, 0.1, ALU.max, ALU.min))
                            v.scalar_tensor_tensor(out=adt[:, :, :], in0=dtc[:, :, :], scalar=-1.0,
                                                   in1=a_exp[:, :].unsqueeze(1).to_broadcast([P, NB, HEADS]), op0=ALU.mult,
                                                   op1=ALU.mult).then_inc(adt_ready, 1)
                        if b == 5:
                            link(v.reciprocal(d_over[:, :, :], dtc[:, :, :]))
                            link(v.tensor_tensor(d_over[:, :, :], d_over[:, :, :], d_par[:, :].unsqueeze(1).to_broadcast([P, NB, HEADS]), ALU.mult))
                        conv(c, b, link)
                        if b == 5:
                            dve.wait_ge(conv_ready, c * 6 + 6)
                            v.tensor_copy(xin[:, :, :, 0:3], xin[:, :, :, P:P + 3]).then_inc(hist, 1)
                            dve.wait_ge(adt_cut, c + 1)
                            v.tensor_tensor(adt_lo[:, :, :], adt[:, :, :], adt_hi[:, :, :].bitcast(F32), ALU.subtract).then_inc(adt_done, 1)
                    elif stage == "E":
                        if b == 0 and not last:
                            norm(c + 1)
                        if b == 7 and first:
                            dve.wait_ge(loaded_late, 16 * N_LATE)
                            for g in range(4):
                                v.tensor_scalar(w_out[:, g, :], w_out[:, g, :], normw[:, g:g + 1], None, ALU.mult).then_inc(w_out_ready, 1)
                    elif stage == "gu":
                        D_wait(c, "u", b)
                        dve.wait_ge(a_done, adone(c, "g", b))
                        v.tensor_tensor(hs[:, b, :, :].rearrange("p b t -> p (b t)"), hs[:, b, :, :].rearrange("p b t -> p (b t)"),
                                        d_bank("u", b)[:, :], ALU.mult).then_inc(d_done, 1)
                    elif stage == "T1":
                        D_wait(c, "xtok", b)
                        ins = v.tensor_tensor(h1(Xd[:, q, :]), h1(d_bank("xtok", b)[:, :]),
                                              dtc[:, b, :].unsqueeze(2).to_broadcast([P, HEADS, 8]), ALU.mult)
                        D_done(ins, "xtok", b)
                        dve.wait_ge(a_done, adone(c, "E", 7))
                        v.tensor_tensor(h8(Xp[:, q, 0:PRE_D, :], PRE_D), h8b(Xd[:, q, :], PRE_D),
                                        E[:, 0:PRE_D, b, :].unsqueeze(3).to_broadcast([P, PRE_D, HEADS, 8]),
                                        ALU.mult).then_inc(XpD_ready, 1)
                        D_wait(c, "G", b)
                        v.tensor_tensor(Gm[:, q, :, :], d_bank("G", b)[:, 0:P].unsqueeze(1).to_broadcast([P, LEVELS, P]),
                                        pairs[:, :, :], ALU.mult).then_inc(Gm_ready, 1)
                        D_done(v.tensor_tensor_reduce(gj[:, :], d_bank("G", b)[:, 0:P], ident[:, :], 1.0, 0.0, ALU.mult, ALU.add,
                                                      gd[:, q:q + 1]), "G", b)
                        v.tensor_scalar(coef[:, q, :], d_over[:, b, :], gd[:, q:q + 1], None, ALU.add).then_inc(coef_ready, 1)
                    elif stage == "T2":
                        for k in SEQ:
                            D_wait(c, "L", b, k)
                            src = d_bank("L", b, k)
                            if k == 0:
                                D_done(v.tensor_tensor(Yd[:, q, :], Yd[:, q, :], src[:, :], ALU.add), "L", b, k)
                                continue
                            e = SUM_START if k == "off" else SUM_POST + k - 1
                            post = E[:, e, b, :].unsqueeze(2).to_broadcast([P, HEADS, 8])
                            if k in POOL_ADDS:
                                j = POOL_ADDS.index(k)
                                dve.wait_ge(T_used, m * 4 + j + 1)
                                v.tensor_tensor(h1(T[:, j % 2, :]), h1(src[:, :]), post, ALU.mult).then_inc(d_done, 1)
                            elif k == 2:
                                D_done(v.tensor_tensor(h1(Yd[:, q, :]), h1(src[:, :]), post, ALU.mult), "L", b, k)
                            else:
                                D_done(v.tensor_tensor(h1(T[:, 2, :]), h1(src[:, :]), post, ALU.mult), "L", b, k)
                                link(v.tensor_tensor(Yd[:, q, :], Yd[:, q, :], T[:, 2, :], ALU.add))
                        D_wait(c, "snew", b)
                        dve.wait_ge(S_decayed, m + 1)
                        v.tensor_tensor(S[:, b, :], S[:, b, :], d_bank("snew", b)[:, :], ALU.add).then_inc(d_done, 1)
                        dve.wait_ge(T_used, m * 4 + 4 + 2)
                        v.tensor_tensor(Yd[:, q, :], Yd[:, q, :], Yp[:, q, :], ALU.add).then_inc(Y_ready, 1)
                    elif stage == "T3":
                        D_wait(c, "yT", b)
                        dve.wait_ge(a_done, adone(own, "z", 3))
                        v.tensor_tensor(yg[:, q, :, :], d_bank("yT", b)[:, :].rearrange("p (g t) -> p g t", g=4),
                                        zs[:, :, b, :], ALU.mult).then_inc(d_done, 1)
                    elif stage == "T4":
                        D_wait(c, "out", b)
                        dve.wait_ge(rss_ready, m + 1)
                        dve.wait_ge(xb_ready, own + 1)
                        dve.wait_ge(stored[q], own * 32 + b // 2 * 16 + 16)
                        v.scalar_tensor_tensor(out=res[:, q, :], in0=d_bank("out", b)[:, 0:D], scalar=rss[:, q:q + 1],
                                               in1=x_res[:, b, :], op0=ALU.mult, op1=ALU.add).then_inc(res_half, 1)
                        dve.wait_ge(res_half, m + 1)
                        v.tensor_tensor(res[:, q, :], res[:, q, :], d_bank("out", b)[:, D:2 * D], ALU.add).then_inc(d_done, 1)
                    if stage == "T4" and b == 3:
                        dve.wait_ge(d_done, done(c, "out", 3))
                        dve.sem_inc(xres_used, 1)
                if order is ORDER:
                    seen["dve"] = n[0]

            dve.sem_inc(d_done, ND)
            dve.sem_inc(T_used, 2)
            dve.sem_inc(hist, 1)
            dve.sem_inc(stored[0], 16)
            dve.sem_inc(stored[1], 16)
            norm_stats(0)
            norm(0, True)
            dve.wait_ge(loaded, 16 * N_LOAD)
            dve.wait_ge(zeroed, 5)
            v.tensor_tensor(dt_add[:, :], dt_add[:, :], dt_add2[:, :], ALU.add).then_inc(dve_step, 1)
            v.memset(lss[:, :], 0.0).then_inc(dve_step, 1)
            dve.wait_ge(dve_step, 2)
            dve.wait_ge(setup, 1)
            steps(dve, body)
        assert (seen["dve"], seen["pool"]) == (DVE_STEPS, POOL_STEPS), seen
def router_phase(nc, io, scratch, keep):
    with ExitStack() as ctx:
        def sb(name, shape, dt=F32):
            return ctx.enter_context(nc.sbuf_tensor("r_" + name, shape, dt))

        def sem(name):
            return ctx.enter_context(nc.semaphore("r_" + name))

        wr = sb("wr", [P, 2, EXPERTS])
        rb = sb("rb", [P, EXPERTS])
        iota = sb("iota", [P, EXPERTS])
        before = sb("before", [P, P])
        ones = sb("ones", [P, P])
        xT = sb("xT", [P, NC, 2, P])
        xr = sb("xr", [P, 2, NC, D])
        sc = sb("sc", [P, NC, EXPERTS])
        mx = sb("mx", [P, NC])
        t8 = sb("t8", [P, NC, 8])
        i8 = sb("i8", [P, NC, 8], U32)
        idx = sb("idx", [P, NC, K0])
        hot = sb("hot", [P, NC, K0, EXPERTS])
        prod = sb("prod", [P, NC, K0, EXPERTS])
        took = sb("took", [P, NC, EXPERTS])
        earlier = sb("earlier", [P, NC + 1, EXPERTS])
        place = sb("place", [P, NC, K0])
        full = sb("full", [P, NC, K0])
        slot = sb("slot", [P, NC, K0])
        slot_f = sb("slot_f", [P, NC, K0])
        to = sb("to", [P, 2, NC, K0], U32)
        ps_l = ctx.enter_context(nc.psum_tensor("r_ps_l", [P, 512], F32))
        ps_p = ctx.enter_context(nc.psum_tensor("r_ps_p", [P, 512], F32))
        loaded, zeroed, weights = sem("loaded"), sem("zeroed"), sem("weights")
        ready = [sem("ready0"), sem("ready1")]
        scattered = [sem("scattered0"), sem("scattered1")]
        logits, exped, counted, to_ready = sem("logits"), sem("exped"), sem("counted"), sem("to_ready")
        shifted, took_ready, step, carry = sem("shifted"), sem("took_ready"), sem("step"), sem("carry")
        SCATTERS = NC * K0
        block = ctx.enter_context(nc.Block())
        xT_t = scratch["xnT"].rearrange("c p (k b t) -> b k p c t", k=2, b=NB)
        xr_t = scratch["xn"].rearrange("(b c t) d -> b t c d", c=NC, t=P)
        STEPS = ROUTER_STEPS
        seen = {}

        @block.sync
        def _(sp):
            sp.dma_start(wr[:, :, :], io["Wr"].rearrange("(k p) e -> p k e", p=P)).then_inc(loaded, 16)
            sp.dma_start(rb[:, :], io["r_bias"].rearrange("(a n) -> a n", a=1).to_broadcast([P, EXPERTS])).then_inc(loaded, 16)
            sp.dma_start(before[:, :], io["before"]).then_inc(loaded, 16)
            for b in range(NB):
                q = b % 2
                if b:
                    sp.wait_ge(logits, b)
                for k in range(2):
                    sp.dma_start(xT[:, :, k, :], xT_t[b, k]).then_inc(ready[q], 16)
                if b >= 2:
                    sp.wait_ge(scattered[q], 16 * SCATTERS)
                sp.dma_start(xr[:, q, :, :], xr_t[b]).then_inc(ready[q], 16)

        @block.gpsimd
        def _(pool):
            nc.gpsimd.iota(iota[:, :], [[1, EXPERTS]], base=0, channel_multiplier=0,
                           allow_small_or_imprecise_dtypes=True).then_inc(zeroed, 1)
            nc.gpsimd.memset(ones[:, :], 1.0).then_inc(zeroed, 1)
            nc.gpsimd.memset(earlier[:, :, :], 0.0).then_inc(zeroed, 1)
            with pool.Fori(0, NB // 2) as i:
                for q in range(2):
                    pool.wait_ge(to_ready, i * 2 + q + 1)
                    pool.sem_inc(carry, 1)
                    for c in range(NC):
                        for k in range(K0):
                            nc.gpsimd.indirect_dma_start(
                                out=scratch["xb"], out_offset=bass.IndirectOffsetOnAxis(ap=to[:, q, c, k:k + 1], axis=0),
                                in_=xr[:, q, c, :], in_offset=None, bounds_check=EXPERTS * CAP - 1, oob_is_err=False,
                            ).then_inc(scattered[q], 16)
            for q in range(2):
                pool.wait_ge(scattered[q], 16 * SCATTERS * NB // 2)

        @block.scalar
        def _(act):
            act.wait_ge(logits, 1)
            for g in range(0, EXPERTS // 2, 4):
                act.dma_start(keep["w0"][:, g:g + 4, :], io["w0"][g:g + 4].rearrange("j p n -> p j n")).then_inc(weights, 16)
            with act.Fori(0, NB) as b:
                act.wait_ge(shifted, b + 1)
                nc.scalar.activation(sc[:, :, :], sc[:, :, :], ACT.Exp).then_inc(exped, 1)
            act.wait_ge(weights, 16 * EXPERTS // 8)

        @block.tensor
        def _(pe):
            pe.wait_ge(loaded, 48)
            pe.wait_ge(zeroed, 3)
            with pe.Fori(0, NB // 2) as i:
                for q in range(2):
                    pe.wait_ge(ready[q], i * 48 + 48)
                    for c in range(NC):
                        for k in range(2):
                            ins = nc.tensor.matmul(ps_l[:, c * EXPERTS:(c + 1) * EXPERTS], xT[:, c, k, :], wr[:, k, :],
                                                   start=(k == 0), stop=(k == 1))
                    ins.then_inc(logits, 1)
                    pe.wait_ge(took_ready, i * 2 + q + 1)
                    nc.tensor.matmul(ps_p[:, :], before[:, :], took[:, :, :].rearrange("p c e -> p (c e)"), start=True, stop=False)
                    nc.tensor.matmul(ps_p[:, :], ones[:, :], earlier[:, 0:NC, :].rearrange("p c e -> p (c e)"),
                                     start=False, stop=True).then_inc(counted, 1)

        @block.vector
        def _(dve):
            n = [0]
            v = nc.vector

            def wide(ap):
                return ap.unsqueeze(2).to_broadcast([P, NC, EXPERTS])

            dve.wait_ge(loaded, 48)
            dve.wait_ge(zeroed, 3)
            def body(b, q):
                n[0] = 0

                def link(ins):
                    n[0] += 1
                    ins.then_inc(step, 1)
                    dve.wait_ge(step, b * STEPS + n[0])

                dve.wait_ge(logits, b + 1)
                link(v.tensor_tensor(sc[:, :, :], ps_l[:, :].rearrange("p (c e) -> p c e", c=NC),
                                     rb[:, :].unsqueeze(1).to_broadcast([P, NC, EXPERTS]), ALU.add))
                link(v.tensor_reduce(mx[:, :], sc[:, :, :], AX.X, ALU.max))
                v.tensor_tensor(sc[:, :, :], sc[:, :, :], wide(mx[:, :]), ALU.subtract).then_inc(shifted, 1)
                dve.wait_ge(exped, b + 1)
                link(v.tensor_reduce(mx[:, :], sc[:, :, :], AX.X, ALU.add))
                link(v.reciprocal(mx[:, :], mx[:, :]))
                link(v.tensor_tensor(sc[:, :, :], sc[:, :, :], wide(mx[:, :]), ALU.mult))
                dve.sem_inc(carry, 1)
                for c in range(NC):
                    ins = v.max(t8[:, c, :], sc[:, c, :])
                link(ins)
                dve.sem_inc(carry, 1)
                for c in range(NC):
                    ins = v.max_index(i8[:, c, :], t8[:, c, :], sc[:, c, :])
                link(ins)
                link(v.tensor_copy(idx[:, :, :], i8[:, :, 0:K0]))
                link(v.tensor_reduce(mx[:, :], t8[:, :, 0:K0], AX.X, ALU.add))
                link(v.reciprocal(mx[:, :], mx[:, :]))
                link(v.tensor_tensor(t8[:, :, 0:K0], t8[:, :, 0:K0], mx[:, :].unsqueeze(2).to_broadcast([P, NC, K0]), ALU.mult))
                link(v.tensor_tensor(hot[:, :, :, :], iota[:, :].unsqueeze(1).unsqueeze(1).to_broadcast([P, NC, K0, EXPERTS]),
                                     idx[:, :, :].unsqueeze(3).to_broadcast([P, NC, K0, EXPERTS]), ALU.is_equal))
                link(v.tensor_reduce(took[:, :, :], hot[:, :, :, :].rearrange("p c k e -> p c e k"), AX.X, ALU.add))
                for c in range(NC):
                    ins = v.tensor_tensor(earlier[:, c + 1, :], earlier[:, c, :], took[:, c, :], ALU.add)
                    if c < NC - 1:
                        link(ins)
                ins.then_inc(took_ready, 1)
                dve.wait_ge(counted, b + 1)
                link(v.tensor_tensor(prod[:, :, :, :], hot[:, :, :, :],
                                     ps_p[:, :].rearrange("p (c e) -> p c e", c=NC).unsqueeze(2).to_broadcast([P, NC, K0, EXPERTS]),
                                     ALU.mult))
                link(v.tensor_copy(earlier[:, 0, :], earlier[:, NC, :]))
                link(v.tensor_reduce(place[:, :, :], prod[:, :, :, :], AX.X, ALU.add))
                link(v.tensor_scalar(full[:, :, :], place[:, :, :], float(CAP), None, ALU.is_lt))
                tile = keep["w_all"][:, bass.ds(b * NC, NC), :]
                link(v.tensor_tensor(tile, t8[:, :, 0:K0], full[:, :, :], ALU.mult))
                link(v.tensor_scalar(full[:, :, :], place[:, :, :], float(CAP), 1e6, ALU.is_ge, ALU.mult))
                link(v.scalar_tensor_tensor(out=slot[:, :, :], in0=idx[:, :, :], scalar=float(CAP), in1=place[:, :, :],
                                            op0=ALU.mult, op1=ALU.add))
                link(v.tensor_tensor(slot[:, :, :], slot[:, :, :], full[:, :, :], ALU.add))
                v.tensor_copy(to[:, q, :, :], slot[:, :, :]).then_inc(to_ready, 1)
                link(v.tensor_scalar(place[:, :, :], place[:, :, :], float(CAP - 1), None, ALU.min))
                link(v.scalar_tensor_tensor(out=slot_f[:, :, :], in0=idx[:, :, :], scalar=float(CAP), in1=place[:, :, :],
                                            op0=ALU.mult, op1=ALU.add))
                link(v.tensor_copy(keep["slot_all"][:, bass.ds(b * NC, NC), :], slot_f[:, :, :]))
                seen["dve"] = n[0]

            with dve.Fori(0, NB // 2) as i:
                for q in range(2):
                    body(i * 2 + q, q)
        assert seen["dve"] == STEPS, seen


def expert_phase(nc, io, scratch, keep):
    with ExitStack() as ctx:
        def sb(name, shape, dt=F32):
            return ctx.enter_context(nc.sbuf_tensor("e_" + name, shape, dt))

        def sem(name):
            return ctx.enter_context(nc.semaphore("e_" + name))

        PAIRS, RING = EXPERTS // 2, 4
        ident = sb("ident", [P, P])
        w_now = sb("w_now", [P, RING, W0])
        xb = sb("xb", [P, RING, D])
        xbT = sb("xbT", [P, RING, 2, P])
        gate = sb("gate", [P, RING, CAP])
        y = sb("y", [P, RING, D])
        ps_x = [ctx.enter_context(nc.psum_tensor(f"e_ps_x{q}", [P, 512], F32)) for q in range(2)]
        ps_h = [ctx.enter_context(nc.psum_tensor(f"e_ps_h{q}", [P, 512], F32)) for q in range(RING)]
        ps_y = [ctx.enter_context(nc.psum_tensor(f"e_ps_y{q}", [P, 512], F32)) for q in range(2)]
        loaded, carry = sem("loaded"), sem("carry")
        ready = [sem(f"ready{q}") for q in range(RING)]
        stored = [sem(f"stored{q}") for q in range(RING)]
        w_ready, turned, xT_ready, gu_ready, silu_ready, h_ready, y_full, y_ready = (
            sem(k) for k in ("w_ready", "turned", "xT_ready", "gu_ready", "silu_ready", "h_ready", "y_full", "y_ready"))
        block = ctx.enter_context(nc.Block())
        xb_t = scratch["xb"].rearrange("(j p) d -> j p d", p=P)
        yb_t = scratch["yb"].rearrange("(j p) d -> j p d", p=P)

        @block.sync
        def _(sp):
            sp.dma_start(ident[:, :], io["ident"]).then_inc(loaded, 16)
            for u in range(RING):
                sp.dma_start(xb[:, u, :], xb_t[u]).then_inc(ready[u], 16)
            with sp.Fori(1, PAIRS // RING) as i:
                for u in range(RING):
                    sp.wait_ge(turned, i * RING + u - RING + 1)
                    sp.dma_start(xb[:, u, :], xb_t[i * RING + u]).then_inc(ready[u], 16)

        @block.scalar
        def _(act):
            def silu(j, u):
                act.wait_ge(gu_ready, j + 1)
                nc.scalar.activation(gate[:, u, :], ps_h[u][:, 0:CAP], ACT.Silu).then_inc(silu_ready, 1)

            def turn(i, last):
                for u in range(RING):
                    k = i * RING + u
                    if not (last and u >= RING - 2):
                        silu(k + 2, (u + 2) % RING)
                    act.wait_ge(stored[u], i * 16 + 16)
                    act.wait_ge(y_full, k + 1)
                    nc.scalar.activation(y[:, u, :], ps_y[u % 2][:, 0:D], ACT.Copy).then_inc(y_ready, 1)
                    act.wait_ge(y_ready, k + 1 + 2)
                    act.dma_start(yb_t[k], y[:, u, :]).then_inc(stored[u], 16)

            for u in range(RING):
                act.sem_inc(stored[u], 16)
            act.sem_inc(y_ready, 2)
            for j in range(2):
                silu(j, j)
            with act.Fori(0, PAIRS // RING - 1) as i:
                turn(i, False)
            turn(PAIRS // RING - 1, True)
            for u in range(RING):
                act.wait_ge(stored[u], 16 * PAIRS // RING + 16)

        @block.tensor
        def _(pe):
            def rows(j, i, u):
                pe.wait_ge(ready[u], i * 16 + 16)
                if not (isinstance(j, int) and j < 2):
                    pe.wait_ge(xT_ready, j - 2 + 1)
                for k in range(2):
                    ins = nc.tensor.transpose(ps_x[u % 2][:, k * P:(k + 1) * P], xb[:, u, k * P:(k + 1) * P], ident[:, :])
                ins.then_inc(turned, 1)

            def hidden(j, u):
                pe.wait_ge(w_ready, j + 1)
                pe.wait_ge(xT_ready, j + 1)
                pe.sem_inc(carry, 1)
                for a in range(2):
                    for e in range(2):
                        for k in range(2):
                            col = ((a * 2 + e) * 2 + k) * HID0
                            ins = nc.tensor.matmul(ps_h[u][e * HID0:(e + 1) * HID0, a * CAP:(a + 1) * CAP], w_now[:, u, col:col + HID0],
                                                   xbT[:, u, k, e * CAP:(e + 1) * CAP], start=(k == 0), stop=(k == 1))
                ins.then_inc(gu_ready, 1)

            def output(k, u):
                pe.wait_ge(h_ready, k + 1)
                pe.wait_ge(y_ready, k - 2 + 1 + 2)
                pe.sem_inc(carry, 1)
                for e in range(2):
                    half = slice(e * HID0, (e + 1) * HID0)
                    ins = nc.tensor.matmul(ps_y[u % 2][half, 0:D], gate[half, u, :], w_now[half, u, 8 * HID0:W0], start=True, stop=True)
                ins.then_inc(y_full, 1)

            def turn(i, last):
                for u in range(RING):
                    k = i * RING + u
                    if not (last and u >= RING - 3):
                        rows(k + 3, i + (u + 3) // RING, (u + 3) % RING)
                    if not (last and u >= RING - 2):
                        hidden(k + 2, (u + 2) % RING)
                    output(k, u)

            pe.wait_ge(loaded, 16)
            for j in range(3):
                rows(j, 0, j)
            for j in range(2):
                hidden(j, j)
            with pe.Fori(0, PAIRS // RING - 1) as i:
                turn(i, False)
            turn(PAIRS // RING - 1, True)

        @block.vector
        def _(dve):
            v = nc.vector

            def copy(j, u):
                dve.wait_ge(turned, j + 1)
                v.tensor_copy(xbT[:, u, :, :].rearrange("p k t -> p (k t)"), ps_x[u % 2][:, 0:2 * P]).then_inc(xT_ready, 1)

            def product(j, u):
                dve.wait_ge(silu_ready, j + 1)
                v.tensor_tensor(gate[:, u, :], gate[:, u, :], ps_h[u][:, CAP:2 * CAP], ALU.mult).then_inc(h_ready, 1)

            def fetch(j, u):
                v.tensor_copy(w_now[:, u, :], keep["w0"][:, j, :]).then_inc(w_ready, 1)

            def turn(i, last):
                for u in range(RING):
                    k = i * RING + u
                    if not (last and u >= RING - 3):
                        copy(k + 3, (u + 3) % RING)
                    if not (last and u >= RING - 2):
                        product(k + 2, (u + 2) % RING)
                    if not last:
                        dve.wait_ge(y_full, k + 1)
                        fetch(k + RING, u)

            for u in range(RING):
                fetch(u, u)
            for j in range(3):
                copy(j, j)
            for j in range(2):
                product(j, j)
            with dve.Fori(0, PAIRS // RING - 1) as i:
                turn(i, False)
            turn(PAIRS // RING - 1, True)

def attention_constants():
    import numpy as np
    half = DH // 2
    freq = 1.0 / 10000.0 ** (np.arange(0, DH, 2, dtype=np.float32) / np.float32(DH))
    ang = (np.arange(SEQ_LEN, dtype=np.float32)[:, None] * freq[None, :].astype(np.float32)).astype(np.float32).astype(np.float64)
    cos, sin = np.cos(ang).T, np.sin(ang).T
    lam = 2.0 ** (-8.0 * np.arange(1, HQ + 1) / HQ)
    i = np.arange(P)
    v_dec = np.exp(lam[None, :] * (i[:, None] + 1 - P // 2))
    q_dec = np.exp(-lam[:, None] * (i[None, :] + 1 - P // 2))
    half_chunk = np.exp(-lam * (P // 2))
    return {
        "cos": np.concatenate([cos, cos]), "sin": np.concatenate([sin, -sin]),
        "mask": (i[:, None] <= i[None, :]), "v_dec": v_dec,
        "q_dec": np.broadcast_to(q_dec.reshape(1, -1), (P, HQ * P)), "half_chunk": np.broadcast_to(half_chunk[None], (P, HQ)),
    }


def attention_phase(nc, io, scratch, keep):
    with ExitStack() as ctx:
        def sb(name, shape, dt=F32):
            return ctx.enter_context(nc.sbuf_tensor("a_" + name, shape, dt))

        def sem(name):
            return ctx.enter_context(nc.semaphore("a_" + name))

        GR = HQ // HKV
        wq = sb("wq", [P, 2, (HQ - CUT_HEADS) * DH])
        N_CUT = (HKV + CUT_HEADS) * DH
        w_hi = sb("w_hi", [P, 2, N_CUT], FR)
        w_lo = sb("w_lo", [P, 2, N_CUT], FR)
        x_hi = sb("x_hi", [P, 2, NB, P], FR)
        x_lo = sb("x_lo", [P, 2, NB, P], FR)
        wv = sb("wv", [P, 2, HKV * DH])
        wo = sb("wo", [P, HQ, D])
        cos = sb("cos", [P, P])
        sin = sb("sin", [P, P])
        sin_swapped = sb("sin_swapped", [P, P])
        mask = sb("mask", [P, P])
        v_dec = sb("v_dec", [P, HQ])
        q_dec = sb("q_dec", [P, HQ, P])
        half_chunk = sb("half_chunk", [P, HQ])
        ident = sb("ident", [P, P])
        eps = sb("eps", [P, 1])
        x1 = sb("x1", [P, NB, D])
        x1r = sb("x1r", [P, NB, D])
        slot_now = sb("slot_now", [P, NB, K0], U32)
        w_now = sb("w_now", [P, NB, K0])
        gath = [sb(f"gath{q}", [P, K0, D]) for q in range(2)]
        stats = sb("stats", [P, NB, 6])
        mv = sb("mv", [P, NB, 2])
        lnv = sb("lnv", [P, NB])
        rstd = sb("rstd", [P, NB])
        xn = sb("xn", [P, NB, D])
        xnT = sb("xnT", [P, 2, NB, P])
        qT = sb("qT", [P, HQ, NB, P])
        kT = sb("kT", [P, HKV, NB, P])
        rot = sb("rot", [P, 3, NB, P])
        vd = sb("vd", [P, 2, HQ, DH])
        ktok = sb("ktok", [P, 2, HKV, DH])
        Sm = sb("Sm", [P, 2, GR, P])
        oT = sb("oT", [P, HQ, P])
        kv = sb("kv", [P, NB, HQ, DH])
        res = sb("res", [P, 2, D])
        NA, ND = 2, 6
        psA = [ctx.enter_context(nc.psum_tensor(f"a_psA{i}", [P, 512], F32)) for i in range(NA)]
        psD = [ctx.enter_context(nc.psum_tensor(f"a_psD{i}", [P, 512], F32)) for i in range(ND)]

        def rope_of(i):
            g, r = divmod(i, GR + 1)
            return ("k", g) if r == 0 else ("q", GR * g + r - 1)

        SWAPS = [i for i in range(HKV + HQ) if i % 4 == 3]

        def tile_order():
            for b in range(NB):
                yield ("S", b, 0)
                yield ("S", b, 1)
                if b:
                    yield ("wo", b - 1, 0)
                for g in range(HKV):
                    yield ("o", b, g)
                    yield ("kv", b, g)
                    if g + 2 < HKV:
                        yield ("S", b, g + 2)
                yield ("end", b, 0)
            yield ("wo", NB - 1, 0)

        PREP_AT = 2
        A = [("v", b) for b in range(2)] + [("ktok", 0)]
        A += [x for b in range(1, NB) for x in ([("v", b + 1)] if b + 1 < NB else []) + [("ktok", b)]] + [("xt", 0), ("xt", 1)]
        DJ = [("rope", i) for i in range(HKV + HQ)] + [t for t in tile_order() if t[0] != "end"]
        PA, PD = len(A), len(DJ)
        PRE_A = 2

        def a_bank(*job):
            return psA[A.index(job) % NA]

        def d_bank(*job):
            return psD[DJ.index(job) % ND]

        def done(c, *job):
            return c * PD + DJ.index(job) + 1 + ND

        def adone(c, *job):
            return c * PA + A.index(job) + 1 + NA + PRE_A

        def credit(jobs, n, job):
            j = jobs.index(job)
            before = j - n if j >= n else max(i for i in range(len(jobs)) if i % n == j) - len(jobs)
            return before + 1 + n

        a_full, a_done, d_full, d_done = sem("a_full"), sem("a_done"), sem("d_full"), sem("d_done")
        loaded, setup, x_ready, x1r_ready, x_stored, xnT_stored = (
            sem(k) for k in ("loaded", "setup", "x_ready", "x1r_ready", "x_stored", "xnT_stored"))
        now_ready, stats_ready, mv_ready, lnv_ready, rstd_ready, xn_ready = (
            sem(k) for k in ("now_ready", "stats_ready", "mv_ready", "lnv_ready", "rstd_ready", "xn_ready"))
        gathered = [sem("gathered0"), sem("gathered1")]
        stored = [sem("stored0"), sem("stored1")]
        gath_used, added, roped, decayed, carry, half_decayed = (
            sem(k) for k in ("gath_used", "added", "roped", "decayed", "carry", "half_decayed"))
        swapped, swap_sined = sem("swapped"), sem("swap_sined")
        angles_ready, w_cut, w_done, x_done = sem("angles_ready"), sem("w_cut"), sem("w_done"), sem("x_done")
        ident_ready, loaded_late = sem("ident_ready"), sem("loaded_late")
        first_gathered = [sem(f"first_gathered{b}") for b in range(NB)]
        first_gath = vd[:, :, :, :].rearrange("p q h e -> p (q h e)")
        block = ctx.enter_context(nc.Block())
        acc_t = scratch["acc0"].rearrange("(b c t) d -> c t b d", c=NC, t=P)
        x1_t = scratch["x1"].rearrange("(b c t) d -> c t b d", c=NC, t=P)
        acc1_t = scratch["acc1"].rearrange("(b c t) d -> c b t d", c=NC, t=P)
        slot_t = keep["slot_all"][:, :, :].rearrange("p (b c) k -> p c b k", b=NB)
        w_t = keep["w_all"][:, :, :].rearrange("p (b c) k -> p c b k", b=NB)
        N_LOAD, N_LATE = 5, 4
        cos_t = io["cos"].rearrange("p (c t) -> c p t", c=NC)
        sin_t = io["sin"].rearrange("p (c t) -> c p t", c=NC)
        w_f = qT[:, :, :, :].rearrange("p h b t -> p (h b t)")[:, 0:2 * N_CUT].rearrange("p (k n) -> p k n", k=2)

        def steps(eng, body):
            with eng.Fori(0, NC - 1) as c:
                body(c, False)
            body(NC - 1, True)

        @block.sync
        def _(sp):
            def load(c):
                sp.dma_start(x1[:, :, :], acc_t[c]).then_inc(x_ready, 16)

            def angles(c):
                sp.dma_start(cos[:, :], cos_t[c]).then_inc(angles_ready, 16)
                sp.dma_start(sin[:, :], sin_t[c]).then_inc(angles_ready, 16)
                for lo, hi in ((0, 64), (64, 0)):
                    sp.dma_start(sin_swapped[lo:lo + 64, :], sin_t[c][hi:hi + 64, :]).then_inc(angles_ready, 16)

            load(0)
            angles(0)
            sp.dma_start(ident[:, :], io["ident"]).then_inc(ident_ready, 16)
            for dst, src in (
                (wv[:, :, :], io["wv"]), (v_dec[:, :], io["v_dec"]), (w_f[:, :, 0:HKV * DH], io["wk"]),
                (w_f[:, :, HKV * DH:N_CUT], io["wq"][:, :, 0:CUT_HEADS * DH]), (wq[:, :, :], io["wq"][:, :, CUT_HEADS * DH:HQ * DH]),
            ):
                sp.dma_start(dst, src).then_inc(loaded, 16)
            sp.wait_ge(first_gathered[NB - 1], 16 * K0)
            for dst, src in (
                (mask[:, :], io["mask"]), (half_chunk[:, :], io["half_chunk"]),
                (q_dec[:, :, :], io["q_dec"].rearrange("p (h i) -> p h i", h=HQ)), (wo[:, :, :], io["wo"]),
            ):
                sp.dma_start(dst, src).then_inc(loaded_late, 16)

            def save_prep(c):
                sp.wait_ge(xn_ready, c * NB + NB)
                sp.dma_start(x1_t[c], x1[:, :, :]).then_inc(x_stored, 16)
                sp.wait_ge(a_done, adone(c - 1, "xt", 1))
                sp.dma_start(scratch["xnT1"][c], xnT[:, :, :, :].rearrange("p k b t -> p (k b t)")).then_inc(xnT_stored, 16)

            def body(c, last):
                sp.wait_ge(x_stored, c * 16 + 16)
                if not last:
                    load(c + 1)
                    sp.wait_ge(roped, (c + 1) * (HKV + HQ))
                    angles(c + 1)
                sp.wait_ge(d_done, c * PD + ND)
                sp.dma_start(x1r[:, :, :], x1_t[c]).then_inc(x1r_ready, 16)
                for b in range(NB):
                    if b == NB - 1 and not last:
                        save_prep(c + 1)
                    sp.wait_ge(d_done, done(c, "wo", b, 0))
                    sp.dma_start(acc1_t[c, b], res[:, b % 2, :]).then_inc(stored[b % 2], 16)

            save_prep(0)
            steps(sp, body)
            for s in stored:
                sp.wait_ge(s, 16 * NC * NB // 2 + 16)
            sp.wait_ge(x_stored, 16 * NC)
            sp.wait_ge(xnT_stored, 16 * NC)

        @block.gpsimd
        def _(pool):
            nc.gpsimd.memset(eps[:, :], 1e-5).then_inc(setup, 1)

            def fetch(dst, b, k):
                return nc.gpsimd.indirect_dma_start(
                    out=dst, out_offset=None, in_=scratch["yb"],
                    in_offset=bass.IndirectOffsetOnAxis(ap=slot_now[:, b, k:k + 1], axis=0),
                    bounds_check=EXPERTS * CAP - 1, oob_is_err=False)

            def gather(c, b):
                if b == 0:
                    pool.wait_ge(now_ready, c + 1)
                pool.wait_ge(gath_used, c * NB + b + 1)
                pool.sem_inc(carry, 1)
                for k in range(K0):
                    fetch(gath[b % 2][:, k, :], b, k).then_inc(gathered[b % 2], 16)

            def body(c, last):
                for i in range(HKV + HQ):
                    pool.wait_ge(d_done, done(c, "rope", i))
                    kind, n = rope_of(i)
                    dst = kT[:, n, :, :] if kind == "k" else qT[:, n, :, :]
                    if i in SWAPS:
                        nc.gpsimd.tensor_tensor(rot[:, i % 3, :, :], rot[:, i % 3, :, :],
                                                sin_swapped[:, :].unsqueeze(1).to_broadcast([P, NB, P]), ALU.mult).then_inc(swap_sined, 1)
                        pool.wait_ge(swap_sined, c * len(SWAPS) + SWAPS.index(i) + 1)
                    nc.gpsimd.tensor_tensor(dst, dst, rot[:, i % 3, :, :], ALU.add).then_inc(roped, 1)
                if not last:
                    gather(c + 1, 0)
                    gather(c + 1, 1)
                for b in range(NB):
                    pool.wait_ge(d_done, done(c, "kv", b, HKV - 1))
                    dec = half_chunk[:, :].unsqueeze(2).to_broadcast([P, HQ, DH])
                    nc.gpsimd.tensor_tensor(kv[:, b, :, :], kv[:, b, :, :], dec, ALU.mult).then_inc(half_decayed, 1)
                    pool.wait_ge(half_decayed, c * NB + b + 1)
                    nc.gpsimd.tensor_tensor(kv[:, b, :, :], kv[:, b, :, :], dec, ALU.mult).then_inc(decayed, 1)
                    if b == PREP_AT - 1 and not last:
                        gather(c + 1, 2)
                        gather(c + 1, 3)

            pool.wait_ge(now_ready, 1)
            for b in range(NB):
                for k in range(K0):
                    at = (b * K0 + k) * D
                    fetch(first_gath[:, at:at + D], b, k).then_inc(first_gathered[b], 16)
            nc.gpsimd.memset(kv[:, :, :, :], 0.0).then_inc(setup, 1)
            pool.wait_ge(setup, 2)
            pool.wait_ge(loaded_late, 16 * N_LATE)
            steps(pool, body)

        @block.scalar
        def _(act):
            def A_wait(c, *job):
                act.wait_ge(a_full, c * PA + A.index(job) + 1 + PRE_A)

            def prep(c):
                act.wait_ge(mv_ready, c * NB + NB)
                nc.scalar.activation(lnv[:, :], mv[:, :, 1], ACT.Ln, bias=eps[:, :]).then_inc(lnv_ready, 1)
                act.wait_ge(lnv_ready, c + 1)
                nc.scalar.activation(rstd[:, :], lnv[:, :], ACT.Exp, scale=-0.5).then_inc(rstd_ready, 1)

            def turned(c, first=False):
                for i in range(2):
                    A_wait(c - 1, "xt", i)
                    if i == 0 and not first:
                        act.wait_ge(xnT_stored, c * 16)
                    nc.scalar.activation(xnT[:, :, 2 * i:2 * i + 2, :].rearrange("p k b t -> p b k t"),
                                         a_bank("xt", i)[:, :].rearrange("p (b k t) -> p b k t", b=2, k=2),
                                         ACT.Copy)
                    nc.scalar.activation(x_hi[:, :, 2 * i:2 * i + 2, :].rearrange("p k b t -> p b k t"),
                                         a_bank("xt", i)[:, :].rearrange("p (b k t) -> p b k t", b=2, k=2),
                                         ACT.Copy).then_inc(a_done, 1)

            def values(c, b):
                A_wait(c, "v", b)
                for h in range(HQ):
                    g = h // GR
                    ins = nc.scalar.activation(vd[:, b % 2, h, :], a_bank("v", b)[:, g * DH:(g + 1) * DH], ACT.Copy, scale=v_dec[:, h:h + 1])
                ins.then_inc(a_done, 1)

            def keys(c, b):
                A_wait(c, "ktok", b)
                nc.scalar.activation(ktok[:, b % 2, :, :].rearrange("p g e -> p (g e)"), a_bank("ktok", b)[:, :], ACT.Copy).then_inc(a_done, 1)

            def swaps(c):
                for i in SWAPS:
                    act.wait_ge(d_full, c * PD + DJ.index(("rope", i)) + 1)
                    act.wait_ge(roped, c * (HKV + HQ) + i - 2)
                    for lo, hi in ((0, 64), (64, 0)):
                        ins = nc.scalar.activation(rot[lo:lo + 64, i % 3, :, :], d_bank("rope", i)[hi:hi + 64, :].rearrange("p (b t) -> p b t", b=NB),
                                                   ACT.Copy)
                    ins.then_inc(swapped, 1)

            def body(c, last):
                for kind, b in A:
                    if kind == "v":
                        values(c, b)
                    if kind == "ktok":
                        if b == 0:
                            swaps(c)
                        keys(c, b)
                        if b == PREP_AT and not last:
                            prep(c + 1)
                if not last:
                    turned(c + 1)

            act.sem_inc(a_done, NA)
            act.wait_ge(setup, 1)
            prep(0)
            turned(0, True)
            act.wait_ge(loaded, 16 * N_LOAD)
            nc.scalar.activation(w_hi[:, :, :], w_f, ACT.Copy).then_inc(w_cut, 1)
            steps(act, body)

        @block.tensor
        def _(pe):
            def A_open(c, *job):
                pe.wait_ge(a_done, c * PA + credit(A, NA, job) + PRE_A)

            def D_open(c, *job):
                pe.wait_ge(d_done, c * PD + credit(DJ, ND, job))

            def turn(c):
                pe.wait_ge(xn_ready, c * NB + NB)
                for i in range(2):
                    A_open(c - 1, "xt", i)
                    for b in range(2):
                        for k in range(2):
                            o = (b * 2 + k) * P
                            ins = nc.tensor.transpose(a_bank("xt", i)[:, o:o + P], xn[:, 2 * i + b, k * P:(k + 1) * P], ident[:, :])
                    ins.then_inc(a_full, 1)

            def values(c, b):
                A_open(c, "v", b)
                for k in range(2):
                    ins = nc.tensor.matmul(a_bank("v", b)[:, :], xnT[:, k, b, :], wv[:, k, :], start=(k == 0), stop=(k == 1))
                ins.then_inc(a_full, 1)

            def keys(c, b):
                A_open(c, "ktok", b)
                for g in range(HKV):
                    ins = nc.tensor.transpose(a_bank("ktok", b)[:, g * P:(g + 1) * P], kT[:, g, b, :], ident[:, :])
                ins.then_inc(a_full, 1)

            def body(c, last):
                pe.wait_ge(a_done, adone(c - 1, "xt", 1))
                values(c, 0)
                values(c, 1)
                for i in range(HKV + HQ):
                    D_open(c, "rope", i)
                    kind, n = rope_of(i)
                    if i == 0:
                        pe.wait_ge(x_done, c + 1)
                        pe.wait_ge(w_done, 1)
                    at = n if kind == "k" else HKV + n
                    if at < HKV + CUT_HEADS:
                        terms = [(w[:, k, at * P:at * P + P], x[:, k, :, :].rearrange("p b t -> p (b t)"))
                                 for k in range(2) for w, x in ((w_hi, x_hi), (w_hi, x_lo), (w_lo, x_hi))]
                        for j, (w, x) in enumerate(terms):
                            ins = nc.tensor.matmul(d_bank("rope", i)[:, :], w, x, start=(j == 0), stop=(j == len(terms) - 1))
                        ins.then_inc(d_full, 1)
                        continue
                    w, n = wq, n - CUT_HEADS
                    for k in range(2):
                        ins = nc.tensor.matmul(d_bank("rope", i)[:, :], w[:, k, n * P:(n + 1) * P],
                                               xnT[:, k, :, :].rearrange("p b t -> p (b t)"), start=(k == 0), stop=(k == 1))
                    ins.then_inc(d_full, 1)
                pe.wait_ge(setup, 2)
                pe.wait_ge(loaded_late, 16 * N_LATE)
                for job in tile_order():
                    stage, b, g = job
                    q = b % 2
                    if stage == "end":
                        continue
                    if stage == "S" and g == 0 and b:
                        if b + 1 < NB:
                            values(c, b + 1)
                        keys(c, b)
                    D_open(c, *job)
                    out = d_bank(*job)
                    if stage == "S":
                        if b == 0:
                            pe.wait_ge(roped, c * (HKV + HQ) + (g + 1) * (GR + 1))
                        nc.tensor.matmul(out[:, :], kT[:, g, b, :], qT[:, GR * g:GR * g + GR, b, :], start=True, stop=True).then_inc(d_full, 1)
                        if b == 0 and g == 1:
                            pe.wait_ge(roped, c * (HKV + HQ) + (HKV - 1) * (GR + 1) + 1)
                            keys(c, 0)
                    if stage == "o":
                        if g == 0:
                            pe.wait_ge(a_done, adone(c, "v", b))
                            pe.wait_ge(decayed, c * NB + b + 1)
                        pe.wait_ge(d_done, done(c, "S", b, g))
                        for r in range(GR):
                            h = GR * g + r
                            nc.tensor.matmul(out[:, r * P:(r + 1) * P], vd[:, q, h, :], Sm[:, g % 2, r, :], start=True, stop=False)
                            ins = nc.tensor.matmul(out[:, r * P:(r + 1) * P], kv[:, b, h, :], qT[:, h, b, :], start=False, stop=True)
                        ins.then_inc(d_full, 1)
                    if stage == "kv":
                        pe.wait_ge(a_done, adone(c, "ktok", b))
                        nc.tensor.matmul(out[:, :], ktok[:, q, g, :], vd[:, q, GR * g:GR * g + GR, :], start=True, stop=True).then_inc(d_full, 1)
                    if stage == "wo":
                        if b == NB - 1 and not last:
                            turn(c + 1)
                        pe.wait_ge(d_done, done(c, "o", b, HKV - 1))
                        for h in range(HQ):
                            ins = nc.tensor.matmul(out[:, 0:D], oT[:, h, :], wo[:, h, :], start=(h == 0), stop=(h == HQ - 1))
                        ins.then_inc(d_full, 1)

            pe.sem_inc(decayed, NB)
            pe.wait_ge(ident_ready, 16)
            turn(0)
            pe.wait_ge(loaded, 16 * N_LOAD)
            steps(pe, body)

        @block.vector
        def _(dve):
            n = [0]
            vec = nc.vector

            def now(c):
                vec.tensor_copy(slot_now[:, :, :], slot_t[:, c, :, :]).then_inc(now_ready, 1)
                vec.tensor_copy(w_now[:, :, :], w_t[:, c, :, :]).then_inc(added, 1)

            ADDS = 1 + NB * K0

            def combine(c, b, first=False):
                q = b % 2
                if b == 0:
                    dve.wait_ge(x_ready, c * 16 + 16)
                if first:
                    dve.wait_ge(first_gathered[b], 16 * K0)
                else:
                    dve.wait_ge(gathered[q], ((c - 1) * 2 + b // 2) * 16 * K0 + 16 * K0)
                for k in range(K0):
                    dve.wait_ge(added, c * ADDS + 1 + b * K0 + k)
                    at = (b * K0 + k) * D
                    rows = first_gath[:, at:at + D] if first else gath[q][:, k, :]
                    vec.scalar_tensor_tensor(out=x1[:, b, :], in0=rows, scalar=w_now[:, b, k:k + 1],
                                             in1=x1[:, b, :], op0=ALU.mult, op1=ALU.add).then_inc(added, 1)
                dve.wait_ge(added, c * ADDS + 1 + b * K0 + K0)
                dve.sem_inc(gath_used, 1)

            def norm(c):
                for b in range(NB):
                    ins = vec.bn_stats(stats[:, b, :], x1[:, b, :])
                ins.then_inc(stats_ready, 1)
                dve.wait_ge(stats_ready, c + 1)
                dve.sem_inc(carry, 1)
                for b in range(NB):
                    vec.bn_aggr(mv[:, b, :], stats[:, b, :]).then_inc(mv_ready, 1)
                dve.wait_ge(rstd_ready, c + 1)
                for b in range(NB):
                    vec.tensor_scalar(xn[:, b, :], x1[:, b, :], mv[:, b, 0:1], rstd[:, b:b + 1], ALU.subtract,
                                      ALU.mult).then_inc(xn_ready, 1)

            def body(c, last):
                dve.wait_ge(a_done, adone(c - 1, "xt", 1))
                vec.tensor_tensor(x_lo[:, :, :, :], xnT[:, :, :, :], x_hi[:, :, :, :].bitcast(F32), ALU.subtract).then_inc(x_done, 1)
                dve.wait_ge(angles_ready, c * 64 + 64)
                for i in range(HKV + HQ):
                    dve.wait_ge(d_full, c * PD + DJ.index(("rope", i)) + 1)
                    if i >= 3:
                        dve.wait_ge(roped, c * (HKV + HQ) + i - 2)
                    src = d_bank("rope", i)
                    kind, head = rope_of(i)
                    dst = kT[:, head, :, :] if kind == "k" else qT[:, head, :, :]
                    if i in SWAPS:
                        dve.wait_ge(swapped, c * len(SWAPS) + SWAPS.index(i) + 1)
                    ins = vec.tensor_tensor(dst, src[:, :].rearrange("p (b t) -> p b t", b=NB),
                                            cos[:, :].unsqueeze(1).to_broadcast([P, NB, P]), ALU.mult)
                    if i in SWAPS:
                        ins.then_inc(d_done, 1)
                        continue
                    for lo, hi in ((0, 64), (64, 0)):
                        ins = vec.tensor_tensor(rot[lo:lo + 64, i % 3, :, :], src[hi:hi + 64, :].rearrange("p (b t) -> p b t", b=NB),
                                                sin[hi:hi + 64, :].unsqueeze(1).to_broadcast([64, NB, P]), ALU.mult)
                    ins.then_inc(d_done, 1)
                if not last:
                    now(c + 1)
                dve.wait_ge(loaded_late, 16 * N_LATE)
                dve.wait_ge(setup, 2)
                for job in tile_order():
                    stage, b, g = job
                    if stage == "end":
                        if not last and b == PREP_AT - 1:
                            combine(c + 1, 0)
                            combine(c + 1, 1)
                        if not last and b == PREP_AT:
                            combine(c + 1, 2)
                            combine(c + 1, 3)
                            norm(c + 1)
                        continue
                    dve.wait_ge(d_full, c * PD + DJ.index(job) + 1)
                    src = d_bank(*job)
                    if stage == "S":
                        vec.tensor_tensor(Sm[:, g % 2, :, :], src[:, :].rearrange("p (r i) -> p r i", r=GR),
                                          mask[:, :].unsqueeze(1).to_broadcast([P, GR, P]), ALU.mult).then_inc(d_done, 1)
                    if stage == "o":
                        vec.tensor_tensor(oT[:, GR * g:GR * g + GR, :], src[:, :].rearrange("p (r i) -> p r i", r=GR),
                                          q_dec[:, GR * g:GR * g + GR, :], ALU.mult).then_inc(d_done, 1)
                    if stage == "kv":
                        part = kv[:, b, GR * g:GR * g + GR, :]
                        vec.tensor_tensor(part, part, src[:, :].rearrange("p (r i) -> p r i", r=GR), ALU.add).then_inc(d_done, 1)
                    if stage == "wo":
                        if b == 0:
                            dve.wait_ge(x1r_ready, c * 16 + 16)
                        dve.wait_ge(stored[b % 2], c * 32 + b // 2 * 16 + 16)
                        vec.tensor_tensor(res[:, b % 2, :], src[:, 0:D], x1r[:, b, :], ALU.add).then_inc(d_done, 1)

            dve.sem_inc(d_done, ND)
            dve.sem_inc(gath_used, 2)
            for s in stored:
                dve.sem_inc(s, 16)
            now(0)
            for b in range(NB):
                combine(0, b, True)
            norm(0)
            dve.wait_ge(loaded, 16 * N_LOAD)
            dve.wait_ge(w_cut, 1)
            vec.tensor_tensor(w_lo[:, :, :], w_f, w_hi[:, :, :].bitcast(F32), ALU.subtract).then_inc(w_done, 1)
            dve.wait_ge(w_done, 1)
            steps(dve, body)


def ffn_phase(nc, io, scratch, out):
    with ExitStack() as ctx:
        def sb(name, shape, dt=F32):
            return ctx.enter_context(nc.sbuf_tensor("f_" + name, shape, dt))

        def sem(name):
            return ctx.enter_context(nc.semaphore("f_" + name))

        NE = E1 + 1
        W1 = 2 * P + 2 * P + D
        w_f = sb("w_f", [P, 3, W1])
        w_hi = sb("w_hi", [P, NE, W1], FR)
        w_lo = sb("w_lo", [P, NE, W1], FR)
        gw = sb("gw", [P, 2, E1])
        bias = sb("bias", [P, E1])
        iota = sb("iota", [P, E1])
        x_f = sb("x_f", [P, 2, 2, NB, P])
        x_hi = sb("x_hi", [P, 2, 2, NB * P], FR)
        x_lo = sb("x_lo", [P, 2, 2, NB * P], FR)
        acc = sb("acc", [P, 2, NB, D])
        score = sb("score", [P, NB, E1])
        picked = sb("picked", [P, NB, E1])
        t8 = sb("t8", [P, NB, 8])
        i8 = sb("i8", [P, NB, 8], U32)
        idx = sb("idx", [P, NB, 4])
        hot = sb("hot", [P, NB, 4, E1])
        tot = sb("tot", [P, NB])
        cw = sb("cw", [P, 2, NB, NE])
        h_f = sb("h_f", [P, 2, NB * P])
        h_hi = sb("h_hi", [P, 2, NB * P], FR)
        h_lo = sb("h_lo", [P, 2, NB * P], FR)
        psG = [ctx.enter_context(nc.psum_tensor(f"f_psG{i}", [P, 512], F32)) for i in range(2)]
        psU = [ctx.enter_context(nc.psum_tensor(f"f_psU{i}", [P, 512], F32)) for i in range(2)]
        psY = [ctx.enter_context(nc.psum_tensor(f"f_psY{i}", [P, 512], F32)) for i in range(4)]
        loaded, setup, carry = sem("loaded"), sem("setup"), sem("carry")
        w_ready = [sem(f"w_ready{i}") for i in range(3)]
        ready = [sem("ready0"), sem("ready1")]
        stored = [sem("stored0"), sem("stored1")]
        w_cut, w_done, x_cut, x_done = sem("w_cut"), sem("w_done"), sem("x_cut"), sem("x_done")
        logit, scored, step, g_full, u_full, silu, h_ready, hi_ready, lo_ready, y_full, y_used = (
            sem(k) for k in ("logit", "scored", "step", "g_full", "u_full", "silu", "h_ready", "hi_ready", "lo_ready",
                             "y_full", "y_used"))
        block = ctx.enter_context(nc.Block())
        acc1_t = scratch["acc1"].rearrange("(b c t) d -> c t b d", c=NC, t=P)
        out_t = out.rearrange("b (c t) d -> c t b d", t=P)
        STEPS = GATE_STEPS
        SLOTS = 2 * NE + 2
        LOGIT_SLOT = 2 * (NE - 2)
        assert SLOTS % 4 == 0

        def slot(e, j):
            return 2 * e + j + (2 if e >= NE - 2 else 0)

        def at(q, e):
            return (q * NE + e) % 2

        def steps(eng, body):
            body(0, 0, 0, False)
            body(1, 0, 1, False)
            with eng.Fori(1, NC // 2 - 1) as i:
                body(i * 2, i, 0, False)
                body(i * 2 + 1, i, 1, False)
            body(NC - 2, NC // 2 - 1, 0, False)
            body(NC - 1, NC // 2 - 1, 1, True)

        PRE = 3

        def first_step(c):
            return isinstance(c, int) and c == 0

        def after(c, q, e, last):
            return (c, q, e + 1) if e + 1 < NE else None if last else (c + 1, 1 - q, 0)

        @block.sync
        def _(sp):
            sp.dma_start(gw[:, :, :], io["gw1"]).then_inc(loaded, 16)
            sp.dma_start(bias[:, :], io["bias1"].rearrange("(a n) -> a n", a=1).to_broadcast([P, E1])).then_inc(loaded, 16)

            def x_load(c, i, q):
                sp.wait_ge(stored[q], i * 16 + 16)
                sp.dma_start(x_f[:, q, :, :, :].rearrange("p k b t -> p (k b t)"), scratch["xnT1"][c]).then_inc(ready[q], 16)
                sp.dma_start(acc[:, q, :, :], acc1_t[c]).then_inc(ready[q], 16)

            for e in range(NE):
                if e == 0:
                    x_load(0, 0, 0)
                if e == 5:
                    x_load(1, 0, 1)
                if e >= 3:
                    sp.wait_ge(w_done, e - 2)
                sp.dma_start(w_f[:, e % 3, :], io["w1"][e]).then_inc(w_ready[e % 3], 16)

            def store(c, q):
                sp.wait_ge(y_used, c * SLOTS + SLOTS + 4)
                sp.dma_start(out_t[c], acc[:, q, :, :]).then_inc(stored[q], 16)

            with sp.Fori(1, NC // 2) as i:
                for q in range(2):
                    store(i * 2 - 2 + q, q)
                    x_load(i * 2 + q, i, q)
            for q in range(2):
                store(NC - 2 + q, q)
            for s in stored:
                sp.wait_ge(s, 16 * NC // 2 + 16)

        @block.gpsimd
        def _(pool):
            nc.gpsimd.iota(iota[:, :], [[1, E1]], base=0, channel_multiplier=0,
                           allow_small_or_imprecise_dtypes=True).then_inc(setup, 1)
            nc.gpsimd.memset(cw[:, :, :, :], 1.0).then_inc(setup, 1)

            def body(c, i, q, last):
                for e in range(NE):
                    pool.wait_ge(hi_ready, c * NE + e + 1)
                    n = at(q, e)
                    nc.gpsimd.tensor_tensor(h_lo[:, n, :], h_f[:, n, :], h_hi[:, n, :].bitcast(F32), ALU.subtract).then_inc(lo_ready, 1)

            pool.sem_inc(lo_ready, 2)
            steps(pool, body)

        @block.scalar
        def _(act):
            def cut_x(c, i, q):
                act.wait_ge(ready[q], i * 32 + 32)
                nc.scalar.activation(x_hi[:, q, :, :].rearrange("p k n -> p (k n)"),
                                     x_f[:, q, :, :, :].rearrange("p k b t -> p (k b t)"), ACT.Copy).then_inc(x_cut, 1)

            def cut_w(e):
                act.wait_ge(w_ready[e % 3], e // 3 * 16 + 16)
                nc.scalar.activation(w_hi[:, e, :], w_f[:, e % 3, :], ACT.Copy).then_inc(w_cut, 1)

            def gate(c, q, e):
                m = c * NE + e
                act.wait_ge(g_full, m + 1)
                act.wait_ge(lo_ready, m - 2 + 1 + 2)
                nc.scalar.activation(h_f[:, at(q, e), :], psG[at(q, e)][:, :], ACT.Silu).then_inc(silu, 1)

            def high(c, q, e):
                m = c * NE + e
                act.wait_ge(h_ready, m + 1 + 2)
                act.wait_ge(y_full, (m - 2) * 2 + 2 + 4)
                nc.scalar.activation(h_hi[:, at(q, e), :], h_f[:, at(q, e), :], ACT.Copy).then_inc(hi_ready, 1)

            def sigmoid(c):
                act.wait_ge(logit, c + 1)
                nc.scalar.activation(score[:, :, :], psY[LOGIT_SLOT % 4][:, 0:NB * E1].rearrange("p (b e) -> p b e", b=NB),
                                     ACT.Sigmoid).then_inc(scored, 1)

            def body(c, i, q, last):
                for e in range(NE):
                    if first_step(c) and e + PRE < NE:
                        cut_w(e + PRE)
                    if e == NE // 2 and not last:
                        cut_x(c + 1, i + q, 1 - q)
                    if e == NE - 2 and not last:
                        sigmoid(c + 1)
                    nxt = after(c, q, e, last)
                    if nxt:
                        gate(*nxt)
                    high(c, q, e)

            act.sem_inc(stored[0], 16)
            act.sem_inc(stored[1], 16)
            act.wait_ge(setup, 2)
            cut_x(0, 0, 0)
            for e in range(PRE):
                cut_w(e)
            sigmoid(0)
            gate(0, 0, 0)
            steps(act, body)

        @block.tensor
        def _(pe):
            def exact(dst, pairs, start, stop):
                terms = [(w[i], x[j]) for w, x in pairs for i, j in ((0, 0), (0, 1), (1, 0))]
                for n, (w, x) in enumerate(terms):
                    ins = nc.tensor.matmul(dst, w, x, start=start and n == 0, stop=stop and n == len(terms) - 1)
                return ins

            def project(dst, q, e, col):
                return exact(dst[:, :], [((w_hi[:, e, col + k * P:col + k * P + P], w_lo[:, e, col + k * P:col + k * P + P]),
                                          (x_hi[:, q, k, :], x_lo[:, q, k, :])) for k in range(2)], True, True)

            def up(c, q, e):
                m = c * NE + e
                if first_step(c):
                    pe.wait_ge(w_done, e + 1)
                pe.wait_ge(silu, m - 2 + 1 + 2)
                project(psG[at(q, e)], q, e, 0).then_inc(g_full, 1)
                pe.wait_ge(h_ready, m - 2 + 1 + 2)
                project(psU[at(q, e)], q, e, 2 * P).then_inc(u_full, 1)

            def down(c, q, e):
                pe.wait_ge(lo_ready, c * NE + e + 1 + 2)
                for j in range(2):
                    s = slot(e, j)
                    pe.wait_ge(y_used, c * SLOTS + s - 3 + 4)
                    for r in range(2):
                        cols = slice((2 * j + r) * P, (2 * j + r + 1) * P)
                        n = at(q, e)
                        ins = exact(psY[s % 4][:, r * D:(r + 1) * D],
                                    [((h_hi[:, n, cols], h_lo[:, n, cols]), (w_hi[:, e, 4 * P:W1], w_lo[:, e, 4 * P:W1]))], True, True)
                    ins.then_inc(y_full, 1)

            def logits(c, q, first=False):
                pe.wait_ge(x_done, c + 1)
                if not first:
                    pe.wait_ge(y_used, (c - 1) * SLOTS + LOGIT_SLOT + 1 - 3 + 4)
                for b in range(NB):
                    for k in range(2):
                        ins = nc.tensor.matmul(psY[LOGIT_SLOT % 4][:, b * E1:(b + 1) * E1], x_f[:, q, k, b, :], gw[:, k, :],
                                               start=(k == 0), stop=(k == 1))
                ins.then_inc(logit, 1)

            def body(c, i, q, last):
                for e in range(NE):
                    if e == NE - 2 and not last:
                        logits(c + 1, 1 - q)
                    n1 = after(c, q, e, last)
                    n2 = after(*n1, last) if n1 else None
                    if n2:
                        up(*n2)
                    down(c, q, e)

            pe.sem_inc(silu, 2)
            pe.sem_inc(y_full, 4)
            pe.wait_ge(loaded, 32)
            logits(0, 0, True)
            for e in range(2):
                up(0, 0, e)
            steps(pe, body)

        @block.vector
        def _(dve):
            v = nc.vector

            def cut_x(c, q):
                dve.wait_ge(x_cut, c + 1)
                v.tensor_tensor(x_lo[:, q, :, :].rearrange("p k n -> p (k n)"), x_f[:, q, :, :, :].rearrange("p k b t -> p (k b t)"),
                                x_hi[:, q, :, :].rearrange("p k n -> p (k n)").bitcast(F32), ALU.subtract).then_inc(x_done, 1)

            def cut_w(e):
                dve.wait_ge(w_cut, e + 1)
                v.tensor_tensor(w_lo[:, e, :], w_f[:, e % 3, :], w_hi[:, e, :].bitcast(F32), ALU.subtract).then_inc(w_done, 1)

            def link(c, n, ins):
                ins.then_inc(step, 1)
                dve.wait_ge(step, c * STEPS + n)

            def choose(c):
                dve.wait_ge(scored, c + 1)
                dve.sem_inc(y_used, 2)
                link(c, 1, v.tensor_tensor(picked[:, :, :], score[:, :, :], bias[:, :].unsqueeze(1).to_broadcast([P, NB, E1]), ALU.add))
                dve.sem_inc(carry, 1)
                for b in range(NB):
                    ins = v.max(t8[:, b, :], picked[:, b, :])
                link(c, 2, ins)
                dve.sem_inc(carry, 1)
                for b in range(NB):
                    ins = v.max_index(i8[:, b, :], t8[:, b, :], picked[:, b, :])
                link(c, 3, ins)
                link(c, 4, v.tensor_copy(idx[:, :, :], i8[:, :, 0:4]))

            def weigh(c, q):
                link(c, 5, v.tensor_tensor(hot[:, :, :, :], iota[:, :].unsqueeze(1).unsqueeze(1).to_broadcast([P, NB, 4, E1]),
                                           idx[:, :, :].unsqueeze(3).to_broadcast([P, NB, 4, E1]), ALU.is_equal))
                link(c, 6, v.tensor_reduce(picked[:, :, :], hot[:, :, :, :].rearrange("p b k e -> p b e k"), AX.X, ALU.add))
                link(c, 7, v.tensor_tensor(picked[:, :, :], picked[:, :, :], score[:, :, :], ALU.mult))
                link(c, 8, v.tensor_reduce(tot[:, :], picked[:, :, :], AX.X, ALU.add))
                link(c, 9, v.reciprocal(tot[:, :], tot[:, :]))
                link(c, 10, v.tensor_tensor(cw[:, q, :, 0:E1], picked[:, :, :], tot[:, :].unsqueeze(2).to_broadcast([P, NB, E1]), ALU.mult))

            def product(c, q, e):
                m = c * NE + e
                n = at(q, e)
                dve.wait_ge(u_full, m + 1)
                dve.wait_ge(silu, m + 1 + 2)
                v.tensor_tensor(h_f[:, n, :], h_f[:, n, :], psU[n][:, :], ALU.mult).then_inc(h_ready, 1)

            def collect(c, q, e):
                for j in range(2):
                    dve.wait_ge(y_full, (c * NE + e) * 2 + j + 1 + 4)
                    for r in range(2):
                        b = 2 * j + r
                        ins = v.scalar_tensor_tensor(out=acc[:, q, b, :], in0=psY[slot(e, j) % 4][:, r * D:(r + 1) * D],
                                                     scalar=cw[:, q, b, e:e + 1], in1=acc[:, q, b, :], op0=ALU.mult, op1=ALU.add)
                    ins.then_inc(y_used, 1)

            def body(c, i, q, last):
                dve.wait_ge(ready[q], i * 32 + 32)
                for e in range(NE):
                    if first_step(c) and e + PRE < NE:
                        cut_w(e + PRE)
                    if e == NE // 2 and not last:
                        cut_x(c + 1, 1 - q)
                    nxt = after(c, q, e, last)
                    if nxt:
                        product(*nxt)
                    if e == NE - 2:
                        dve.wait_ge(y_used, c * SLOTS + LOGIT_SLOT + 4)
                        if last:
                            dve.sem_inc(y_used, 2)
                        else:
                            choose(c + 1)
                    if e:
                        s = slot(e, 0)
                        dve.wait_ge(y_used, c * SLOTS + s + 4)
                    collect(c, q, e)
                    if e == NE - 1 and not last:
                        weigh(c + 1, 1 - q)

            dve.sem_inc(h_ready, 2)
            dve.sem_inc(y_used, 2)
            dve.wait_ge(setup, 2)
            dve.wait_ge(loaded, 32)
            cut_x(0, 0)
            for e in range(PRE):
                cut_w(e)
            choose(0)
            weigh(0, 0)
            product(0, 0, 0)
            steps(dve, body)

def kernel(**inputs):
    import numpy as np
    import concourse.bacc as bacc
    from concourse.bass_utils import run_bass_kernel_spmd as run

    nc = bacc.Bacc("TRN2", target_bir_lowering=False, num_devices=1)
    arrays, io = {}, {}

    def give(name, a):
        arrays["in_" + name] = np.ascontiguousarray(a)
        io[name] = nc.dram_tensor("in_" + name, arrays["in_" + name].shape, F32, kind="ExternalInput").ap()

    I = {k: np.asarray(v) for k, v in inputs.items()}
    m = "L0_attn_"
    give("x", I[m + "x"])
    give("W_in", I[m + "W_in"])
    give("b_in", I[m + "b_in"])
    give("b_xbc", I[m + "b_in"][INNER:2 * INNER + 2 * D_STATE].reshape(6, P).T)
    give("b_z", I[m + "b_in"][:INNER].reshape(4, P).T)
    give("conv_w", I[m + "conv_w"].reshape(4, 6, P).transpose(2, 1, 0))
    give("conv_b", I[m + "conv_b"].reshape(6, P).T)
    give("norm_w", I[m + "norm_w"].reshape(4, P).T)
    for n in ("A_log", "dt_bias", "D_param", "W_out", "b_out"):
        give(n, I[m + n])
    give("Sg", I["L0_ffn_Sg"].reshape(2, 2, P, 256).transpose(2, 1, 0, 3))
    give("Su", I["L0_ffn_Su"].reshape(2, 2, P, 256).transpose(2, 1, 0, 3))
    give("Sd", I["L0_ffn_Sd"])
    sums, pairs = level_constants()
    give("sums", sums)
    give("pairs", pairs)
    give("ident", np.eye(P, dtype=np.float32))
    give("Wr", I["L0_ffn_Wr"])
    give("r_bias", I["L0_ffn_router_bias"])
    give("before", np.triu(np.ones((P, P), np.float32), 1))
    gu = np.stack([I["L0_ffn_Wg"], I["L0_ffn_Wu"]]).reshape(2, EXPERTS // 2, 2, 2, P, HID0)
    give("w0", np.concatenate([gu.transpose(1, 4, 0, 2, 3, 5).reshape(EXPERTS // 2, P, 8 * HID0),
                               I["L0_ffn_Wd"].reshape(EXPERTS // 2, P, D)], axis=2))
    n = "L1_attn_"
    for w in ("wq", "wk", "wv"):
        a = I[n + w]
        give(w, a.T.reshape(2, P, a.shape[0]).transpose(1, 0, 2))
    give("wo", I[n + "wo"].T.reshape(HQ, P, D).transpose(1, 0, 2))
    for k, a in attention_constants().items():
        give(k, a.astype(np.float32))
    f = "L1_ffn_"
    gate, up = (np.concatenate([I[f + "w_" + w], I[f + "sw_" + w][None]]).reshape(E1 + 1, P, 2, P).transpose(0, 3, 2, 1)
                for w in ("gate", "up"))
    down = np.concatenate([I[f + "w_down"], I[f + "sw_down"][None]]).transpose(0, 2, 1)
    give("w1", np.concatenate([gate.reshape(E1 + 1, P, 2 * P), up.reshape(E1 + 1, P, 2 * P), down], axis=2))
    give("gw1", I[f + "gate_w"].T.reshape(2, P, E1).transpose(1, 0, 2))
    give("bias1", I[f + "expert_bias"])
    scratch = {}
    for n, shape in (("acc0", (N_TOK, D)), ("xb", (EXPERTS * CAP, D)), ("yb", (EXPERTS * CAP, D)), ("xn", (N_TOK, D)),
                     ("xnT", (NC, P, 2 * NB * P)), ("x1", (N_TOK, D)), ("acc1", (N_TOK, D)), ("xnT1", (NC, P, 2 * NB * P))):
        scratch[n] = nc.dram_tensor("s_" + n, shape, F32, kind="Internal").ap()
    out = nc.dram_tensor("out", (NB, SEQ_LEN, D), F32, kind="ExternalOutput").ap()
    mixer_phase(nc, io, scratch)
    with ExitStack() as ctx:
        keep = {"w_all": ctx.enter_context(nc.sbuf_tensor("w_all", [P, NB * NC, K0], F32)),
                "slot_all": ctx.enter_context(nc.sbuf_tensor("slot_all", [P, NB * NC, K0], U32))}
        with ExitStack() as weights:
            keep["w0"] = weights.enter_context(nc.sbuf_tensor("w0", [P, EXPERTS // 2, W0], F32))
            router_phase(nc, io, scratch, keep)
            expert_phase(nc, io, scratch, keep)
        attention_phase(nc, io, scratch, keep)
    ffn_phase(nc, io, scratch, out)
    r = run(nc, [arrays], core_ids=[0])
    return r.results[0]["out"]
```
